# Optimizing a Trainium2 kernel written in Bass

```python
import numpy as np
import jax
import jax.numpy as jnp

def _softmax(x, axis=-1):
    return jax.nn.softmax(x, axis=axis)

def _gelu(x):
    return jax.nn.gelu(x, approximate=True)

def _silu(x):
    return jax.nn.silu(x)

def _sigmoid(x):
    return jax.nn.sigmoid(x)

def _layernorm(x, axis=-1, eps=1e-05):
    m = jnp.mean(x, axis=axis, keepdims=True)
    v = jnp.var(x, axis=axis, keepdims=True)
    return (x - m) / jnp.sqrt(v + eps)

def _scatter_add(tgt, idx, src, axis=0):
    return tgt.at[idx].add(src)

def _segment_sum(src, seg, n):
    return jax.ops.segment_sum(src, seg, n)
kernel_name = 'mk_seq_postln_d2_jaxref_r8_ec1300'

def setup_inputs(seed: int=0):
    np.random.seed(seed)
    _w = jnp.asarray

    def _L0_attn_setup():
        import jax, jax.numpy as jnp
        import numpy as np
        from functools import partial
        B, S, D = (8, 256, 128)
        HEADS, DIM_HEAD = (16, 64)
        MAX_ALLOWABLE = 128 * 128 * 8

        def _max_pow2_divides(n):
            i = 1
            while n % 2 == 0:
                i *= 2
                n //= 2
            return i

        def _n_splits(bh, sq, sk):
            dimprod = bh * sq * sk
            true_divisor = dimprod / MAX_ALLOWABLE
            if true_divisor < 1:
                return 1
            if true_divisor >= bh:
                return bh
            nearest_pow2 = 2 ** np.round(np.log2(true_divisor))
            return int(min(_max_pow2_divides(bh), nearest_pow2))

        def _sdp_attention(q, k, v, scale):
            scores = jnp.einsum('bid,bjd->bij', q, k) * scale
            probs = jax.nn.softmax(scores, axis=2)
            return jnp.einsum('bij,bjd->bid', probs, v)

        def _scan_attention(q, k, v, scale, n_splits):
            bh = q.shape[0]
            nq, nk, nv = [h.reshape(n_splits, bh // n_splits, h.shape[-2], h.shape[-1]) for h in (q, k, v)]

            def body(carry, args):
                cq, ck, cv = args
                return (None, _sdp_attention(cq, ck, cv, scale))
            outs = jax.lax.scan(body, None, (nq, nk, nv))[1]
            return outs.reshape(-1, outs.shape[-2], outs.shape[-1])

        def _heads_to_batch(t, heads):
            b, s, d = t.shape
            return t.reshape(b, s, heads, d // heads).transpose(0, 2, 1, 3).reshape(b * heads, s, d // heads)

        def _batch_to_heads(t, heads):
            bh, s, d = t.shape
            return t.reshape(bh // heads, heads, s, d).transpose(0, 2, 1, 3).reshape(bh // heads, s, d * heads)
        key = jax.random.key(seed)
        k1, k2, k3, k4 = jax.random.split(key, 4)
        inner = HEADS * DIM_HEAD
        return {'hidden_states': jax.random.normal(k1, (B, S, D), jnp.float32), 'Wq': jax.random.normal(k2, (D, inner), jnp.float32) * D ** (-0.5), 'Wkv': jax.random.normal(k3, (D, 2 * inner), jnp.float32) * D ** (-0.5), 'Wo': jax.random.normal(k4, (inner, D), jnp.float32) * inner ** (-0.5), 'bo': jnp.zeros((D,), jnp.float32)}
    _L0_attn_in = _L0_attn_setup()

    def _L0_ffn_setup():
        import jax, jax.numpy as jnp
        import numpy as np
        D_MODEL = 128
        NUM_TILES = 64
        TPC = 8
        NUM_CLUSTERS = NUM_TILES // TPC
        GRID = 16
        COMP_H = 32
        NUM_KNOTS = 8
        EPS_LN = 1e-05

        def _calibrate(scores, knots, temperature):
            K = knots.shape[0]
            normalized = jax.nn.sigmoid(scores / (temperature[0] + 1e-06))
            idx_float = normalized * (K - 1)
            idx_low = jnp.clip(idx_float.astype(jnp.int32), 0, K - 2)
            idx_high = idx_low + 1
            t = idx_float - idx_low.astype(scores.dtype)
            val_low = knots[idx_low]
            val_high = knots[idx_high]
            return val_low + t * (val_high - val_low)

        def _forward(x, signatures_raw, knot_values, temperature, compress_w1, compress_b1, compress_w2, compress_b2, spline_w1, spline_b1, spline_w2, spline_b2, directions, norm_gamma, norm_beta, output_scale):
            B, T, D = x.shape
            xf = x.reshape(-1, D)
            q = jnp.where(signatures_raw > 0.3, 1.0, jnp.where(signatures_raw < -0.3, -1.0, 0.0)).astype(signatures_raw.dtype)
            sigs = signatures_raw + jax.lax.stop_gradient(q - signatures_raw)
            cluster_sigs = jnp.sign(sigs.reshape(NUM_CLUSTERS, TPC, D).mean(axis=1))
            cluster_scores = xf @ cluster_sigs.T
            cluster_gates = _calibrate(cluster_scores, knot_values, temperature)
            cluster_idx = jnp.argmax(cluster_gates, axis=-1)
            tile_scores = xf @ sigs.T
            tile_gates = _calibrate(tile_scores, knot_values, temperature)
            gates_by_cluster = tile_gates.reshape(-1, NUM_CLUSTERS, TPC)
            sel_gates = jnp.take_along_axis(gates_by_cluster, cluster_idx[:, None, None], axis=1)[:, 0, :]
            local_idx = jnp.argmax(sel_gates, axis=-1)
            tile_idx = cluster_idx * TPC + local_idx
            h = jax.nn.gelu(xf @ compress_w1 + compress_b1, approximate=False)
            comp = jnp.tanh(h @ compress_w2 + compress_b2)
            w1 = spline_w1[tile_idx]
            b1 = spline_b1[tile_idx]
            hh = jax.nn.relu(jnp.einsum('ni,nig->ng', comp, w1) + b1)
            w2 = spline_w2[tile_idx]
            b2 = spline_b2[tile_idx]
            mag = jnp.einsum('ng,ngo->no', hh, w2) + b2
            ffn_out = mag * directions[tile_idx] * output_scale[0]
            y = xf + ffn_out
            mu = y.mean(axis=-1, keepdims=True)
            var = ((y - mu) ** 2).mean(axis=-1, keepdims=True)
            y = (y - mu) / jnp.sqrt(var + EPS_LN) * norm_gamma + norm_beta
            return y.reshape(B, T, D)
        key = jax.random.key(seed)
        ks = jax.random.split(key, 12)
        B, T = (4, 512)
        x = jax.random.normal(ks[0], (B, T, D_MODEL), dtype=jnp.float32)
        signatures_raw = jax.random.normal(ks[1], (NUM_TILES, D_MODEL), dtype=jnp.float32) * 0.5
        knot_values = jax.nn.sigmoid(jnp.linspace(-3.0, 3.0, NUM_KNOTS).astype(jnp.float32))
        temperature = jnp.ones((1,), dtype=jnp.float32)
        compress_w1 = jax.random.normal(ks[2], (D_MODEL, COMP_H), dtype=jnp.float32) * (1.0 / np.sqrt(D_MODEL))
        compress_b1 = jnp.zeros((COMP_H,), dtype=jnp.float32)
        compress_w2 = jax.random.normal(ks[3], (COMP_H, 2), dtype=jnp.float32) * (1.0 / np.sqrt(COMP_H))
        compress_b2 = jnp.zeros((2,), dtype=jnp.float32)
        spline_w1 = jax.random.normal(ks[4], (NUM_TILES, 2, GRID), dtype=jnp.float32) * (1.0 / np.sqrt(2.0))
        spline_b1 = jnp.zeros((NUM_TILES, GRID), dtype=jnp.float32)
        spline_w2 = jax.random.normal(ks[5], (NUM_TILES, GRID, 1), dtype=jnp.float32) * (1.0 / np.sqrt(GRID))
        spline_b2 = jnp.zeros((NUM_TILES, 1), dtype=jnp.float32)
        directions = jax.random.normal(ks[6], (NUM_TILES, D_MODEL), dtype=jnp.float32) * 0.02
        norm_gamma = jnp.ones((D_MODEL,), dtype=jnp.float32)
        norm_beta = jnp.zeros((D_MODEL,), dtype=jnp.float32)
        output_scale = jnp.ones((1,), dtype=jnp.float32) * 0.1
        return dict(x=x, signatures_raw=signatures_raw, knot_values=knot_values, temperature=temperature, compress_w1=compress_w1, compress_b1=compress_b1, compress_w2=compress_w2, compress_b2=compress_b2, spline_w1=spline_w1, spline_b1=spline_b1, spline_w2=spline_w2, spline_b2=spline_b2, directions=directions, norm_gamma=norm_gamma, norm_beta=norm_beta, output_scale=output_scale)
    _L0_ffn_in = _L0_ffn_setup()

    def _L1_attn_setup():
        import jax, jax.numpy as jnp
        import numpy as np
        D_MODEL = 128
        N_HEADS = 16
        WINDOW = 64
        HEAD_DIM = D_MODEL // N_HEADS
        HALF = WINDOW // 2
        NWIN = WINDOW + 1
        LN_EPS = 1e-05

        def _layernorm(x, g, b):
            mu = jnp.mean(x, axis=-1, keepdims=True)
            var = jnp.var(x, axis=-1, keepdims=True)
            return (x - mu) * jax.lax.rsqrt(var + LN_EPS) * g + b

        def _linear_attention(q, k, v):
            q = jax.nn.elu(q) + 1.0
            k = jax.nn.elu(k) + 1.0
            kv = jnp.einsum('bsd,bse->bde', k, v)
            num = jnp.einsum('bsd,bde->bse', q, kv)
            denom = jnp.einsum('bsd,bd->bs', q, k.sum(axis=1))
            return num / (denom[..., None] + 1e-06)

        def _window_attention(q, k, v, rel_bias):
            B, S, _ = q.shape
            qh = q.reshape(B, S, N_HEADS, HEAD_DIM).transpose(0, 2, 1, 3)
            kh = k.reshape(B, S, N_HEADS, HEAD_DIM).transpose(0, 2, 1, 3)
            vh = v.reshape(B, S, N_HEADS, HEAD_DIM).transpose(0, 2, 1, 3)
            kp = jnp.pad(kh, ((0, 0), (0, 0), (HALF, HALF), (0, 0)))
            vp = jnp.pad(vh, ((0, 0), (0, 0), (HALF, HALF), (0, 0)))
            pos = jnp.arange(S)
            scale = np.float32(1.0 / np.sqrt(HEAD_DIM))

            def score_step(_, w):
                off = w - HALF
                ks = jax.lax.dynamic_slice_in_dim(kp, w, S, axis=2)
                s = jnp.einsum('bhsd,bhsd->bhs', qh, ks) * scale
                s = s + rel_bias[off + WINDOW][None, :, None]
                valid = (pos + off >= 0) & (pos + off < S)
                s = jnp.where(valid[None, None, :], s, -jnp.inf)
                return (None, s)
            _, scores = jax.lax.scan(score_step, None, jnp.arange(NWIN))
            attn = jax.nn.softmax(scores, axis=0)

            def out_step(acc, aw):
                a, w = aw
                vs = jax.lax.dynamic_slice_in_dim(vp, w, S, axis=2)
                return (acc + a[..., None] * vs, None)
            out, _ = jax.lax.scan(out_step, jnp.zeros_like(qh), (attn, jnp.arange(NWIN)))
            return out.transpose(0, 2, 1, 3).reshape(B, S, D_MODEL)
        key = jax.random.key(seed)
        ks = jax.random.split(key, 16)

        def lin(k, fan_in, shape):
            return (jax.random.normal(k, shape, jnp.float32) / np.sqrt(fan_in)).astype(jnp.float32)
        D = D_MODEL
        inp = {'x': jax.random.normal(ks[0], (2, 256, D), jnp.float32), 'wq_lin': lin(ks[1], D, (D, D)), 'bq_lin': jnp.zeros((D,), jnp.float32), 'wk_lin': lin(ks[2], D, (D, D)), 'bk_lin': jnp.zeros((D,), jnp.float32), 'wv_lin': lin(ks[3], D, (D, D)), 'bv_lin': jnp.zeros((D,), jnp.float32), 'wq_loc': lin(ks[4], D, (D, D)), 'bq_loc': jnp.zeros((D,), jnp.float32), 'wk_loc': lin(ks[5], D, (D, D)), 'bk_loc': jnp.zeros((D,), jnp.float32), 'wv_loc': lin(ks[6], D, (D, D)), 'bv_loc': jnp.zeros((D,), jnp.float32), 'wo': lin(ks[7], D, (D, D)), 'bo': jnp.zeros((D,), jnp.float32), 'wg1': lin(ks[8], 3 * D, (3 * D, D)), 'bg1': jnp.zeros((D,), jnp.float32), 'wg2': lin(ks[9], D, (D, D)), 'bg2': jnp.zeros((D,), jnp.float32), 'rel_bias': jax.random.normal(ks[10], (2 * WINDOW + 1, N_HEADS), jnp.float32), 'ln_g': jnp.ones((D,), jnp.float32), 'ln_b': jnp.zeros((D,), jnp.float32)}
        return inp
    _L1_attn_in = _L1_attn_setup()

    def _L1_ffn_setup():
        import jax, jax.numpy as jnp
        import numpy as np
        QK_SCALE = 10.0
        NEG_INF = -1000000000.0

        def layernorm(x, g, b, eps=1e-05):
            mu = jnp.mean(x, axis=-1, keepdims=True)
            var = jnp.var(x, axis=-1, keepdims=True)
            return (x - mu) * jax.lax.rsqrt(var + eps) * g + b

        def l2norm(x, eps=1e-12):
            return x / jnp.sqrt(jnp.sum(x * x, axis=-1, keepdims=True) + eps)
        key = jax.random.key(seed)
        ks = jax.random.split(key, 10)
        B, S, D, H, DH, E, FF = (2, 128, 128, 16, 64, 8, 512)
        sd = lambda fan: 1.0 / np.sqrt(fan)
        return {'x': jax.random.normal(ks[0], (B, S, D), jnp.float32), 'ln_g': jnp.ones((D,), jnp.float32), 'ln_b': jnp.zeros((D,), jnp.float32), 'Wq': jax.random.normal(ks[1], (D, H * DH), jnp.float32) * sd(D), 'Wk': jax.random.normal(ks[2], (D, H * DH), jnp.float32) * sd(D), 'Wv': jax.random.normal(ks[3], (D, H * DH), jnp.float32) * sd(D), 'q_scale': jnp.ones((H, 1, DH), jnp.float32), 'k_scale': jnp.ones((H, 1, DH), jnp.float32), 'Wo': jax.random.normal(ks[4], (H * DH, D), jnp.float32) * sd(H * DH), 'gate_w': jax.random.normal(ks[5], (D, E), jnp.float32) * sd(D), 'gate_b': jnp.zeros((E,), jnp.float32), 'w1': jax.random.normal(ks[6], (E, D, FF), jnp.float32) * sd(D), 'b1': jnp.zeros((E, FF), jnp.float32), 'w2': jax.random.normal(ks[7], (E, FF, D), jnp.float32) * sd(FF), 'b2': jnp.zeros((E, D), jnp.float32)}
    _L1_ffn_in = _L1_ffn_setup()
    _d = {'L0_attn_hidden_states': _L0_attn_in['hidden_states'], 'L0_attn_Wq': _L0_attn_in['Wq'], 'L0_attn_Wkv': _L0_attn_in['Wkv'], 'L0_attn_Wo': _L0_attn_in['Wo'], 'L0_attn_bo': _L0_attn_in['bo'], 'L0_ffn_signatures_raw': _L0_ffn_in['signatures_raw'], 'L0_ffn_knot_values': _L0_ffn_in['knot_values'], 'L0_ffn_temperature': _L0_ffn_in['temperature'], 'L0_ffn_compress_w1': _L0_ffn_in['compress_w1'], 'L0_ffn_compress_b1': _L0_ffn_in['compress_b1'], 'L0_ffn_compress_w2': _L0_ffn_in['compress_w2'], 'L0_ffn_compress_b2': _L0_ffn_in['compress_b2'], 'L0_ffn_spline_w1': _L0_ffn_in['spline_w1'], 'L0_ffn_spline_b1': _L0_ffn_in['spline_b1'], 'L0_ffn_spline_w2': _L0_ffn_in['spline_w2'], 'L0_ffn_spline_b2': _L0_ffn_in['spline_b2'], 'L0_ffn_directions': _L0_ffn_in['directions'], 'L0_ffn_norm_gamma': _L0_ffn_in['norm_gamma'], 'L0_ffn_norm_beta': _L0_ffn_in['norm_beta'], 'L0_ffn_output_scale': _L0_ffn_in['output_scale'], 'L1_attn_wq_lin': _L1_attn_in['wq_lin'], 'L1_attn_bq_lin': _L1_attn_in['bq_lin'], 'L1_attn_wk_lin': _L1_attn_in['wk_lin'], 'L1_attn_bk_lin': _L1_attn_in['bk_lin'], 'L1_attn_wv_lin': _L1_attn_in['wv_lin'], 'L1_attn_bv_lin': _L1_attn_in['bv_lin'], 'L1_attn_wq_loc': _L1_attn_in['wq_loc'], 'L1_attn_bq_loc': _L1_attn_in['bq_loc'], 'L1_attn_wk_loc': _L1_attn_in['wk_loc'], 'L1_attn_bk_loc': _L1_attn_in['bk_loc'], 'L1_attn_wv_loc': _L1_attn_in['wv_loc'], 'L1_attn_bv_loc': _L1_attn_in['bv_loc'], 'L1_attn_wo': _L1_attn_in['wo'], 'L1_attn_bo': _L1_attn_in['bo'], 'L1_attn_wg1': _L1_attn_in['wg1'], 'L1_attn_bg1': _L1_attn_in['bg1'], 'L1_attn_wg2': _L1_attn_in['wg2'], 'L1_attn_bg2': _L1_attn_in['bg2'], 'L1_attn_rel_bias': _L1_attn_in['rel_bias'], 'L1_attn_ln_g': _L1_attn_in['ln_g'], 'L1_attn_ln_b': _L1_attn_in['ln_b'], 'L1_ffn_ln_g': _L1_ffn_in['ln_g'], 'L1_ffn_ln_b': _L1_ffn_in['ln_b'], 'L1_ffn_Wq': _L1_ffn_in['Wq'], 'L1_ffn_Wk': _L1_ffn_in['Wk'], 'L1_ffn_Wv': _L1_ffn_in['Wv'], 'L1_ffn_q_scale': _L1_ffn_in['q_scale'], 'L1_ffn_k_scale': _L1_ffn_in['k_scale'], 'L1_ffn_Wo': _L1_ffn_in['Wo'], 'L1_ffn_gate_w': _L1_ffn_in['gate_w'], 'L1_ffn_gate_b': _L1_ffn_in['gate_b'], 'L1_ffn_w1': _L1_ffn_in['w1'], 'L1_ffn_b1': _L1_ffn_in['b1'], 'L1_ffn_w2': _L1_ffn_in['w2'], 'L1_ffn_b2': _L1_ffn_in['b2']}
    _x0 = _d['L0_attn_hidden_states']
    _d['L0_attn_hidden_states'] = jax.random.normal(jax.random.fold_in(jax.random.key(seed), 1), (16, 256, 128), dtype=_x0.dtype)
    del _x0
    return _d

def reference(L0_attn_hidden_states, L0_attn_Wq, L0_attn_Wkv, L0_attn_Wo, L0_attn_bo, L0_ffn_signatures_raw, L0_ffn_knot_values, L0_ffn_temperature, L0_ffn_compress_w1, L0_ffn_compress_b1, L0_ffn_compress_w2, L0_ffn_compress_b2, L0_ffn_spline_w1, L0_ffn_spline_b1, L0_ffn_spline_w2, L0_ffn_spline_b2, L0_ffn_directions, L0_ffn_norm_gamma, L0_ffn_norm_beta, L0_ffn_output_scale, L1_attn_wq_lin, L1_attn_bq_lin, L1_attn_wk_lin, L1_attn_bk_lin, L1_attn_wv_lin, L1_attn_bv_lin, L1_attn_wq_loc, L1_attn_bq_loc, L1_attn_wk_loc, L1_attn_bk_loc, L1_attn_wv_loc, L1_attn_bv_loc, L1_attn_wo, L1_attn_bo, L1_attn_wg1, L1_attn_bg1, L1_attn_wg2, L1_attn_bg2, L1_attn_rel_bias, L1_attn_ln_g, L1_attn_ln_b, L1_ffn_ln_g, L1_ffn_ln_b, L1_ffn_Wq, L1_ffn_Wk, L1_ffn_Wv, L1_ffn_q_scale, L1_ffn_k_scale, L1_ffn_Wo, L1_ffn_gate_w, L1_ffn_gate_b, L1_ffn_w1, L1_ffn_b1, L1_ffn_w2, L1_ffn_b2):

    def _L0_attn_ref(hidden_states, Wq, Wkv, Wo, bo):
        import jax, jax.numpy as jnp
        import numpy as np
        from functools import partial
        B, S, D = (8, 256, 128)
        HEADS, DIM_HEAD = (16, 64)
        MAX_ALLOWABLE = 128 * 128 * 8

        def _max_pow2_divides(n):
            i = 1
            while n % 2 == 0:
                i *= 2
                n //= 2
            return i

        def _n_splits(bh, sq, sk):
            dimprod = bh * sq * sk
            true_divisor = dimprod / MAX_ALLOWABLE
            if true_divisor < 1:
                return 1
            if true_divisor >= bh:
                return bh
            nearest_pow2 = 2 ** np.round(np.log2(true_divisor))
            return int(min(_max_pow2_divides(bh), nearest_pow2))

        def _sdp_attention(q, k, v, scale):
            scores = jnp.einsum('bid,bjd->bij', q, k) * scale
            probs = jax.nn.softmax(scores, axis=2)
            return jnp.einsum('bij,bjd->bid', probs, v)

        def _scan_attention(q, k, v, scale, n_splits):
            bh = q.shape[0]
            nq, nk, nv = [h.reshape(n_splits, bh // n_splits, h.shape[-2], h.shape[-1]) for h in (q, k, v)]

            def body(carry, args):
                cq, ck, cv = args
                return (None, _sdp_attention(cq, ck, cv, scale))
            outs = jax.lax.scan(body, None, (nq, nk, nv))[1]
            return outs.reshape(-1, outs.shape[-2], outs.shape[-1])

        def _heads_to_batch(t, heads):
            b, s, d = t.shape
            return t.reshape(b, s, heads, d // heads).transpose(0, 2, 1, 3).reshape(b * heads, s, d // heads)

        def _batch_to_heads(t, heads):
            bh, s, d = t.shape
            return t.reshape(bh // heads, heads, s, d).transpose(0, 2, 1, 3).reshape(bh // heads, s, d * heads)
        scale = DIM_HEAD ** (-0.5)
        q = hidden_states @ Wq
        kv = hidden_states @ Wkv
        k, v = jnp.split(kv, 2, axis=-1)
        q = _heads_to_batch(q, HEADS)
        k = _heads_to_batch(k, HEADS)
        v = _heads_to_batch(v, HEADS)
        n_splits = _n_splits(q.shape[0], q.shape[1], k.shape[1])
        out = _scan_attention(q, k, v, scale, n_splits)
        out = _batch_to_heads(out, HEADS)
        return out @ Wo + bo

    def _L0_ffn_ref(x, signatures_raw, knot_values, temperature, compress_w1, compress_b1, compress_w2, compress_b2, spline_w1, spline_b1, spline_w2, spline_b2, directions, norm_gamma, norm_beta, output_scale):
        import jax, jax.numpy as jnp
        import numpy as np
        D_MODEL = 128
        NUM_TILES = 64
        TPC = 8
        NUM_CLUSTERS = NUM_TILES // TPC
        GRID = 16
        COMP_H = 32
        NUM_KNOTS = 8
        EPS_LN = 1e-05

        def _calibrate(scores, knots, temperature):
            K = knots.shape[0]
            normalized = jax.nn.sigmoid(scores / (temperature[0] + 1e-06))
            idx_float = normalized * (K - 1)
            idx_low = jnp.clip(idx_float.astype(jnp.int32), 0, K - 2)
            idx_high = idx_low + 1
            t = idx_float - idx_low.astype(scores.dtype)
            val_low = knots[idx_low]
            val_high = knots[idx_high]
            return val_low + t * (val_high - val_low)

        def _forward(x, signatures_raw, knot_values, temperature, compress_w1, compress_b1, compress_w2, compress_b2, spline_w1, spline_b1, spline_w2, spline_b2, directions, norm_gamma, norm_beta, output_scale):
            B, T, D = x.shape
            xf = x.reshape(-1, D)
            q = jnp.where(signatures_raw > 0.3, 1.0, jnp.where(signatures_raw < -0.3, -1.0, 0.0)).astype(signatures_raw.dtype)
            sigs = signatures_raw + jax.lax.stop_gradient(q - signatures_raw)
            cluster_sigs = jnp.sign(sigs.reshape(NUM_CLUSTERS, TPC, D).mean(axis=1))
            cluster_scores = xf @ cluster_sigs.T
            cluster_gates = _calibrate(cluster_scores, knot_values, temperature)
            cluster_idx = jnp.argmax(cluster_gates, axis=-1)
            tile_scores = xf @ sigs.T
            tile_gates = _calibrate(tile_scores, knot_values, temperature)
            gates_by_cluster = tile_gates.reshape(-1, NUM_CLUSTERS, TPC)
            sel_gates = jnp.take_along_axis(gates_by_cluster, cluster_idx[:, None, None], axis=1)[:, 0, :]
            local_idx = jnp.argmax(sel_gates, axis=-1)
            tile_idx = cluster_idx * TPC + local_idx
            h = jax.nn.gelu(xf @ compress_w1 + compress_b1, approximate=False)
            comp = jnp.tanh(h @ compress_w2 + compress_b2)
            w1 = spline_w1[tile_idx]
            b1 = spline_b1[tile_idx]
            hh = jax.nn.relu(jnp.einsum('ni,nig->ng', comp, w1) + b1)
            w2 = spline_w2[tile_idx]
            b2 = spline_b2[tile_idx]
            mag = jnp.einsum('ng,ngo->no', hh, w2) + b2
            ffn_out = mag * directions[tile_idx] * output_scale[0]
            y = xf + ffn_out
            mu = y.mean(axis=-1, keepdims=True)
            var = ((y - mu) ** 2).mean(axis=-1, keepdims=True)
            y = (y - mu) / jnp.sqrt(var + EPS_LN) * norm_gamma + norm_beta
            return y.reshape(B, T, D)
        return _forward(x, signatures_raw, knot_values, temperature, compress_w1, compress_b1, compress_w2, compress_b2, spline_w1, spline_b1, spline_w2, spline_b2, directions, norm_gamma, norm_beta, output_scale)

    def _L1_attn_ref(x, wq_lin, bq_lin, wk_lin, bk_lin, wv_lin, bv_lin, wq_loc, bq_loc, wk_loc, bk_loc, wv_loc, bv_loc, wo, bo, wg1, bg1, wg2, bg2, rel_bias, ln_g, ln_b):
        import jax, jax.numpy as jnp
        import numpy as np
        D_MODEL = 128
        N_HEADS = 16
        WINDOW = 64
        HEAD_DIM = D_MODEL // N_HEADS
        HALF = WINDOW // 2
        NWIN = WINDOW + 1
        LN_EPS = 1e-05

        def _layernorm(x, g, b):
            mu = jnp.mean(x, axis=-1, keepdims=True)
            var = jnp.var(x, axis=-1, keepdims=True)
            return (x - mu) * jax.lax.rsqrt(var + LN_EPS) * g + b

        def _linear_attention(q, k, v):
            q = jax.nn.elu(q) + 1.0
            k = jax.nn.elu(k) + 1.0
            kv = jnp.einsum('bsd,bse->bde', k, v)
            num = jnp.einsum('bsd,bde->bse', q, kv)
            denom = jnp.einsum('bsd,bd->bs', q, k.sum(axis=1))
            return num / (denom[..., None] + 1e-06)

        def _window_attention(q, k, v, rel_bias):
            B, S, _ = q.shape
            qh = q.reshape(B, S, N_HEADS, HEAD_DIM).transpose(0, 2, 1, 3)
            kh = k.reshape(B, S, N_HEADS, HEAD_DIM).transpose(0, 2, 1, 3)
            vh = v.reshape(B, S, N_HEADS, HEAD_DIM).transpose(0, 2, 1, 3)
            kp = jnp.pad(kh, ((0, 0), (0, 0), (HALF, HALF), (0, 0)))
            vp = jnp.pad(vh, ((0, 0), (0, 0), (HALF, HALF), (0, 0)))
            pos = jnp.arange(S)
            scale = np.float32(1.0 / np.sqrt(HEAD_DIM))

            def score_step(_, w):
                off = w - HALF
                ks = jax.lax.dynamic_slice_in_dim(kp, w, S, axis=2)
                s = jnp.einsum('bhsd,bhsd->bhs', qh, ks) * scale
                s = s + rel_bias[off + WINDOW][None, :, None]
                valid = (pos + off >= 0) & (pos + off < S)
                s = jnp.where(valid[None, None, :], s, -jnp.inf)
                return (None, s)
            _, scores = jax.lax.scan(score_step, None, jnp.arange(NWIN))
            attn = jax.nn.softmax(scores, axis=0)

            def out_step(acc, aw):
                a, w = aw
                vs = jax.lax.dynamic_slice_in_dim(vp, w, S, axis=2)
                return (acc + a[..., None] * vs, None)
            out, _ = jax.lax.scan(out_step, jnp.zeros_like(qh), (attn, jnp.arange(NWIN)))
            return out.transpose(0, 2, 1, 3).reshape(B, S, D_MODEL)
        h = _layernorm(x, ln_g, ln_b)
        lin_out = _linear_attention(h @ wq_lin + bq_lin, h @ wk_lin + bk_lin, h @ wv_lin + bv_lin)
        win_out = _window_attention(h @ wq_loc + bq_loc, h @ wk_loc + bk_loc, h @ wv_loc + bv_loc, rel_bias)
        gate_in = jnp.concatenate([lin_out, win_out, h], axis=-1)
        gate = jax.nn.sigmoid(jnp.maximum(gate_in @ wg1 + bg1, 0.0) @ wg2 + bg2)
        out = gate * lin_out + (1.0 - gate) * win_out
        return out @ wo + bo + x

    def _L1_ffn_ref(x, ln_g, ln_b, Wq, Wk, Wv, q_scale, k_scale, Wo, gate_w, gate_b, w1, b1, w2, b2):
        import jax, jax.numpy as jnp
        import numpy as np
        QK_SCALE = 10.0
        NEG_INF = -1000000000.0

        def layernorm(x, g, b, eps=1e-05):
            mu = jnp.mean(x, axis=-1, keepdims=True)
            var = jnp.var(x, axis=-1, keepdims=True)
            return (x - mu) * jax.lax.rsqrt(var + eps) * g + b

        def l2norm(x, eps=1e-12):
            return x / jnp.sqrt(jnp.sum(x * x, axis=-1, keepdims=True) + eps)
        B, S, D = x.shape
        H = q_scale.shape[0]
        DH = q_scale.shape[-1]
        h = layernorm(x, ln_g, ln_b)
        q = (h @ Wq).reshape(B, S, H, DH).transpose(0, 2, 1, 3)
        k = (h @ Wk).reshape(B, S, H, DH).transpose(0, 2, 1, 3)
        v = (h @ Wv).reshape(B, S, H, DH).transpose(0, 2, 1, 3)
        q = l2norm(q) * q_scale
        k = l2norm(k) * k_scale
        logits = jnp.einsum('bhid,bhjd->bhij', q, k) * QK_SCALE
        causal = jnp.tril(jnp.ones((S, S), bool))
        logits = jnp.where(causal, logits, NEG_INF)
        attn = jax.nn.softmax(logits, axis=-1)
        out = jnp.einsum('bhij,bhjd->bhid', attn, v)
        out = out.transpose(0, 2, 1, 3).reshape(B, S, H * DH) @ Wo
        h = layernorm(out, ln_g, ln_b)
        gate = jax.nn.softmax(h @ gate_w + gate_b, axis=-1)
        hid = jax.nn.gelu(jnp.einsum('bsd,edf->bsef', h, w1) + b1)
        exp_out = jnp.einsum('bsef,efd->bsed', hid, w2) + b2
        moe = jnp.einsum('bse,bsed->bsd', gate, exp_out)
        return layernorm(moe, ln_g, ln_b)
    x = L0_attn_hidden_states
    x = _layernorm(x + _L0_attn_ref(x, L0_attn_Wq, L0_attn_Wkv, L0_attn_Wo, L0_attn_bo), axis=-1)
    x = _layernorm(x + _L0_ffn_ref(x, L0_ffn_signatures_raw, L0_ffn_knot_values, L0_ffn_temperature, L0_ffn_compress_w1, L0_ffn_compress_b1, L0_ffn_compress_w2, L0_ffn_compress_b2, L0_ffn_spline_w1, L0_ffn_spline_b1, L0_ffn_spline_w2, L0_ffn_spline_b2, L0_ffn_directions, L0_ffn_norm_gamma, L0_ffn_norm_beta, L0_ffn_output_scale), axis=-1)
    x = _layernorm(x + _L1_attn_ref(x, L1_attn_wq_lin, L1_attn_bq_lin, L1_attn_wk_lin, L1_attn_bk_lin, L1_attn_wv_lin, L1_attn_bv_lin, L1_attn_wq_loc, L1_attn_bq_loc, L1_attn_wk_loc, L1_attn_bk_loc, L1_attn_wv_loc, L1_attn_bv_loc, L1_attn_wo, L1_attn_bo, L1_attn_wg1, L1_attn_bg1, L1_attn_wg2, L1_attn_bg2, L1_attn_rel_bias, L1_attn_ln_g, L1_attn_ln_b), axis=-1)
    x = _layernorm(x + _L1_ffn_ref(x, L1_ffn_ln_g, L1_ffn_ln_b, L1_ffn_Wq, L1_ffn_Wk, L1_ffn_Wv, L1_ffn_q_scale, L1_ffn_k_scale, L1_ffn_Wo, L1_ffn_gate_w, L1_ffn_gate_b, L1_ffn_w1, L1_ffn_b1, L1_ffn_w2, L1_ffn_b2), axis=-1)
    return x

_drawn_inputs = setup_inputs


def setup_inputs(seed=0):
    import zlib

    import numpy as np

    out = dict(_drawn_inputs(seed))
    spreads = {'L0_attn_bo': (0.0, 0.1),
     'L0_ffn_compress_b1': (0.0, 0.8),
     'L0_ffn_compress_b2': (0.0, 2.0),
     'L0_ffn_spline_b1': (0.0, 0.8),
     'L0_ffn_spline_b2': (0.0, 2.0),
     'L0_ffn_norm_gamma': (1.0, 0.2),
     'L0_ffn_norm_beta': (0.0, 0.1),
     'L1_attn_bq_lin': (0.0, 2.0),
     'L1_attn_bk_lin': (0.0, 2.0),
     'L1_attn_bv_lin': (0.0, 0.1),
     'L1_attn_bq_loc': (0.0, 0.619),
     'L1_attn_bk_loc': (0.0, 2.0),
     'L1_attn_bv_loc': (0.0, 0.1),
     'L1_attn_bo': (0.0, 0.1),
     'L1_attn_bg1': (0.0, 0.8),
     'L1_attn_bg2': (0.0, 0.594),
     'L1_attn_ln_g': (1.0, 0.2),
     'L1_attn_ln_b': (0.0, 0.1),
     'L1_ffn_ln_g': (1.0, 0.2),
     'L1_ffn_ln_b': (0.0, 0.1),
     'L1_ffn_q_scale': (1.0, 0.2),
     'L1_ffn_k_scale': (1.0, 0.2),
     'L1_ffn_gate_b': (0.0, 0.1),
     'L1_ffn_b1': (0.0, 0.1),
     'L1_ffn_b2': (0.0, 0.1)}
    factors = {'L0_ffn_signatures_raw': 8.0,
     'L0_ffn_knot_values': 8.0,
     'L0_ffn_compress_w1': 8.0,
     'L0_ffn_compress_w2': 8.0,
     'L0_ffn_spline_w1': 8.0,
     'L0_ffn_spline_w2': 8.0,
     'L0_ffn_directions': 8.0,
     'L1_attn_wq_lin': 64.0,
     'L1_attn_wk_lin': 41.386}
    for name, (base, spread) in spreads.items():
        noise = np.random.default_rng([zlib.crc32(name.encode()), seed]).standard_normal(out[name].shape)
        drawn = base * np.exp(spread * noise) if base else spread * noise
        out[name] = jnp.asarray(drawn.astype(out[name].dtype))
    for name, factor in factors.items():
        out[name] = (out[name] * factor).astype(out[name].dtype)
    return out
```

```python
import concourse.bass as bass
from concourse import mybir
from contextlib import ExitStack

F32 = mybir.dt.float32
BF16 = mybir.dt.bfloat16
ALU = mybir.AluOpType
ACT = mybir.ActivationFunctionType
AX = mybir.AxisListType.X

NB, S, D = 16, 256, 128
P = 128
NT = S // P
NH, DH = 16, 64
NC = NH * DH // P
CL, TPC, KN = 8, 8, 8
TILES = CL * TPC
GRID, COMP = 16, 32
WH, WD = 16, 8
QT = 64
HALF = 32
KEY0 = [0, 32, 96, 128]
NE, FF = 8, 512
FC = FF // P
EPS = 1e-5
NEG = -1e30
CAUSAL_FILL = -1e9
TBL = 2 * GRID + GRID + GRID + 1 + D

COLS = {}
ROWS = {}


def _place(table, names):
    at = 0
    for name, n in names:
        table[name] = (at, n)
        at += n
    return at


N_COLS = _place(COLS, [("l1_g", 1), ("l1_b", 1), ("bq_lin", 1), ("bq_loc", 1), ("bk_loc", 1), ("bv_loc", 1),
                       ("bg1", 1), ("bg2", 1), ("f_g", 1), ("f_b", 1), ("cb1", 1), ("oscale", 1), ("temp", 1),
                       ("qs", NC), ("ks", NC), ("b1", NE * FC), ("headmask", WH)])
N_ROWS = _place(ROWS, [("bo0", D), ("gamma", D), ("beta", D), ("bk_lin", D), ("bv_lin", D), ("bo1", D),
                       ("f_g", D), ("f_b", D), ("gate_b", NE), ("knots", KN), ("jlo", KN - 1), ("jhi", KN - 1),
                       ("first", 8)])


def merged(*programs):
    live = [[next(g, None), g] for g in programs]
    while live := [x for x in live if x[0] is not None]:
        first = min(live, key=lambda x: x[0])
        first[0] = next(first[1], None)


def whole_net(nc, d):
    ctx = ExitStack()
    with ctx:
        def sb(name, shape, dt=F32):
            return ctx.enter_context(nc.sbuf_tensor(name, shape, dt))

        def sem(name):
            return ctx.enter_context(nc.semaphore(name))

        cols = sb("cols", [P, N_COLS])
        rows = sb("rows", [P, N_ROWS])
        ident = sb("ident", [P, P])
        ident_bf = sb("ident_bf", [P, P], BF16)
        causal = sb("causal", [P, P], BF16)
        A = sb("A", [P, NH, P])
        wv0 = sb("wv0", [P, NH * DH])
        wo0 = sb("wo0", [P, NC, D])
        router = sb("router", [P, CL + TILES])
        cw1 = sb("cw1", [P, COMP])
        cw2 = sb("cw2", [COMP + 1, 2])
        tbl = sb("tbl", [TILES, TBL])
        w1a = sb("w1a", [P, 6, D])
        wg1 = sb("wg1", [P, 3, D])
        wg2 = sb("wg2", [P, D])
        wo1 = sb("wo1", [P, D])
        bias_t = sb("bias_t", [P, 2, WH, P])
        wqkv = sb("wqkv", [P, 3, NH * DH])
        wo2 = sb("wo2", [P, NC, D])
        gate_w = sb("gate_w", [P, NE])
        w1 = sb("w1", [P, NE, FF])
        w2 = sb("w2", [P, NE, FC, D])
        b2 = sb("b2", [NE, D])
        half_neg = sb("half_neg", [P, 32])
        neg_bg2 = sb("neg_bg2", [P, 1])
        inv_t = sb("inv_t", [P, 1])
        kqs = sb("kqs", [P, NC])
        knot_tab = sb("knot_tab", [P, 3, KN - 1])

        xT = sb("xT", [P, S])
        xr = sb("xr", [P, NT, D])
        xb = sb("xb", [P, NT, D])
        GQ = sb("GQ", [P, NH, S])
        OT0 = GQ[:, :, :].rearrange("p (c a) n -> p c a n", a=2)[:, :, 0, :]
        ETw = sb("ETw", [P, WH, P])
        V0 = ETw[:, :, :].rearrange("p (t a) n -> p t (a n)", t=NT)
        E0 = sb("E0", [P, 3, NT, S])
        ET0 = sb("ET0", [P, 2, 2, S])
        nm0 = sb("nm0", [P, NH, NT])
        rs0 = sb("rs0", [P, NH, NT])
        ri0 = sb("ri0", [P, NH, NT])
        y1 = sb("y1", [P, NT, D])
        x1 = sb("x1", [P, NT, D])
        x1b = xb
        x2 = sb("x2", [P, NT, D])
        x2b = xb
        xn = sb("xn", [P, NT, D])
        x3 = sb("x3", [P, NT, D])
        fT = sb("fT", [P, S])
        hT = sb("hT", [P, S])
        st1 = sb("st1", [P, NT, 6])
        mv1 = sb("mv1", [P, NT, 2])
        ve1 = sb("ve1", [P, NT])
        rstd1 = sb("rstd1", [P, NT])
        scores = sb("scores", [P, NT, CL + TILES])
        gel = sb("gel", [COMP + 1, S])
        comp = sb("comp", [P, NT, 2])
        ec = sb("ec", [P, NT * 8])
        el = sb("el", [P, NT * 8])
        fx = sb("fx", [P, NT * 8])
        m_a = sb("m_a", [P, NT * 8, KN - 1])
        m_b = sb("m_b", [P, NT * 8, KN - 1])
        pick = sb("pick", [P, NT * 8, 3, KN - 1])
        picked = sb("picked", [P, NT * 8, 3])
        gates = sb("gates", [P, NT, 8])
        gmax = sb("gmax", [P, NT])
        hot_c = sb("hot_c", [P, NT, 8])
        hot_l = sb("hot_l", [P, NT, 8])
        selp = sb("selp", [P, NT, TPC, CL])
        sel = sb("sel", [P, NT, TPC])
        hot = sb("hot", [P, NT, CL, TPC])
        hotT = sb("hotT", [TILES, S])
        got = sb("got", [P, NT, TBL])
        hh = sb("hh", [P, NT, GRID])
        mag = sb("mag", [P, NT])
        qlinT = ET0[:, 0, 0, :]
        q_e = ET0[:, 0, 1, :]
        klin = ET0[:, 1, 0, :].rearrange("p (t n) -> p t n", t=NT)
        k_e = ET0[:, 1, 1, :].rearrange("p (t n) -> p t n", t=NT)
        vlin1 = sb("vlin1", [P, NT, 2, D])
        kv = sb("kv", [P, 2, D])
        den = fT
        linT = qlinT
        winT = q_e
        qloc = sb("qloc", [P, S])
        kloc = sb("kloc", [P, S])
        VM = sb("VM", [P, 2, WH * (P + WD)])
        Sw = E0[:, :, :, :].rearrange("p a t (g n) -> p a (t g) n", n=P)
        nmw = sb("nmw", [P, 3, 4])
        rsw = sb("rsw", [P, 3, 4])
        hidg = qloc
        gt = kloc

        xh = sb("xh", [P, NT, D])
        xn2 = sb("xn2", [P, NT, D])
        h2T = sb("h2T", [P, S])
        QK = sb("QK", [P, 2, NC, S])
        hid = QK[:, :, :, :].rearrange("p a (g f) n -> p (a g) f n", f=FC)
        V2 = sb("V2", [P, NT, NH * DH])
        OT2 = QK[:, 0, :, :]
        work2 = sb("work2", [P, 2048])
        sq = work2[:, 0:1024].rearrange("p (a h n) -> p a h n", a=2, h=8)
        qn = work2[:, 1024:2048].rearrange("p (a h n) -> p a h n", a=2, h=8)
        ss = sb("ss", [P, 8, 8])
        rn = sb("rn", [P, 8, 8])
        E2 = work2[:, 0:1152].rearrange("p (a n) -> p a n", a=3)
        ET2 = work2[:, 1152:1920].rearrange("p (a n) -> p a n", a=2)
        nm2 = sb("nm2", [P, NH, NT])
        rs2 = sb("rs2", [P, NH, NT])
        ri2 = sb("ri2", [P, NH, NT])
        st2 = sb("st2", [P, NT, 6])
        mv2 = sb("mv2", [P, NT, 2])
        ve2 = sb("ve2", [P, NT])
        rstd2 = sb("rstd2", [P, NT])
        gl = sb("gl", [P, NT, NE])
        gm = sb("gm", [P, NT])
        gs = sb("gs", [P, NT])
        gateT = sb("gateT", [NE, S])
        acc = sb("acc", [P, NT, D])
        yo = xn2

        wqT = GQ[0:DH, :, :].rearrange("p h n -> p (h n)")[:, 0:NH * P].rearrange("p (h n) -> p h n", h=NH)
        wkT = GQ[0:DH, :, :].rearrange("p h n -> p (h n)")[:, NH * P:2 * NH * P].rearrange("p (h n) -> p h n", h=NH)
        raw = GQ[:, 0, :]

        ps = ctx.enter_context(nc.psum_tensor("ps", [P, 8, 512], F32))
        bank1 = [ps[:, n, :] for n in range(4)]
        bank2 = [ps[:, 4 + n, :] for n in range(4)]

        def col(name, n=0, w=1):
            at = COLS[name][0] + n
            return cols[:, at:at + w]

        def row(name):
            at, n = ROWS[name]
            return rows[:, at:at + n]

        def row_t(name):
            at, n = ROWS[name]
            return rows[:, at:at + n].unsqueeze(1).broadcast_to((P, NT, n))

        def tri(ap, a):
            return ap.rearrange("p (a n) -> p a n", a=a)

        w_first = sem("w_first")
        w_second = sem("w_second")
        setup_pool = sem("setup_pool")
        setup_dve = sem("setup_dve")
        a_ready = sem("a_ready")
        a_copied = sem("a_copied")

        first_loads = [(wqT, d["wqT"]), (wkT, d["wkT"]), (cols[:, :], d["cols"]), (rows[:, :], d["rows"]),
                       (ident[:, :], d["ident"]), (xT[:, :], d["xT"][0, :, :]), (xr[:, :, :], d["xr"][0, :, :, :]),
                       (wv0[:, :], d["wv0"]), (wo0[:, :, :], d["wo0"]), (router[:, CL:CL + TILES], d["sigT"]),
                       (cw1[:, :], d["cw1"]), (cw2[:, :], d["cw2"]), (tbl[:, :], d["tbl"]),
                       (w1a[:, :, :], d["w1a"]), (wg1[:, :, :], d["wg1"]), (wg2[:, :], d["wg2"]),
                       (wo1[:, :], d["wo1"]), (bias_t[:, :, :, :], d["bias_t"])]
        second_loads = [(wqkv[:, :, :], d["wqkv"]), (wo2[:, :, :], d["wo2"]), (gate_w[:, :], d["gate_w"]),
                        (w1[:, :, :], d["w1"]), (w2[:, :, :, :], d["w2"]), (b2[:, :], d["b2"])]

        with nc.Block(no_gpsimd_drain=True) as block:
            @block.sync
            def _(sp):
                for dst, src in first_loads:
                    sp.dma_start(dst, src).then_inc(w_first, 16)
                for dst, src in second_loads:
                    sp.dma_start(dst, src).then_inc(w_second, 16)

            @block.gpsimd
            def _(pool):
                for n, (ap, value) in enumerate(((half_neg[:, :], -0.5), (vlin1[:, :, 1, :], 1.0), (gel[COMP:COMP + 1, :], 1.0),
                                                 (causal[:, :], 0.0), (VM[:, :, :], 0.0))):
                    nc.gpsimd.memset(ap, value).then_inc(setup_pool, 1)
                    pool.wait_ge(setup_pool, n + 1)
                nc.gpsimd.affine_select(out=causal[:, :], in_=causal[:, :], compare_op=ALU.is_ge, fill=CAUSAL_FILL,
                                        base=0, pattern=[[-1, P]], channel_multiplier=1)

            @block.vector
            def _(dve):
                n = [0]

                def link(ins):
                    n[0] += 1
                    ins.then_inc(setup_dve, 1)
                    dve.wait_ge(setup_dve, n[0])

                dve.wait_ge(w_first, 16 * len(first_loads))
                nc.vector.tensor_copy(ident_bf[:, :], ident[:, :])
                nc.vector.tensor_scalar(neg_bg2[:, :], col("bg2"), -1.0, None, ALU.mult)
                link(nc.vector.tensor_scalar(inv_t[:, :], col("temp"), 1e-6, None, ALU.add))
                link(nc.vector.reciprocal(inv_t[:, :], inv_t[:, :]))
                link(nc.vector.tensor_tensor(kqs[:, :], col("qs", 0, NC), col("ks", 0, NC), ALU.mult))
                link(nc.vector.tensor_scalar(kqs[:, :], kqs[:, :], 10.0, None, ALU.mult))
                k = row("knots")
                nc.vector.tensor_copy(knot_tab[:, 0, :], k[:, 0:KN - 1])
                nc.vector.tensor_tensor(knot_tab[:, 1, :], k[:, 1:KN], k[:, 0:KN - 1], ALU.subtract)
                nc.vector.tensor_copy(knot_tab[:, 2, :], row("jlo"))
                dve.wait_ge(a_ready, 4)
                sig = router[:, CL:CL + TILES]
                q, low = raw[:, 0:TILES], raw[:, TILES:2 * TILES]
                nc.vector.tensor_scalar(q, sig, 0.3, None, ALU.is_gt)
                link(nc.vector.tensor_scalar(low, sig, -0.3, None, ALU.is_lt))
                link(nc.vector.tensor_tensor(q, q, low, ALU.subtract))
                link(nc.vector.tensor_tensor(q, q, sig, ALU.subtract))
                link(nc.vector.tensor_tensor(sig, sig, q, ALU.add))
                by = sig.rearrange("p (c t) -> p t c", c=CL)
                total, neg = raw[:, 128:128 + CL], raw[:, 136:136 + CL]
                link(nc.vector.tensor_tensor(total, by[:, 0, :], by[:, 1, :], ALU.add))
                for t in range(2, TPC):
                    link(nc.vector.tensor_tensor(total, total, by[:, t, :], ALU.add))
                nc.vector.tensor_scalar(neg, total, 0.0, None, ALU.is_lt)
                link(nc.vector.tensor_scalar(total, total, 0.0, None, ALU.is_gt))
                link(nc.vector.tensor_tensor(router[:, 0:CL], total, neg, ALU.subtract))

            @block.tensor
            def _(pe):
                pe.wait_ge(w_first, 16 * len(first_loads))
                for u in range(4):
                    for h in range(4 * u, 4 * u + 4):
                        last = nc.tensor.matmul(bank1[u][:, (h % 4) * P:(h % 4 + 1) * P], wqT[:, h, :], wkT[:, h, :],
                                                start=True, stop=True)
                    last.then_inc(a_ready, 1)

            @block.scalar
            def _(act):
                for u in range(4):
                    act.wait_ge(a_ready, u + 1)
                    nc.scalar.activation(A[:, 4 * u:4 * u + 4, :], tri(bank1[u], 4), ACT.Copy).then_inc(a_copied, 1)
                act.wait_ge(a_copied, 4)

        names = """
            x_next x_taken
            proj0 proj0_act proj0_dve sc0 max0 exp0 ri0_ready norm0 tr0 et0_act et0_dve av0 ot0_act wo0_done
            xb_ready dve1 ve1_ready rstd1_ready x1b_ready
            x1_ready x1tr x1T_ready route_ready gelu_ready compress_ready comp_ready sc_copied exp_c sel_ready exp_l
            hot_ready hot_tr hotT_ready got_ready x2_ready x2b_ready xn_ready xn_tr hT_ready
            lin_proj q_exp k_exp klin_raw qlin_ready klin_ready kv_done kv_copied lin_done lin_ready linT_ready
            loc_q loc_kv qloc_ready kloc_ready qm_ready vm_ready vm_proj
            w_sc w_max w_sub w_exp w_sum w_norm w_tr w_et w_av winT_ready
            g1_done g1_ready g2_done g_exp mixed o1_done x3_ready
            x3_taken dve2 ve2_ready rstd2_ready xn2_ready tr2 hT2_ready
            v2_proj v2_copied qk_proj sq_ready ss_ready rn_ready qn_ready qk_tr q_copied k_copied
            sc2 max2 exp2 ri2_ready norm2 tr2e et2_act et2_dve av2 ot2_done wo2_done
            o2_ready o2_tr o2T_ready gate_done gl_ready gexp_done gate_ready gate_tr gateT_ready
            hid_done hid_ready out_done out_used y_ready y_stored
        """.split()
        s = {name: sem(name) for name in names}
        loop_sems = range(min(x.num for x in s.values()), max(x.num for x in s.values()) + 1)
        assert len(loop_sems) == len(names)

        def chain(eng, name):
            n = [0]

            def link(ins):
                n[0] += 1
                ins.then_inc(s[name], 1)
                eng.wait_ge(s[name], n[0])
            return link

        def first_sync(sp, next_batch):
            yield 34
            sp.wait_ge(s["sc0"], NH)
            sp.wait_ge(s["xb_ready"], 1)
            sp.wait_ge(s["proj0"], 12)
            sp.dma_start(xT[:, :], d["xT"][bass.ds(next_batch, 1), :, :].rearrange("a p n -> (a p) n"))\
                .then_inc(s["x_next"], 16)
            sp.dma_start(xr[:, :, :], d["xr"][bass.ds(next_batch, 1), :, :, :].rearrange("a p t n -> (a p) t n"))\
                .then_inc(s["x_next"], 16)
            yield 60
            sp.wait_ge(s["x_next"], 32)

        def k0(h):
            return 4 + 1.6 * h

        def proj_bank(u):
            return bank1[u % 3]

        def first_pe(pe):
            for u in range(12):
                yield 0
                if u >= 3:
                    v = u - 3
                    pe.wait_ge(s["proj0_dve" if v % 2 else "proj0_act"], v // 2 + 1)
                if u < 8:
                    for j in range(2):
                        last = nc.tensor.matmul(proj_bank(u)[:, j * S:(j + 1) * S], A[:, 2 * u + j, :], xT[:, :],
                                                start=True, stop=True)
                else:
                    t, c = divmod(u - 8, 2)
                    last = nc.tensor.matmul(proj_bank(u), xT[:, t * P:(t + 1) * P], wv0[:, c * 512:(c + 1) * 512],
                                            start=True, stop=True)
                last.then_inc(s["proj0"], 1)
            for h in range(NH + 3):
                yield k0(h)
                if h < NH:
                    if h == 0:
                        pe.wait_ge(s["proj0_act"], 6)
                        pe.wait_ge(s["proj0_dve"], 6)
                    if h >= 2:
                        pe.wait_ge(s["exp0"], 2 * (h - 1))
                    for t in range(NT):
                        last = nc.tensor.matmul(bank1[h % 2][:, t * S:(t + 1) * S], GQ[:, h, t * P:(t + 1) * P],
                                                xT[:, :], start=True, stop=True)
                    last.then_inc(s["sc0"], 1)
                if 0 <= h - 2 < NH:
                    g = h - 2
                    pe.wait_ge(s["norm0"], g + 1)
                    if g >= 1:
                        et_wait(pe, "et0", g - 1)
                    for k in range(2):
                        for t in range(NT):
                            last = nc.tensor.transpose(bank1[2][:, k * S + t * P:k * S + (t + 1) * P],
                                                       E0[:, g % 3, t, k * P:(k + 1) * P], ident[:, :])
                    last.then_inc(s["tr0"], 1)
                if 0 <= h - 3:
                    g = h - 3
                    et_wait(pe, "et0", g)
                    if g >= 2 and g % 2 == 0:
                        pe.wait_ge(s["ot0_act"], g // 2)
                    r = 64 * (g % 2)
                    for k in range(2):
                        last = nc.tensor.matmul(bank1[3][r:r + DH, 0:S], V0[:, k, g * DH:(g + 1) * DH],
                                                ET0[:, g % 2, k, :], start=(k == 0), stop=(k == 1))
                    last.then_inc(s["av0"], 1)
            yield k0(NH + 3)
            pe.wait_ge(s["ot0_act"], NC)
            out_proj(bank1[0], OT0, wo0).then_inc(s["wo0_done"], 1)
            yield 36
            pe.wait_ge(s["x1_ready"], 1)
            transposed(bank1[2], x1).then_inc(s["x1tr"], 1)
            yield 37
            pe.wait_ge(s["x1T_ready"], 1)
            last = nc.tensor.matmul(bank1[1][0:COMP, 0:S], cw1[:, :], fT[:, :], start=True, stop=True)
            for t in range(NT):
                last = nc.tensor.matmul(bank1[0][:, t * P:t * P + CL + TILES], fT[:, t * P:(t + 1) * P], router[:, :],
                                        start=True, stop=True)
            last.then_inc(s["route_ready"], 1)
            yield 38
            pe.wait_ge(s["gelu_ready"], 1)
            for t in range(NT):
                last = nc.tensor.matmul(bank1[3][:, 2 * t:2 * t + 2], gel[:, t * P:(t + 1) * P], cw2[:, :],
                                        start=True, stop=True)
            last.then_inc(s["compress_ready"], 1)
            yield 42
            pe.wait_ge(s["hot_ready"], 1)
            for t in range(NT):
                last = nc.tensor.transpose(bank1[2][0:TILES, t * P:(t + 1) * P],
                                           hot[:, t, :, :].rearrange("p c l -> p (c l)"), ident[:, :])
            last.then_inc(s["hot_tr"], 1)
            pe.wait_ge(s["hotT_ready"], 1)
            for t in range(NT):
                last = nc.tensor.matmul(bank1[0][:, t * S:t * S + TBL], hotT[:, t * P:(t + 1) * P], tbl[:, :],
                                        start=True, stop=True)
            last.then_inc(s["got_ready"], 1)
            yield 46
            pe.wait_ge(s["xn_ready"], 1)
            transposed(bank1[2], xn).then_inc(s["xn_tr"], 1)
            pe.wait_ge(s["hT_ready"], 1)
            for j, w in enumerate((3, 4)):
                last = nc.tensor.matmul(bank1[0][:, j * S:(j + 1) * S], w1a[:, w, :], hT[:, :], start=True, stop=True)
            last.then_inc(s["loc_q"], 1)
            last = nc.tensor.matmul(bank1[1][:, 0:S], w1a[:, 0, :], hT[:, :], start=True, stop=True)
            for t in range(NT):
                for j, w in enumerate((1, 2)):
                    last = nc.tensor.matmul(bank1[3 if j else 1][:, S + t * P:S + (t + 1) * P],
                                            hT[:, t * P:(t + 1) * P], w1a[:, w, :], start=True, stop=True)
            last.then_inc(s["lin_proj"], 1)
            yield 48
            pe.wait_ge(s["klin_ready"], 1)
            pe.wait_ge(s["qlin_ready"], 1)
            for t in range(NT):
                last = nc.tensor.matmul(bank1[2][:, 0:2 * D], klin[:, t, :], vlin1[:, t, :, :].rearrange("p a n -> p (a n)"),
                                        start=(t == 0), stop=(t == NT - 1))
            last.then_inc(s["kv_done"], 1)
            pe.wait_ge(s["kv_copied"], 1)
            for j in range(2):
                last = nc.tensor.matmul(bank1[3][:, j * S:(j + 1) * S], kv[:, j, :], qlinT, start=True, stop=True)
            last.then_inc(s["lin_done"], 1)
            pe.wait_ge(s["kloc_ready"], 1)
            for u in range(8 + 2):
                yield kw(u)
                p, g = divmod(u, 4)
                if u == 0:
                    pe.wait_ge(s["linT_ready"], 1)
                    window_values(0)
                if u < 8:
                    pe.wait_ge(s["qm_ready"], g + 1)
                    if u >= 2:
                        pe.wait_ge(s["w_max"], 2 * (u - 1) - 1)
                    for hd in range(4):
                        for j in range(2):
                            h, t = 4 * g + hd, 2 * p + j
                            last = nc.tensor.matmul(bank1[u % 2][QT * j:QT * (j + 1), hd * P:(hd + 1) * P],
                                                    GQ[:, h, t * QT:(t + 1) * QT], kloc[:, KEY0[t]:KEY0[t] + P],
                                                    start=True, stop=True)
                    last.then_inc(s["w_sc"], 1)
                if u == 6:
                    window_out(0)
                    window_values(1)
                if u >= 2:
                    v = u - 2
                    pe.wait_ge(s["w_norm"], v + 1)
                    if v >= 1:
                        pe.wait_ge(s["w_et"], v)
                    for hd in range(4):
                        last = nc.tensor.transpose(bank1[2][:, hd * P:(hd + 1) * P], Sw[:, v % 3, hd, :], ident[:, :])
                    last.then_inc(s["w_tr"], 1)
                if u == 9:
                    window_out(1)
            yield 66
            pe.wait_ge(s["winT_ready"], 1)
            for j, r in enumerate((linT, winT, hT[:, :])):
                last = nc.tensor.matmul(bank1[0][:, 0:S], wg1[:, j, :], r, start=(j == 0), stop=(j == 2))
            last.then_inc(s["g1_done"], 1)
            pe.wait_ge(s["g1_ready"], 1)
            nc.tensor.matmul(bank1[1][:, 0:S], wg2[:, :], hidg[:, :], start=True, stop=True).then_inc(s["g2_done"], 1)
            pe.wait_ge(s["mixed"], 1)
            for t in range(NT):
                last = nc.tensor.matmul(bank1[0][:, t * P:(t + 1) * P], gt[:, t * P:(t + 1) * P], wo1[:, :],
                                        start=True, stop=True)
            last.then_inc(s["o1_done"], 1)

        def window_out(pp):
            pe = nc.tensor
            pe.wait_ge(s["w_et"], 4 * (pp + 1))
            pe.wait_ge(s["vm_ready"], pp + 1)
            for j in range(2):
                t = 2 * pp + j
                for h in range(WH):
                    last = nc.tensor.matmul(bank1[3][:, t * QT:(t + 1) * QT], VM[:, j, h * P:(h + 1) * P],
                                            ETw[:, h, j * QT:(j + 1) * QT], start=(h == 0), stop=(h == WH - 1))
            last.then_inc(s["w_av"], 1)

        def window_values(pp):
            for j in range(2):
                k = KEY0[2 * pp + j]
                last = nc.tensor.matmul(bank1[3][:, pp * S + j * P:pp * S + (j + 1) * P], hT[:, k:k + P],
                                        w1a[:, 5, :], start=True, stop=True)
            last.then_inc(s["vm_proj"], 1)

        def kw(u):
            return 50 + 1.6 * u

        def et_wait(eng, name, g):
            eng.wait_ge(s[name + ("_dve" if g % 2 else "_act")], g // 2 + 1)

        def transposed(bank, src):
            for t in range(NT):
                last = nc.tensor.transpose(bank[:, t * P:(t + 1) * P], src[:, t, :], ident[:, :])
            return last

        def out_proj(bank, OT, wo):
            for t in range(NT):
                for c in range(NC):
                    last = nc.tensor.matmul(bank[:, t * P:(t + 1) * P], OT[:, c, t * P:(t + 1) * P], wo[:, c, :],
                                            start=(c == 0), stop=(c == NC - 1))
            return last

        def first_act(act):
            for u in range(0, 12, 2):
                yield 0
                act.wait_ge(s["proj0"], u + 1)
                if u < 8:
                    nc.scalar.activation(GQ[:, 2 * u:2 * u + 2, :], tri(proj_bank(u), 2), ACT.Copy,
                                         scale=DH ** -0.5).then_inc(s["proj0_act"], 1)
                else:
                    t, c = divmod(u - 8, 2)
                    nc.scalar.activation(V0[:, t, c * 512:(c + 1) * 512], proj_bank(u), ACT.Copy)\
                        .then_inc(s["proj0_act"], 1)
            for h in range(NH + 3):
                yield k0(h)
                if h < NH:
                    act.wait_ge(s["max0"], h + 1)
                    if h >= 3:
                        act.wait_ge(s["tr0"], h - 2)
                    for t in range(NT):
                        nc.scalar.activation(E0[:, h % 3, t, :], bank1[h % 2][:, t * S:(t + 1) * S], ACT.Exp,
                                             bias=nm0[:, h, t:t + 1],
                                             accum_out=rs0[:, h, t:t + 1]).then_inc(s["exp0"], 1)
                g = h - 2
                if 0 <= g < NH and g % 2 == 0:
                    act.wait_ge(s["tr0"], g + 1)
                    if g >= 2:
                        act.wait_ge(s["av0"], g - 1)
                    nc.scalar.activation(ET0[:, 0, :, :], tri(bank1[2], 2), ACT.Copy).then_inc(s["et0_act"], 1)
                g = h - 3
                if g >= 0 and g % 2:
                    act.wait_ge(s["av0"], g + 1)
                    nc.scalar.activation(OT0[:, g // 2, :], bank1[3][:, 0:S], ACT.Copy).then_inc(s["ot0_act"], 1)
            yield 37
            act.wait_ge(s["x1tr"], 1)
            nc.scalar.activation(fT[:, :], bank1[2][:, 0:S], ACT.Copy).then_inc(s["x1T_ready"], 1)
            act.wait_ge(s["route_ready"], 1)
            yield 38
            nc.scalar.activation(gel[0:COMP, :], bank1[1][0:COMP, 0:S], ACT.Gelu, bias=cols[0:COMP, COLS["cb1"][0]:COLS["cb1"][0] + 1])\
                .then_inc(s["gelu_ready"], 1)
            act.wait_ge(s["compress_ready"], 1)
            nc.scalar.activation(comp[:, :, :].rearrange("p t n -> p (t n)"), bank1[3][:, 0:4], ACT.Tanh)\
                .then_inc(s["comp_ready"], 1)
            yield 39
            act.wait_ge(s["sc_copied"], 1)
            nc.scalar.activation(ec[:, :].rearrange("p (t n) -> p t n", t=NT), scores[:, :, 0:CL], ACT.Exp,
                                 scale=-1.0).then_inc(s["exp_c"], 1)
            yield 40
            act.wait_ge(s["sel_ready"], 1)
            nc.scalar.activation(el[:, :], sel[:, :, :].rearrange("p t n -> p (t n)"), ACT.Exp,
                                 scale=-1.0).then_inc(s["exp_l"], 1)
            yield 46
            act.wait_ge(s["xn_tr"], 1)
            nc.scalar.activation(hT[:, :], bank1[2][:, 0:S], ACT.Identity, bias=col("l1_b"), scale=col("l1_g"))\
                .then_inc(s["hT_ready"], 1)
            act.wait_ge(s["loc_q"], 1)
            nc.scalar.activation(qloc[:, :], bank1[0][:, 0:S], ACT.Identity, bias=col("bq_loc"))\
                .then_inc(s["qloc_ready"], 1)
            nc.scalar.activation(kloc[:, :], bank1[0][:, S:2 * S], ACT.Identity, bias=col("bk_loc"))\
                .then_inc(s["kloc_ready"], 1)
            act.wait_ge(s["klin_raw"], 1)
            nc.scalar.activation(q_e, q_e, ACT.Exp).then_inc(s["q_exp"], 1)
            nc.scalar.activation(k_e[:, :, :], k_e[:, :, :], ACT.Exp).then_inc(s["k_exp"], 1)
            yield 48
            act.wait_ge(s["kv_done"], 1)
            nc.scalar.activation(kv[:, :, :], tri(bank1[2][:, 0:2 * D], 2), ACT.Copy).then_inc(s["kv_copied"], 1)
            for u in range(8 + 2):
                yield kw(u)
                if 1 <= u < 9:
                    v = u - 1
                    act.wait_ge(s["w_sub"], v + 1)
                    nc.scalar.activation(Sw[:, v % 3, :, :], Sw[:, v % 3, :, :], ACT.Exp).then_inc(s["w_exp"], 1)
                if u >= 2:
                    v = u - 2
                    p, g = divmod(v, 4)
                    act.wait_ge(s["w_tr"], v + 1)
                    if v == 4:
                        act.wait_ge(s["w_av"], 1)
                    nc.scalar.activation(ETw[:, 4 * g:4 * g + 4, :], tri(bank1[2], 4), ACT.Copy)\
                        .then_inc(s["w_et"], 1)
            yield 66
            act.wait_ge(s["g2_done"], 1)
            nc.scalar.activation(gt[:, :], bank1[1][:, 0:S], ACT.Exp, bias=neg_bg2[:, :], scale=-1.0)\
                .then_inc(s["g_exp"], 1)

        def layer_norm(link, dve, src, dst, st, mv, ve, half, k):
            for t in range(NT):
                ins = nc.vector.bn_stats(st[:, t, :], src[:, t, :])
            link(ins)
            for t in range(NT):
                ins = nc.vector.bn_aggr(mv[:, t, :], st[:, t, :])
            link(ins)
            nc.vector.tensor_scalar(ve[:, :], mv[:, :, 1], EPS, None, ALU.add).then_inc(s[f"ve{half}_ready"], 1)
            dve.wait_ge(s[f"rstd{half}_ready"], k + 1)
            rstd = rstd1 if half == 1 else rstd2
            for t in range(NT):
                ins = nc.vector.tensor_scalar(dst[:, t, :], src[:, t, :], mv[:, t, 0:1], rstd[:, t:t + 1],
                                              ALU.subtract, ALU.mult)
            return ins

        def rstd_step(pool, half, k):
            ve, rstd = (ve1, rstd1) if half == 1 else (ve2, rstd2)
            pool.wait_ge(s[f"ve{half}_ready"], k + 1)
            nc.gpsimd.tensor_tensor(rstd[:, :], ve[:, :], half_neg[:, 0:NT], ALU.pow)\
                .then_inc(s[f"rstd{half}_ready"], 1)

        def calibrate(link, e):
            n = NT * 8
            link(nc.vector.tensor_scalar(fx[:, :], e[:, :], 1.0, None, ALU.add))
            link(nc.vector.reciprocal(fx[:, :], fx[:, :]))
            link(nc.vector.tensor_scalar(fx[:, :], fx[:, :], float(KN - 1), None, ALU.mult))
            f = fx[:, :].unsqueeze(2).broadcast_to((P, n, KN - 1))
            nc.vector.tensor_tensor(m_a[:, :, :], f, row("jlo").unsqueeze(1).broadcast_to((P, n, KN - 1)), ALU.is_ge)
            link(nc.vector.tensor_tensor(m_b[:, :, :], f, row("jhi").unsqueeze(1).broadcast_to((P, n, KN - 1)),
                                         ALU.is_lt))
            link(nc.vector.tensor_tensor(m_a[:, :, :], m_a[:, :, :], m_b[:, :, :], ALU.mult))
            link(nc.vector.tensor_tensor(pick[:, :, :, :], m_a[:, :, :].unsqueeze(2).broadcast_to((P, n, 3, KN - 1)),
                                         knot_tab[:, :, :].unsqueeze(1).broadcast_to((P, n, 3, KN - 1)), ALU.mult))
            link(nc.vector.tensor_reduce(picked[:, :, :], pick[:, :, :, :], AX, ALU.add))
            g = gates[:, :, :].rearrange("p t n -> p (t n)")
            link(nc.vector.tensor_tensor(g, fx[:, :], picked[:, :, 2], ALU.subtract))
            link(nc.vector.tensor_tensor(g, g, picked[:, :, 1], ALU.mult))
            link(nc.vector.tensor_tensor(g, g, picked[:, :, 0], ALU.add))

        def first_max(link, hot_):
            b = (P, NT, 8)
            link(nc.vector.tensor_reduce(gmax[:, :], gates[:, :, :], AX, ALU.max))
            link(nc.vector.tensor_tensor(gates[:, :, :], gates[:, :, :], gmax[:, :].unsqueeze(2).broadcast_to(b), ALU.is_ge))
            link(nc.vector.tensor_tensor(gates[:, :, :], gates[:, :, :], row_t("first"), ALU.mult))
            link(nc.vector.tensor_reduce(gmax[:, :], gates[:, :, :], AX, ALU.max))
            return nc.vector.tensor_tensor(hot_[:, :, :], gates[:, :, :], gmax[:, :].unsqueeze(2).broadcast_to(b), ALU.is_equal)

        def first_dve(dve, both):
            count = [0]

            def link(ins):
                count[0] += 1
                ins.then_inc(s["dve1"], 1)
                dve.wait_ge(s["dve1"], count[0])

            for u in range(1, 12, 2):
                yield 0
                dve.wait_ge(s["proj0"], u + 1)
                if u < 8:
                    nc.vector.tensor_scalar(GQ[:, 2 * u:2 * u + 2, :], tri(proj_bank(u), 2), DH ** -0.5, None,
                                            ALU.mult).then_inc(s["proj0_dve"], 1)
                else:
                    t, c = divmod(u - 8, 2)
                    nc.vector.tensor_copy(V0[:, t, c * 512:(c + 1) * 512], proj_bank(u)).then_inc(s["proj0_dve"], 1)
            for h in range(NH + 3):
                yield k0(h)
                if h < NH:
                    dve.wait_ge(s["sc0"], h + 1)
                    nc.vector.tensor_reduce(nm0[:, h, :], tri(bank1[h % 2], 2), AX, ALU.max, negate=True)\
                        .then_inc(s["max0"], 1)
                if 1 <= h <= NH:
                    dve.wait_ge(s["exp0"], 2 * h)
                    nc.vector.reciprocal(ri0[:, h - 1, :], rs0[:, h - 1, :]).then_inc(s["ri0_ready"], 1)
                g = h - 2
                if 0 <= g < NH and g % 2:
                    dve.wait_ge(s["tr0"], g + 1)
                    if g >= 2:
                        dve.wait_ge(s["av0"], g - 1)
                    nc.vector.tensor_copy(ET0[:, 1, :, :], tri(bank1[2], 2)).then_inc(s["et0_dve"], 1)
            yield k0(NH + 3)
            dve.wait_ge(s["wo0_done"], 1)
            dve.wait_ge(s["xb_ready"], 1)
            link(nc.vector.tensor_tensor(y1[:, :, :], tri(bank1[0][:, 0:S], 2), xb[:, :, :], ALU.add))
            layer_norm(link, dve, y1, x1, st1, mv1, ve1, 1, 0).then_inc(s["x1_ready"], 1)
            yield 38
            dve.wait_ge(s["route_ready"], 1)
            nc.vector.tensor_scalar(scores[:, :, :], tri(bank1[0][:, 0:S], 2)[:, :, 0:CL + TILES], inv_t[:, :], -87.0,
                                    ALU.mult, ALU.max).then_inc(s["sc_copied"], 1)
            yield 39
            dve.wait_ge(s["exp_c"], 1)
            calibrate(link, ec)
            link(first_max(link, hot_c))
            by = scores[:, :, CL:CL + TILES].rearrange("p t (c l) -> p t l c", c=CL)
            link(nc.vector.tensor_tensor(selp[:, :, :, :], by, hot_c[:, :, :].unsqueeze(2).broadcast_to((P, NT, TPC, CL)),
                                         ALU.mult))
            nc.vector.tensor_reduce(sel[:, :, :], selp[:, :, :, :], AX, ALU.add).then_inc(s["sel_ready"], 1)
            yield 40
            dve.wait_ge(s["exp_l"], 1)
            calibrate(link, el)
            link(first_max(link, hot_l))
            yield 41
            for t in range(NT):
                ins = nc.vector.tensor_tensor(hot[:, t, :, :], hot_c[:, t, :].unsqueeze(2).broadcast_to((P, CL, TPC)),
                                              hot_l[:, t, :].unsqueeze(1).broadcast_to((P, CL, TPC)), ALU.mult)
            ins.then_inc(s["hot_ready"], 1)
            yield 42
            dve.wait_ge(s["hot_tr"], 1)
            nc.vector.tensor_copy(hotT[:, :], bank1[2][0:TILES, 0:S]).then_inc(s["hotT_ready"], 1)
            dve.wait_ge(s["got_ready"], 1)
            link(nc.vector.tensor_copy(got[:, :, :], tri(bank1[0], 2)[:, :, 0:TBL]))
            dve.wait_ge(s["comp_ready"], 1)
            G = GRID
            for t in range(NT):
                ins = nc.vector.scalar_tensor_tensor(out=hh[:, t, :], in0=got[:, t, 0:G], scalar=comp[:, t, 0:1],
                                                     in1=got[:, t, 2 * G:3 * G], op0=ALU.mult, op1=ALU.add)
            link(ins)
            for t in range(NT):
                ins = nc.vector.scalar_tensor_tensor(out=hh[:, t, :], in0=got[:, t, G:2 * G], scalar=comp[:, t, 1:2],
                                                     in1=hh[:, t, :], op0=ALU.mult, op1=ALU.add)
            link(ins)
            for t in range(NT):
                ins = nc.vector.scalar_tensor_tensor(out=hh[:, t, :], in0=hh[:, t, :], scalar=0.0,
                                                     in1=got[:, t, 3 * G:4 * G], op0=ALU.max, op1=ALU.mult)
            link(ins)
            link(nc.vector.tensor_reduce(mag[:, :], hh[:, :, :], AX, ALU.add))
            link(nc.vector.tensor_tensor(mag[:, :], mag[:, :], got[:, :, 4 * G], ALU.add))
            link(nc.vector.tensor_scalar(mag[:, :], mag[:, :], col("oscale"), None, ALU.mult))
            for t in range(NT):
                ins = nc.vector.scalar_tensor_tensor(out=y1[:, t, :], in0=got[:, t, 4 * G + 1:TBL],
                                                     scalar=mag[:, t:t + 1], in1=x1[:, t, :], op0=ALU.mult, op1=ALU.add)
            link(ins)
            yield 43
            link(layer_norm(link, dve, y1, xn, st1, mv1, ve1, 1, 1))
            link(nc.vector.tensor_tensor(xn[:, :, :], xn[:, :, :], row_t("gamma"), ALU.mult))
            dve.wait_ge(s["x1b_ready"], 1)
            link(nc.vector.tensor_tensor(y1[:, :, :], xn[:, :, :], x1b[:, :, :], ALU.add))
            yield 44
            ins = layer_norm(link, dve, y1, x2, st1, mv1, ve1, 1, 2)
            ins.then_inc(s["x2_ready"], 1)
            dve.wait_ge(s["x2_ready"], 1)
            yield 45
            layer_norm(link, dve, x2, xn, st1, mv1, ve1, 1, 3).then_inc(s["xn_ready"], 1)
            yield 46
            dve.wait_ge(s["lin_proj"], 1)
            b = (P, NT, D)
            nc.vector.tensor_tensor(vlin1[:, :, 0, :], tri(bank1[3][:, S:2 * S], 2), row_t("bv_lin"), ALU.add)
            link(nc.vector.tensor_tensor(klin[:, :, :], tri(bank1[1][:, S:2 * S], 2), row_t("bk_lin"), ALU.add))
            nc.vector.tensor_scalar(q_e, bank1[1][:, 0:S], col("bq_lin"), 0.0, ALU.add, ALU.min)
            nc.vector.tensor_scalar(k_e[:, :, :], klin[:, :, :], 0.0, None, ALU.min).then_inc(s["klin_raw"], 1)
            link(nc.vector.tensor_scalar(qlinT, bank1[1][:, 0:S], col("bq_lin"), 0.0, ALU.add, ALU.max))
            link(nc.vector.tensor_scalar(klin[:, :, :], klin[:, :, :], 0.0, None, ALU.max))
            dve.wait_ge(s["q_exp"], 1)
            nc.vector.tensor_tensor(qlinT, q_e, qlinT, ALU.add).then_inc(s["qlin_ready"], 1)
            dve.wait_ge(s["k_exp"], 1)
            nc.vector.tensor_tensor(klin[:, :, :], k_e[:, :, :], klin[:, :, :], ALU.add).then_inc(s["klin_ready"], 1)
            yield 48
            dve.wait_ge(s["lin_done"], 1)
            link(nc.vector.tensor_scalar(den[:, :], bank1[3][:, S:2 * S], 1e-6, None, ALU.add))
            link(nc.vector.reciprocal(den[:, :], den[:, :]))
            nc.vector.tensor_tensor(linT, bank1[3][:, 0:S], den[:, :], ALU.mult).then_inc(s["linT_ready"], 1)

            def vm_copy(pp):
                dve.wait_ge(s["vm_proj"], pp + 1)
                for j in range(2):
                    src = bank1[3][:, pp * S + j * P:pp * S + (j + 1) * P]
                    dst = VM[:, j, :].rearrange("p (h n) -> p h n", h=WH)[:, :, 0:WD]
                    ins = nc.vector.tensor_copy(dst, src.rearrange("p (h n) -> p h n", h=WH))
                ins.then_inc(s["vm_ready"], 1)

            for u in range(8 + 2):
                yield kw(u)
                p, g = divmod(u, 4)
                if u == 0:
                    vm_copy(0)
                if u < 8:
                    dve.wait_ge(s["w_sc"], u + 1)
                    if u >= 3:
                        dve.wait_ge(s["w_tr"], u - 2)
                    nc.vector.tensor_tensor(Sw[:, u % 3, :, :], tri(bank1[u % 2], 4), bias_t[:, p, 4 * g:4 * g + 4, :],
                                            ALU.add).then_inc(s["w_max"], 1)
                    dve.wait_ge(s["w_max"], 2 * u + 1)
                    nc.vector.tensor_reduce(nmw[:, u % 3, :], Sw[:, u % 3, :, :], AX, ALU.max)\
                        .then_inc(s["w_max"], 1)
                if 1 <= u < 9:
                    v = u - 1
                    dve.wait_ge(s["w_exp"], v + 1)
                    link(nc.vector.tensor_reduce(rsw[:, v % 3, :], Sw[:, v % 3, :, :], AX, ALU.add))
                    nc.vector.reciprocal(rsw[:, v % 3, :], rsw[:, v % 3, :]).then_inc(s["w_sum"], 1)
                if u == 6:
                    vm_copy(1)
            yield kw(9) + 0.1
            dve.wait_ge(s["w_av"], 2)
            nc.vector.tensor_scalar(winT, bank1[3][:, 0:S], col("bv_loc"), None, ALU.add)\
                .then_inc(s["winT_ready"], 1)
            yield 66
            dve.wait_ge(s["g1_done"], 1)
            nc.vector.tensor_scalar(hidg[:, :], bank1[0][:, 0:S], col("bg1"), 0.0, ALU.add, ALU.max)\
                .then_inc(s["g1_ready"], 1)
            dve.wait_ge(s["winT_ready"], 1)
            dve.wait_ge(s["g1_done"], 1)
            link(nc.vector.tensor_tensor(linT, linT, winT, ALU.subtract))
            dve.wait_ge(s["g_exp"], 1)
            link(nc.vector.tensor_scalar(gt[:, :], gt[:, :], 1.0, None, ALU.add))
            link(nc.vector.reciprocal(gt[:, :], gt[:, :]))
            link(nc.vector.tensor_tensor(gt[:, :], gt[:, :], linT, ALU.mult))
            nc.vector.tensor_tensor(gt[:, :], gt[:, :], winT, ALU.add).then_inc(s["mixed"], 1)
            yield 68
            dve.wait_ge(s["o1_done"], 1)
            dve.wait_ge(s["x2b_ready"], 2)
            link(nc.vector.tensor_tensor(y1[:, :, :], tri(bank1[0][:, 0:S], 2), x2b[:, :, :], ALU.add))
            if both:
                dve.wait_ge(s["x3_taken"], 1)
            layer_norm(link, dve, y1, x3, st1, mv1, ve1, 1, 4).then_inc(s["x3_ready"], 1)

        def first_pool(pool):
            yield 0
            nc.gpsimd.tensor_tensor(xb[:, :, :], xr[:, :, :], row_t("bo0"), ALU.add).then_inc(s["xb_ready"], 1)
            for h in range(1, NH + 1):
                yield k0(h)
                g = h - 1
                pool.wait_ge(s["ri0_ready"], g + 1)
                nc.gpsimd.tensor_tensor(E0[:, g % 3, :, :], E0[:, g % 3, :, :],
                                        ri0[:, g, :].unsqueeze(2).broadcast_to((P, NT, S)), ALU.mult)\
                    .then_inc(s["norm0"], 1)
            yield k0(NH + 3)
            rstd_step(pool, 1, 0)
            yield 38
            pool.wait_ge(s["x1_ready"], 1)
            nc.gpsimd.tensor_tensor(x1b[:, :, :], x1[:, :, :], row_t("beta"), ALU.add).then_inc(s["x1b_ready"], 1)
            yield 43
            rstd_step(pool, 1, 1)
            yield 44
            rstd_step(pool, 1, 2)
            yield 45
            rstd_step(pool, 1, 3)
            yield 46
            pool.wait_ge(s["x2_ready"], 1)
            nc.gpsimd.tensor_tensor(x2b[:, :, :], x2[:, :, :], x2[:, :, :], ALU.add).then_inc(s["x2b_ready"], 1)
            pool.wait_ge(s["x2b_ready"], 1)
            nc.gpsimd.tensor_tensor(x2b[:, :, :], x2b[:, :, :], row_t("bo1"), ALU.add).then_inc(s["x2b_ready"], 1)
            pool.wait_ge(s["qloc_ready"], 1)
            for g in range(4):
                nc.gpsimd.tensor_tensor(GQ[:, 4 * g:4 * g + 4, :], qloc[:, :].unsqueeze(1).broadcast_to((P, 4, S)),
                                        col("headmask", 4 * g, 4).unsqueeze(2).broadcast_to((P, 4, S)), ALU.mult)\
                    .then_inc(s["qm_ready"], 1)
            for u in range(8 + 1):
                yield kw(u) + 0.05
                if u < 8:
                    pool.wait_ge(s["w_max"], 2 * u + 2)
                    nc.gpsimd.tensor_tensor(Sw[:, u % 3, :, :], Sw[:, u % 3, :, :],
                                            nmw[:, u % 3, :].unsqueeze(2).broadcast_to((P, 4, P)), ALU.subtract)\
                        .then_inc(s["w_sub"], 1)
                if u >= 1:
                    v = u - 1
                    pool.wait_ge(s["w_sum"], v + 1)
                    nc.gpsimd.tensor_tensor(Sw[:, v % 3, :, :], Sw[:, v % 3, :, :],
                                            rsw[:, v % 3, :].unsqueeze(2).broadcast_to((P, 4, P)), ALU.mult)\
                        .then_inc(s["w_norm"], 1)
            yield 68
            rstd_step(pool, 1, 4)

        QKU = [(half, kind, t) for half in range(2) for kind in range(2) for t in range(NT)]

        BLOCKS = [(0, 0), (1, 0), (1, 1)]

        def kq(u):
            return 6 + 1.5 * u

        def k2(h):
            return 19 + 1.3 * h

        def kx(e):
            return 48 + 3 * e

        def second_pe(pe):
            yield 1
            pe.wait_ge(s["xn2_ready"], 1)
            transposed(bank2[2], xn2).then_inc(s["tr2"], 1)
            pe.wait_ge(s["hT2_ready"], 1)
            for u in range(4):
                yield 2
                if u >= 2:
                    pe.wait_ge(s["v2_copied"], u - 1)
                t, c = divmod(u, 2)
                nc.tensor.matmul(bank2[u % 2], h2T[:, t * P:(t + 1) * P], wqkv[:, 2, c * 512:(c + 1) * 512],
                                 start=True, stop=True).then_inc(s["v2_proj"], 1)
            for u in range(len(QKU) + 1):
                yield kq(u)
                if u < len(QKU):
                    half, kind, t = QKU[u]
                    if u == 0:
                        pe.wait_ge(s["v2_copied"], 4)
                    if u >= 2:
                        pe.wait_ge(s["qn_ready"], u - 1)
                    nc.tensor.matmul(bank2[u % 2], h2T[:, t * P:(t + 1) * P],
                                     wqkv[:, kind, half * 512:(half + 1) * 512], start=True, stop=True)\
                        .then_inc(s["qk_proj"], 1)
                if u >= 1:
                    v = u - 1
                    pe.wait_ge(s["qn_ready"], v + 1)
                    if v >= 1:
                        qk_wait(pe, v - 1)
                    for c in range(4):
                        last = nc.tensor.transpose(bank2[2][:, c * P:(c + 1) * P],
                                                   qn[:, v % 2, 2 * c:2 * c + 2, :].rearrange("p a n -> p (a n)"),
                                                   ident[:, :])
                    last.then_inc(s["qk_tr"], 1)
            for h in range(NH + 3):
                yield k2(h)
                if h < NH:
                    if h == 0:
                        pe.wait_ge(s["q_copied"], 4)
                        pe.wait_ge(s["k_copied"], 4)
                    if h >= 2:
                        pe.wait_ge(s["exp2"], 2 * (h - 1))
                    c, r = h // 2, 64 * (h % 2)
                    for j, (t, k) in enumerate(BLOCKS):
                        o = bank2[h % 2][:, j * P:(j + 1) * P]
                        last = nc.tensor.matmul(o, QK[r:r + DH, 0, c, t * P:(t + 1) * P],
                                                QK[r:r + DH, 1, c, k * P:(k + 1) * P], start=True, stop=(t != k))
                        if t == k:
                            last = nc.tensor.matmul(o, ident_bf[:, :], causal[:, :], start=False, stop=True)
                    last.then_inc(s["sc2"], 1)
                g = h - 2
                if 0 <= g < NH:
                    pe.wait_ge(s["norm2"], g + 1)
                    if g >= 1:
                        et_wait(pe, "et2", g - 1)
                    for j in range(len(BLOCKS)):
                        last = nc.tensor.transpose(bank2[2][:, j * P:(j + 1) * P], E2[:, g % 3, j * P:(j + 1) * P],
                                                   ident[:, :])
                    last.then_inc(s["tr2e"], 1)
                g = h - 3
                if g >= 0:
                    et_wait(pe, "et2", g)
                    if g >= 2 and g % 2 == 0:
                        pe.wait_ge(s["ot2_done"], g // 2)
                    r = 64 * (g % 2)
                    for j, (t, k) in enumerate(BLOCKS):
                        last = nc.tensor.matmul(bank2[3][r:r + DH, t * P:(t + 1) * P], V2[:, k, g * DH:(g + 1) * DH],
                                                ET2[:, g % 2, j * P:(j + 1) * P], start=(k == 0), stop=(k == t))
                    last.then_inc(s["av2"], 1)
            yield k2(NH + 3)
            pe.wait_ge(s["ot2_done"], NC)
            out_proj(bank2[0], OT2, wo2).then_inc(s["wo2_done"], 1)
            yield 45
            pe.wait_ge(s["o2_ready"], 1)
            transposed(bank2[2], xn2).then_inc(s["o2_tr"], 1)
            pe.wait_ge(s["o2T_ready"], 1)
            for t in range(NT):
                last = nc.tensor.matmul(bank2[3][:, t * NE:(t + 1) * NE], h2T[:, t * P:(t + 1) * P], gate_w[:, :],
                                        start=True, stop=True)
            last.then_inc(s["gate_done"], 1)
            for u in range(2 * (NE + 1)):
                e, j = divmod(u, 2)
                yield kx(e)
                if e < NE:
                    if u >= 2:
                        pe.wait_ge(s["hid_ready"], 2 * (u - 1))
                    for f in range(2):
                        last = nc.tensor.matmul(bank2[u % 2][:, f * S:(f + 1) * S],
                                                w1[:, e, (2 * j + f) * P:(2 * j + f + 1) * P], h2T[:, :],
                                                start=True, stop=True)
                    last.then_inc(s["hid_done"], 1)
                if u == 1:
                    pe.wait_ge(s["gate_ready"], 1)
                    for t in range(NT):
                        last = nc.tensor.transpose(bank2[2][0:NE, t * P:(t + 1) * P], gl[:, t, :], ident[:, :])
                    last.then_inc(s["gate_tr"], 1)
                    pe.wait_ge(s["gateT_ready"], 1)
                    for t in range(NT):
                        last = nc.tensor.matmul(bank2[3][:, t * P:(t + 1) * P], gateT[:, t * P:(t + 1) * P], b2[:, :],
                                                start=True, stop=True)
                    last.then_inc(s["out_done"], 1)
                if e >= 1 and j == 1:
                    x = e - 1
                    pe.wait_ge(s["hid_ready"], 4 * (x + 1))
                    if x >= 1:
                        pe.wait_ge(s["out_used"], x)
                    for t in range(NT):
                        for f in range(FC):
                            last = nc.tensor.matmul(bank2[2 + x % 2][:, t * P:(t + 1) * P],
                                                    hid[:, x % 2, f, t * P:(t + 1) * P], w2[:, x, f, :],
                                                    start=(f == 0), stop=(f == FC - 1))
                    last.then_inc(s["out_done"], 1)

        def qk_wait(eng, v):
            kind = QKU[v][1]
            n = sum(1 for x in QKU[:v + 1] if x[1] == kind)
            eng.wait_ge(s["k_copied" if kind else "q_copied"], n)

        def second_act(act):
            yield 1
            act.wait_ge(s["tr2"], 1)
            nc.scalar.activation(h2T[:, :], bank2[2][:, 0:S], ACT.Identity, bias=col("f_b"), scale=col("f_g"))\
                .then_inc(s["hT2_ready"], 1)
            for u in range(4):
                yield 2
                t, c = divmod(u, 2)
                act.wait_ge(s["v2_proj"], u + 1)
                nc.scalar.activation(V2[:, t, c * 512:(c + 1) * 512], bank2[u % 2], ACT.Copy)\
                    .then_inc(s["v2_copied"], 1)
            for u in range(len(QKU) + 1):
                yield kq(u)
                if u < len(QKU):
                    act.wait_ge(s["qk_proj"], u + 1)
                    if u >= 2:
                        act.wait_ge(s["ss_ready"], u - 1)
                    nc.scalar.activation(sq[:, u % 2, :, :], tri(bank2[u % 2], 8), ACT.Square).then_inc(s["sq_ready"], 1)
                if u >= 1 and QKU[u - 1][1] == 0:
                    half, _, t = QKU[u - 1]
                    act.wait_ge(s["qk_tr"], u)
                    nc.scalar.activation(QK[:, 0, 4 * half:4 * half + 4, t * P:(t + 1) * P], tri(bank2[2], 4),
                                         ACT.Copy).then_inc(s["q_copied"], 1)
            for h in range(NH + 3):
                yield k2(h)
                if h < NH:
                    act.wait_ge(s["max2"], h + 1)
                    if h >= 3:
                        act.wait_ge(s["tr2e"], h - 2)
                    for t in range(NT):
                        o = slice(t * P, t * P + (t + 1) * P)
                        nc.scalar.activation(E2[:, h % 3, o], bank2[h % 2][:, o], ACT.Exp, bias=nm2[:, h, t:t + 1],
                                             accum_out=rs2[:, h, t:t + 1]).then_inc(s["exp2"], 1)
                g = h - 2
                if 0 <= g < NH and g % 2 == 0:
                    act.wait_ge(s["tr2e"], g + 1)
                    if g >= 2:
                        act.wait_ge(s["av2"], g - 1)
                    nc.scalar.activation(ET2[:, 0, :], bank2[2][:, 0:384], ACT.Copy).then_inc(s["et2_act"], 1)
                g = h - 3
                if g >= 0 and g % 2:
                    act.wait_ge(s["av2"], g + 1)
                    nc.scalar.activation(OT2[:, g // 2, :], bank2[3][:, 0:S], ACT.Copy).then_inc(s["ot2_done"], 1)
            yield 45
            act.wait_ge(s["o2_tr"], 1)
            nc.scalar.activation(h2T[:, :], bank2[2][:, 0:S], ACT.Identity, bias=col("f_b"), scale=col("f_g"))\
                .then_inc(s["o2T_ready"], 1)
            act.wait_ge(s["gl_ready"], 1)
            nc.scalar.activation(gl[:, :, :], gl[:, :, :], ACT.Exp).then_inc(s["gexp_done"], 1)
            for u in range(2 * NE):
                e, j = divmod(u, 2)
                yield kx(e)
                act.wait_ge(s["hid_done"], u + 1)
                if e >= 2:
                    act.wait_ge(s["out_done"], e)
                for f in range(2):
                    fc = 2 * j + f
                    nc.scalar.activation(hid[:, e % 2, fc, :], bank2[u % 2][:, f * S:(f + 1) * S], ACT.Gelu_apprx_tanh,
                                         bias=col("b1", e * FC + fc)).then_inc(s["hid_ready"], 1)

        def second_dve(dve):
            count = [0]

            def link(ins):
                count[0] += 1
                ins.then_inc(s["dve2"], 1)
                dve.wait_ge(s["dve2"], count[0])

            yield 0.5
            nc.vector.tensor_copy(xh[:, :, :], x3[:, :, :]).then_inc(s["x3_taken"], 1)
            dve.wait_ge(s["x3_taken"], 1)
            layer_norm(link, dve, xh, xn2, st2, mv2, ve2, 2, 0).then_inc(s["xn2_ready"], 1)
            for u in range(len(QKU) + 1):
                yield kq(u)
                if u < len(QKU):
                    dve.wait_ge(s["sq_ready"], u + 1)
                    link(nc.vector.tensor_reduce(ss[:, u, :], sq[:, u % 2, :, :], AX, ALU.add))
                    nc.vector.tensor_scalar(ss[:, u, :], ss[:, u, :], 1e-12, None, ALU.add).then_inc(s["ss_ready"], 1)
                if u >= 1 and QKU[u - 1][1] == 1:
                    half, _, t = QKU[u - 1]
                    dve.wait_ge(s["qk_tr"], u)
                    nc.vector.tensor_tensor(QK[:, 1, 4 * half:4 * half + 4, t * P:(t + 1) * P], tri(bank2[2], 4),
                                            kqs[:, 4 * half:4 * half + 4].unsqueeze(2).broadcast_to((P, 4, P)),
                                            ALU.mult).then_inc(s["k_copied"], 1)
                if u < len(QKU):
                    dve.wait_ge(s["rn_ready"], u + 1)
                    if u >= 2:
                        dve.wait_ge(s["qk_tr"], u - 1)
                    nc.vector.tensor_tensor(qn[:, u % 2, :, :], tri(bank2[u % 2], 8),
                                            rn[:, u, :].unsqueeze(2).broadcast_to((P, 8, DH)), ALU.mult)\
                        .then_inc(s["qn_ready"], 1)
            for h in range(NH + 3):
                yield k2(h)
                if h < NH:
                    dve.wait_ge(s["sc2"], h + 1)
                    for t in range(NT):
                        ins = nc.vector.tensor_reduce(nm2[:, h, t:t + 1], bank2[h % 2][:, t * P:t * P + (t + 1) * P],
                                                      AX, ALU.max, negate=True)
                    ins.then_inc(s["max2"], 1)
                if 1 <= h <= NH:
                    dve.wait_ge(s["exp2"], 2 * h)
                    nc.vector.reciprocal(ri2[:, h - 1, :], rs2[:, h - 1, :]).then_inc(s["ri2_ready"], 1)
                g = h - 2
                if 0 <= g < NH and g % 2:
                    dve.wait_ge(s["tr2e"], g + 1)
                    if g >= 2:
                        dve.wait_ge(s["av2"], g - 1)
                    nc.vector.tensor_copy(ET2[:, 1, :], bank2[2][:, 0:384]).then_inc(s["et2_dve"], 1)
            yield k2(NH + 3)
            dve.wait_ge(s["wo2_done"], 1)
            link(nc.vector.tensor_copy(acc[:, :, :], tri(bank2[0][:, 0:S], 2)))
            layer_norm(link, dve, acc, xn2, st2, mv2, ve2, 2, 1).then_inc(s["o2_ready"], 1)
            yield 45
            b = (P, NT, NE)
            dve.wait_ge(s["gate_done"], 1)
            link(nc.vector.tensor_tensor(gl[:, :, :], tri(bank2[3][:, 0:NT * NE], NT), row_t("gate_b"), ALU.add))
            link(nc.vector.tensor_reduce(gm[:, :], gl[:, :, :], AX, ALU.max))
            nc.vector.tensor_tensor(gl[:, :, :], gl[:, :, :], gm[:, :].unsqueeze(2).broadcast_to(b), ALU.subtract)\
                .then_inc(s["gl_ready"], 1)
            dve.wait_ge(s["gexp_done"], 1)
            link(nc.vector.tensor_reduce(gs[:, :], gl[:, :, :], AX, ALU.add))
            link(nc.vector.reciprocal(gs[:, :], gs[:, :]))
            nc.vector.tensor_tensor(gl[:, :, :], gl[:, :, :], gs[:, :].unsqueeze(2).broadcast_to(b), ALU.mult)\
                .then_inc(s["gate_ready"], 1)
            yield kx(0)
            dve.wait_ge(s["gate_tr"], 1)
            nc.vector.tensor_copy(gateT[:, :], bank2[2][0:NE, 0:S]).then_inc(s["gateT_ready"], 1)
            dve.wait_ge(s["out_done"], 1)
            nc.vector.tensor_copy(acc[:, :, :], tri(bank2[3][:, 0:S], 2)).then_inc(s["out_used"], 1)
            dve.wait_ge(s["out_used"], 1)
            for x in range(NE):
                yield kx(x + 1)
                dve.wait_ge(s["out_done"], x + 2)
                for t in range(NT):
                    ins = nc.vector.scalar_tensor_tensor(out=acc[:, t, :], in0=bank2[2 + x % 2][:, t * P:(t + 1) * P],
                                                         scalar=gl[:, t, x:x + 1], in1=acc[:, t, :],
                                                         op0=ALU.mult, op1=ALU.add)
                ins.then_inc(s["out_used"], 1)
                dve.wait_ge(s["out_used"], x + 2)
            yield kx(NE) + 1
            link(layer_norm(link, dve, acc, xn2, st2, mv2, ve2, 2, 2))
            link(nc.vector.tensor_tensor(xn2[:, :, :], xn2[:, :, :], row_t("f_g"), ALU.mult))
            link(nc.vector.tensor_tensor(xn2[:, :, :], xn2[:, :, :], row_t("f_b"), ALU.add))
            link(nc.vector.tensor_tensor(acc[:, :, :], xn2[:, :, :], xh[:, :, :], ALU.add))
            layer_norm(link, dve, acc, yo, st2, mv2, ve2, 2, 3).then_inc(s["y_ready"], 1)

        def second_pool(pool):
            yield 0.5
            rstd_step(pool, 2, 0)
            for u in range(len(QKU)):
                yield kq(u)
                pool.wait_ge(s["ss_ready"], u + 1)
                nc.gpsimd.tensor_tensor(rn[:, u, :], ss[:, u, :], half_neg[:, 0:8], ALU.pow).then_inc(s["rn_ready"], 1)
            for h in range(1, NH + 1):
                yield k2(h)
                g = h - 1
                pool.wait_ge(s["ri2_ready"], g + 1)
                for t in range(NT):
                    o = slice(t * P, t * P + (t + 1) * P)
                    ins = nc.gpsimd.tensor_tensor(E2[:, g % 3, o], E2[:, g % 3, o],
                                                  ri2[:, g, t:t + 1].broadcast_to((P, (t + 1) * P)), ALU.mult)
                ins.then_inc(s["norm2"], 1)
            yield k2(NH + 3)
            rstd_step(pool, 2, 1)
            yield kx(NE) + 1
            rstd_step(pool, 2, 2)
            rstd_step(pool, 2, 3)

        def second_sync(sp, batch):
            yield kx(NE) + 2
            sp.wait_ge(s["y_ready"], 1)
            sp.dma_start(d["y"][bass.ds(batch, 1), :, :, :].rearrange("a p t n -> (a p) t n"), yo[:, :, :])\
                .then_inc(s["y_stored"], 16)
            sp.wait_ge(s["y_stored"], 16)

        def body(first, second, i=0):
            def programs(eng, of_first, of_second):
                merged(*([of_first(eng)] if first else []), *([of_second(eng)] if second else []))

            with nc.Block(no_gpsimd_drain=True) as block:
                @block.vector
                def _(dve):
                    programs(dve, lambda e: first_dve(e, second), second_dve)

                @block.tensor
                def _(pe):
                    programs(pe, first_pe, second_pe)

                @block.scalar
                def _(act):
                    programs(act, first_act, second_act)

                @block.gpsimd
                def _(pool):
                    programs(pool, first_pool, second_pool)

                @block.sync
                def _(sp):
                    programs(sp, lambda e: first_sync(e, i + 2 if second else 1), lambda e: second_sync(e, i))
            nc.sync.sem_clear(loop_sems)
            nc.all_engine_barrier(sem_only=True)

        body(True, False)
        nc.sync.wait_ge(w_second, 16 * len(second_loads))
        nc.all_engine_barrier(sem_only=True)
        with nc.Fori(0, NB - 1) as i:
            body(True, True, i)
        body(False, True, NB - 1)


def kernel(**inputs):
    import numpy as np
    import concourse.bacc as bacc
    from concourse.bass_utils import run_bass_kernel_spmd

    x = {k: np.asarray(v) for k, v in inputs.items()}
    f = np.float32
    X = x["L0_attn_hidden_states"]
    nb = X.shape[0]
    pad = np.zeros((1, P, S), f)

    def chunks(w):
        return w.reshape(-1, P, w.shape[-1]).transpose(1, 0, 2)

    def heads_T(w):
        return w.reshape(D, NH, DH).transpose(2, 1, 0)

    col_of = {"l1_g": x["L1_attn_ln_g"], "l1_b": x["L1_attn_ln_b"], "bq_lin": x["L1_attn_bq_lin"],
              "bq_loc": x["L1_attn_bq_loc"], "bk_loc": x["L1_attn_bk_loc"], "bv_loc": x["L1_attn_bv_loc"],
              "bg1": x["L1_attn_bg1"], "bg2": x["L1_attn_bg2"], "f_g": x["L1_ffn_ln_g"], "f_b": x["L1_ffn_ln_b"],
              "oscale": np.broadcast_to(x["L0_ffn_output_scale"], (P,)),
              "temp": np.broadcast_to(x["L0_ffn_temperature"], (P,)),
              "qs": x["L1_ffn_q_scale"].reshape(NC, P).T, "ks": x["L1_ffn_k_scale"].reshape(NC, P).T,
              "b1": x["L1_ffn_b1"].reshape(NE * FC, P).T,
              "headmask": np.where(np.arange(P)[:, None] // WD == np.arange(WH), f(WD ** -0.5), f(0))}
    cols = np.zeros((P, N_COLS), f)
    for name, v in col_of.items():
        at, n = COLS[name]
        cols[:, at:at + n] = v.reshape(P, n)
    cols[0:COMP, COLS["cb1"][0]] = x["L0_ffn_compress_b1"]
    row_of = {"bo0": x["L0_attn_bo"], "gamma": x["L0_ffn_norm_gamma"], "beta": x["L0_ffn_norm_beta"],
              "bk_lin": x["L1_attn_bk_lin"], "bv_lin": x["L1_attn_bv_lin"], "bo1": x["L1_attn_bo"],
              "f_g": x["L1_ffn_ln_g"], "f_b": x["L1_ffn_ln_b"], "gate_b": x["L1_ffn_gate_b"],
              "knots": x["L0_ffn_knot_values"], "jlo": np.arange(KN - 1, dtype=f),
              "jhi": np.array([*range(1, KN - 1), 1e30], f), "first": np.arange(8, 0, -1, dtype=f)}
    rows = np.zeros((P, N_ROWS), f)
    for name, v in row_of.items():
        at, n = ROWS[name]
        rows[:, at:at + n] = v
    query = np.arange(P)[:, None] + P * np.arange(2)
    key = np.array(KEY0)[query // QT][:, :, None] + np.arange(P)
    off = key - query[:, :, None]
    seen = np.abs(off) <= HALF
    rel = x["L1_attn_rel_bias"]
    bias_t = np.where(seen[..., None], rel[np.where(seen, off, 0) + 2 * HALF], f(NEG)).transpose(0, 1, 3, 2)

    wkv = x["L0_attn_Wkv"]
    names = ["wq_lin", "wk_lin", "wv_lin", "wq_loc", "wk_loc", "wv_loc"]
    arrays = {
        "xT": np.concatenate([X.transpose(0, 2, 1), pad]),
        "xr": np.concatenate([X.reshape(nb, NT, P, D).transpose(0, 2, 1, 3), pad.reshape(1, P, NT, D)]),
        "wqT": heads_T(x["L0_attn_Wq"]), "wkT": heads_T(wkv[:, :NH * DH]), "wv0": wkv[:, NH * DH:],
        "wo0": chunks(x["L0_attn_Wo"]), "sigT": x["L0_ffn_signatures_raw"].T, "cw1": x["L0_ffn_compress_w1"],
        "cw2": np.concatenate([x["L0_ffn_compress_w2"], x["L0_ffn_compress_b2"][None]]),
        "tbl": np.concatenate([x["L0_ffn_spline_w1"].reshape(TILES, -1), x["L0_ffn_spline_b1"],
                               x["L0_ffn_spline_w2"].reshape(TILES, -1), x["L0_ffn_spline_b2"],
                               x["L0_ffn_directions"]], axis=1),
        "w1a": np.stack([x["L1_attn_" + n] for n in names], axis=1),
        "wg1": chunks(x["L1_attn_wg1"]), "wg2": x["L1_attn_wg2"], "wo1": x["L1_attn_wo"], "bias_t": bias_t,
        "wqkv": np.stack([x["L1_ffn_Wq"], x["L1_ffn_Wk"], x["L1_ffn_Wv"]], axis=1),
        "wo2": chunks(x["L1_ffn_Wo"]), "gate_w": x["L1_ffn_gate_w"],
        "w1": x["L1_ffn_w1"].transpose(1, 0, 2),
        "w2": x["L1_ffn_w2"].reshape(NE, FC, P, D).transpose(2, 0, 1, 3), "b2": x["L1_ffn_b2"],
        "cols": cols, "rows": rows, "ident": np.eye(P, dtype=f),
    }
    arrays = {k: np.ascontiguousarray(v, dtype=f) for k, v in arrays.items()}
    nc = bacc.Bacc("TRN2", target_bir_lowering=False, num_devices=1)
    d = {k: nc.dram_tensor("in_" + k, v.shape, F32, kind="ExternalInput").ap() for k, v in arrays.items()}
    d["y"] = nc.dram_tensor("out_y", (NB, P, NT, D), F32, kind="ExternalOutput").ap()
    whole_net(nc, d)
    r = run_bass_kernel_spmd(nc, [{"in_" + k: v for k, v in arrays.items()}], core_ids=[0])
    return r.results[0]["out_y"].transpose(0, 2, 1, 3).reshape(NB, S, D)
```

```python
import concourse.bass as bass
from concourse import mybir
from contextlib import ExitStack

F32 = mybir.dt.float32
BF16 = mybir.dt.bfloat16
ALU = mybir.AluOpType
ACT = mybir.ActivationFunctionType
AX = mybir.AxisListType.X

NB, S, D = 16, 256, 128
P = 128
NT = S // P
NH, DH = 16, 64
NC = NH * DH // P
CL, TPC, KN = 8, 8, 8
TILES = CL * TPC
GRID, COMP = 16, 32
WH, WD = 16, 8
QT = 64
HALF = 32
KEY0 = [0, 32, 96, 128]
NE, FF = 8, 512
FC = FF // P
EPS = 1e-5
NEG = -1e30
CAUSAL_FILL = -1e9
TBL = 2 * GRID + GRID + GRID + 1 + D

COLS = {}
ROWS = {}


def _place(table, names):
    at = 0
    for name, n in names:
        table[name] = (at, n)
        at += n
    return at


N_COLS = _place(COLS, [("l1_g", 1), ("l1_b", 1), ("bq_lin", 1), ("bq_loc", 1), ("bk_loc", 1), ("bv_loc", 1),
                       ("bg1", 1), ("bg2", 1), ("f_g", 1), ("f_b", 1), ("cb1", 1), ("oscale", 1), ("temp", 1),
                       ("qs", NC), ("ks", NC), ("b1", NE * FC), ("headmask", WH)])
N_ROWS = _place(ROWS, [("bo0", D), ("gamma", D), ("beta", D), ("bk_lin", D), ("bv_lin", D), ("bo1", D),
                       ("f_g", D), ("f_b", D), ("gate_b", NE), ("knots", KN), ("jlo", KN - 1), ("jhi", KN - 1),
                       ("first", 8)])


def merged(*programs):
    live = [[next(g, None), g] for g in programs]
    while live := [x for x in live if x[0] is not None]:
        first = min(live, key=lambda x: x[0])
        first[0] = next(first[1], None)


def whole_net(nc, d):
    ctx = ExitStack()
    with ctx:
        def sb(name, shape, dt=F32):
            return ctx.enter_context(nc.sbuf_tensor(name, shape, dt))

        def sem(name):
            return ctx.enter_context(nc.semaphore(name))

        cols = sb("cols", [P, N_COLS])
        rows = sb("rows", [P, N_ROWS])
        ident = sb("ident", [P, P])
        ident_bf = sb("ident_bf", [P, P], BF16)
        causal = sb("causal", [P, P], BF16)
        A = sb("A", [P, NH, P])
        wv0 = sb("wv0", [P, NH * DH])
        wo0 = sb("wo0", [P, NC, D])
        router = sb("router", [P, CL + TILES])
        cw1 = sb("cw1", [P, COMP])
        cw2 = sb("cw2", [COMP + 1, 2])
        tbl = sb("tbl", [TILES, TBL])
        w1a = sb("w1a", [P, 6, D])
        wg1 = sb("wg1", [P, 3, D])
        wg2 = sb("wg2", [P, D])
        wo1 = sb("wo1", [P, D])
        bias_t = sb("bias_t", [P, 2, WH, P])
        wqkv = sb("wqkv", [P, 3, NH * DH])
        wo2 = sb("wo2", [P, NC, D])
        gate_w = sb("gate_w", [P, NE])
        w1 = sb("w1", [P, NE, FF])
        w2 = sb("w2", [P, NE, FC, D])
        b2 = sb("b2", [NE, D])
        half_neg = sb("half_neg", [P, 32])
        neg_bg2 = sb("neg_bg2", [P, 1])
        inv_t = sb("inv_t", [P, 1])
        kqs = sb("kqs", [P, NC])
        knot_tab = sb("knot_tab", [P, 3, KN - 1])

        xT = sb("xT", [P, S])
        xr = sb("xr", [P, NT, D])
        xb = sb("xb", [P, NT, D])
        GQ = sb("GQ", [P, NH, S])
        OT0 = GQ[:, :, :].rearrange("p (c a) n -> p c a n", a=2)[:, :, 0, :]
        ETw = sb("ETw", [P, WH, P])
        V0 = ETw[:, :, :].rearrange("p (t a) n -> p t (a n)", t=NT)
        E0 = sb("E0", [P, 3, NT, S])
        ET0 = sb("ET0", [P, 2, 2, S])
        nm0 = sb("nm0", [P, NH, NT])
        rs0 = sb("rs0", [P, NH, NT])
        ri0 = sb("ri0", [P, NH, NT])
        y1 = sb("y1", [P, NT, D])
        x1 = sb("x1", [P, NT, D])
        x1b = xb
        x2 = sb("x2", [P, NT, D])
        x2b = xb
        xn = sb("xn", [P, NT, D])
        x3 = sb("x3", [P, NT, D])
        fT = sb("fT", [P, S])
        hT = sb("hT", [P, S])
        st1 = sb("st1", [P, NT, 6])
        mv1 = sb("mv1", [P, NT, 2])
        ve1 = sb("ve1", [P, NT])
        rstd1 = sb("rstd1", [P, NT])
        scores = sb("scores", [P, NT, CL + TILES])
        gel = sb("gel", [COMP + 1, S])
        comp = sb("comp", [P, NT, 2])
        ec = sb("ec", [P, NT * 8])
        el = sb("el", [P, NT * 8])
        fx = sb("fx", [P, NT * 8])
        m_a = sb("m_a", [P, NT * 8, KN - 1])
        m_b = sb("m_b", [P, NT * 8, KN - 1])
        pick = sb("pick", [P, NT * 8, 3, KN - 1])
        picked = sb("picked", [P, NT * 8, 3])
        gates = sb("gates", [P, NT, 8])
        gmax = sb("gmax", [P, NT])
        hot_c = sb("hot_c", [P, NT, 8])
        hot_l = sb("hot_l", [P, NT, 8])
        selp = sb("selp", [P, NT, TPC, CL])
        sel = sb("sel", [P, NT, TPC])
        hot = sb("hot", [P, NT, CL, TPC])
        hotT = sb("hotT", [TILES, S])
        got = sb("got", [P, NT, TBL])
        hh = sb("hh", [P, NT, GRID])
        mag = sb("mag", [P, NT])
        qlinT = ET0[:, 0, 0, :]
        q_e = ET0[:, 0, 1, :]
        klin = ET0[:, 1, 0, :].rearrange("p (t n) -> p t n", t=NT)
        k_e = ET0[:, 1, 1, :].rearrange("p (t n) -> p t n", t=NT)
        vlin1 = sb("vlin1", [P, NT, 2, D])
        kv = sb("kv", [P, 2, D])
        den = fT
        linT = qlinT
        winT = q_e
        qloc = sb("qloc", [P, S])
        kloc = sb("kloc", [P, S])
        VM = sb("VM", [P, 2, WH * (P + WD)])
        Sw = E0[:, :, :, :].rearrange("p a t (g n) -> p a (t g) n", n=P)
        nmw = sb("nmw", [P, 3, 4])
        rsw = sb("rsw", [P, 3, 4])
        hidg = qloc
        gt = kloc

        xh = sb("xh", [P, NT, D])
        xn2 = sb("xn2", [P, NT, D])
        h2T = sb("h2T", [P, S])
        QK = sb("QK", [P, 2, NC, S])
        hid = QK[:, :, :, :].rearrange("p a (g f) n -> p (a g) f n", f=FC)
        V2 = sb("V2", [P, NT, NH * DH])
        OT2 = QK[:, 0, :, :]
        work2 = sb("work2", [P, 2048])
        sq = work2[:, 0:1024].rearrange("p (a h n) -> p a h n", a=2, h=8)
        qn = work2[:, 1024:2048].rearrange("p (a h n) -> p a h n", a=2, h=8)
        ss = sb("ss", [P, 8, 8])
        rn = sb("rn", [P, 8, 8])
        E2 = work2[:, 0:1152].rearrange("p (a n) -> p a n", a=3)
        ET2 = work2[:, 1152:1920].rearrange("p (a n) -> p a n", a=2)
        nm2 = sb("nm2", [P, NH, NT])
        rs2 = sb("rs2", [P, NH, NT])
        ri2 = sb("ri2", [P, NH, NT])
        st2 = sb("st2", [P, NT, 6])
        mv2 = sb("mv2", [P, NT, 2])
        ve2 = sb("ve2", [P, NT])
        rstd2 = sb("rstd2", [P, NT])
        gl = sb("gl", [P, NT, NE])
        gm = sb("gm", [P, NT])
        gs = sb("gs", [P, NT])
        gateT = sb("gateT", [NE, S])
        acc = sb("acc", [P, NT, D])
        yo = xn2

        wqT = GQ[0:DH, :, :].rearrange("p h n -> p (h n)")[:, 0:NH * P].rearrange("p (h n) -> p h n", h=NH)
        wkT = GQ[0:DH, :, :].rearrange("p h n -> p (h n)")[:, NH * P:2 * NH * P].rearrange("p (h n) -> p h n", h=NH)
        raw = GQ[:, 0, :]

        ps = ctx.enter_context(nc.psum_tensor("ps", [P, 8, 512], F32))
        bank1 = [ps[:, n, :] for n in range(4)]
        bank2 = [ps[:, 4 + n, :] for n in range(4)]

        def col(name, n=0, w=1):
            at = COLS[name][0] + n
            return cols[:, at:at + w]

        def row(name):
            at, n = ROWS[name]
            return rows[:, at:at + n]

        def row_t(name):
            at, n = ROWS[name]
            return rows[:, at:at + n].unsqueeze(1).broadcast_to((P, NT, n))

        def tri(ap, a):
            return ap.rearrange("p (a n) -> p a n", a=a)

        w_first = sem("w_first")
        w_second = sem("w_second")
        setup_pool = sem("setup_pool")
        setup_dve = sem("setup_dve")
        a_ready = sem("a_ready")
        a_copied = sem("a_copied")

        first_loads = [(wqT, d["wqT"]), (wkT, d["wkT"]), (cols[:, :], d["cols"]), (rows[:, :], d["rows"]),
                       (ident[:, :], d["ident"]), (xT[:, :], d["xT"][0, :, :]), (xr[:, :, :], d["xr"][0, :, :, :]),
                       (wv0[:, :], d["wv0"]), (wo0[:, :, :], d["wo0"]), (router[:, CL:CL + TILES], d["sigT"]),
                       (cw1[:, :], d["cw1"]), (cw2[:, :], d["cw2"]), (tbl[:, :], d["tbl"]),
                       (w1a[:, :, :], d["w1a"]), (wg1[:, :, :], d["wg1"]), (wg2[:, :], d["wg2"]),
                       (wo1[:, :], d["wo1"]), (bias_t[:, :, :, :], d["bias_t"])]
        second_loads = [(wqkv[:, :, :], d["wqkv"]), (wo2[:, :, :], d["wo2"]), (gate_w[:, :], d["gate_w"]),
                        (w1[:, :, :], d["w1"]), (w2[:, :, :, :], d["w2"]), (b2[:, :], d["b2"])]

        with nc.Block(no_gpsimd_drain=True) as block:
            @block.sync
            def _(sp):
                for dst, src in first_loads:
                    sp.dma_start(dst, src).then_inc(w_first, 16)
                for dst, src in second_loads:
                    sp.dma_start(dst, src).then_inc(w_second, 16)

            @block.gpsimd
            def _(pool):
                for n, (ap, value) in enumerate(((half_neg[:, :], -0.5), (vlin1[:, :, 1, :], 1.0), (gel[COMP:COMP + 1, :], 1.0),
                                                 (causal[:, :], 0.0), (VM[:, :, :], 0.0))):
                    nc.gpsimd.memset(ap, value).then_inc(setup_pool, 1)
                    pool.wait_ge(setup_pool, n + 1)
                nc.gpsimd.affine_select(out=causal[:, :], in_=causal[:, :], compare_op=ALU.is_ge, fill=CAUSAL_FILL,
                                        base=0, pattern=[[-1, P]], channel_multiplier=1)

            @block.vector
            def _(dve):
                n = [0]

                def link(ins):
                    n[0] += 1
                    ins.then_inc(setup_dve, 1)
                    dve.wait_ge(setup_dve, n[0])

                dve.wait_ge(w_first, 16 * len(first_loads))
                nc.vector.tensor_copy(ident_bf[:, :], ident[:, :])
                nc.vector.tensor_scalar(neg_bg2[:, :], col("bg2"), -1.0, None, ALU.mult)
                link(nc.vector.tensor_scalar(inv_t[:, :], col("temp"), 1e-6, None, ALU.add))
                link(nc.vector.reciprocal(inv_t[:, :], inv_t[:, :]))
                link(nc.vector.tensor_tensor(kqs[:, :], col("qs", 0, NC), col("ks", 0, NC), ALU.mult))
                link(nc.vector.tensor_scalar(kqs[:, :], kqs[:, :], 10.0, None, ALU.mult))
                k = row("knots")
                nc.vector.tensor_copy(knot_tab[:, 0, :], k[:, 0:KN - 1])
                nc.vector.tensor_tensor(knot_tab[:, 1, :], k[:, 1:KN], k[:, 0:KN - 1], ALU.subtract)
                nc.vector.tensor_copy(knot_tab[:, 2, :], row("jlo"))
                dve.wait_ge(a_ready, 4)
                sig = router[:, CL:CL + TILES]
                q, low = raw[:, 0:TILES], raw[:, TILES:2 * TILES]
                nc.vector.tensor_scalar(q, sig, 0.3, None, ALU.is_gt)
                link(nc.vector.tensor_scalar(low, sig, -0.3, None, ALU.is_lt))
                link(nc.vector.tensor_tensor(q, q, low, ALU.subtract))
                link(nc.vector.tensor_tensor(q, q, sig, ALU.subtract))
                link(nc.vector.tensor_tensor(sig, sig, q, ALU.add))
                by = sig.rearrange("p (c t) -> p t c", c=CL)
                total, neg = raw[:, 128:128 + CL], raw[:, 136:136 + CL]
                link(nc.vector.tensor_tensor(total, by[:, 0, :], by[:, 1, :], ALU.add))
                for t in range(2, TPC):
                    link(nc.vector.tensor_tensor(total, total, by[:, t, :], ALU.add))
                nc.vector.tensor_scalar(neg, total, 0.0, None, ALU.is_lt)
                link(nc.vector.tensor_scalar(total, total, 0.0, None, ALU.is_gt))
                link(nc.vector.tensor_tensor(router[:, 0:CL], total, neg, ALU.subtract))

            @block.tensor
            def _(pe):
                pe.wait_ge(w_first, 16 * len(first_loads))
                for u in range(4):
                    for h in range(4 * u, 4 * u + 4):
                        last = nc.tensor.matmul(bank1[u][:, (h % 4) * P:(h % 4 + 1) * P], wqT[:, h, :], wkT[:, h, :],
                                                start=True, stop=True)
                    last.then_inc(a_ready, 1)

            @block.scalar
            def _(act):
                for u in range(4):
                    act.wait_ge(a_ready, u + 1)
                    nc.scalar.activation(A[:, 4 * u:4 * u + 4, :], tri(bank1[u], 4), ACT.Copy).then_inc(a_copied, 1)
                act.wait_ge(a_copied, 4)

        names = """
            x_next x_taken
            proj0 proj0_act proj0_dve sc0 max0 exp0 ri0_ready norm0 tr0 et0_act et0_dve av0 ot0_act wo0_done
            xb_ready dve1 ve1_ready rstd1_ready x1b_ready
            x1_ready x1tr x1T_ready route_ready gelu_ready compress_ready comp_ready sc_copied exp_c sel_ready exp_l
            hot_ready hot_tr hotT_ready got_ready x2_ready x2b_ready xn_ready xn_tr hT_ready
            lin_proj q_exp k_exp klin_raw qlin_ready klin_ready kv_done kv_copied lin_done lin_ready linT_ready
            loc_q loc_kv qloc_ready kloc_ready qm_ready vm_ready vm_proj
            w_sc w_max w_sub w_exp w_sum w_norm w_tr w_et w_av winT_ready
            g1_done g1_ready g2_done g_exp mixed o1_done x3_ready
            x3_taken dve2 ve2_ready rstd2_ready xn2_ready tr2 hT2_ready
            v2_proj v2_copied qk_proj sq_ready ss_ready rn_ready qn_ready qk_tr q_copied k_copied
            sc2 max2 exp2 ri2_ready norm2 tr2e et2_act et2_dve av2 ot2_done wo2_done
            o2_ready o2_tr o2T_ready gate_done gl_ready gexp_done gate_ready gate_tr gateT_ready
            hid_done hid_ready out_done out_used y_ready y_stored
        """.split()
        s = {name: sem(name) for name in names}
        loop_sems = range(min(x.num for x in s.values()), max(x.num for x in s.values()) + 1)
        assert len(loop_sems) == len(names)

        class Chain:

            def __init__(self, eng, name):
                self.eng, self.sem, self.n, self.key, self.step = eng, s[name], 0, 0.0, 0.0

            def at(self, key, until=None, steps=0):
                self.key, self.step = key, (until - key) / (steps + 1) if steps else 0.0
                return key

            def __call__(self, ins):
                self.n += 1
                ins.then_inc(self.sem, 1)
                self.key += self.step
                yield self.key
                self.eng.wait_ge(self.sem, self.n)

        K = dict(h0=12, h0d=3.0, w=108, wd=2.6, g=134, q=8, qd=2.2, h2=27, h2d=2.8, o=79, e=86, ed=5, z=128)

        KN_W = 3.0

        def kp(u):
            return 0.9 * u

        def k0(h):
            return K["h0"] + K["h0d"] * h

        def kw(u):
            return K["w"] + K["wd"] * u

        def kf(x):
            return k0(NH + 3) + (kw(0) - k0(NH + 3)) * x

        def kv2(u):
            return KN_W + 1 + u

        def kq(u):
            return K["q"] + K["qd"] * u

        def k2(h):
            return K["h2"] + K["h2d"] * h

        def kx(e):
            return K["e"] + K["ed"] * e

        NORM = {1: [k0(NH + 3) + 0.5, kf(0.68), kf(0.75), kf(0.82), K["g"] + 7],
                2: [0.1, K["o"] + 0.05, K["z"], K["z"] + KN_W + 2]}

        def first_sync(sp, next_batch):
            yield k0(NH)
            sp.wait_ge(s["sc0"], NH)
            sp.wait_ge(s["xb_ready"], 1)
            sp.wait_ge(s["proj0"], 12)
            sp.dma_start(xT[:, :], d["xT"][bass.ds(next_batch, 1), :, :].rearrange("a p n -> (a p) n"))\
                .then_inc(s["x_next"], 16)
            sp.dma_start(xr[:, :, :], d["xr"][bass.ds(next_batch, 1), :, :, :].rearrange("a p t n -> (a p) t n"))\
                .then_inc(s["x_next"], 16)
            yield 1000
            sp.wait_ge(s["x_next"], 32)

        def proj_bank(u):
            return bank1[u % 3]

        def first_pe(pe):
            for u in range(12):
                yield kp(u)
                if u >= 3:
                    v = u - 3
                    pe.wait_ge(s["proj0_dve" if v % 2 else "proj0_act"], v // 2 + 1)
                if u < 8:
                    for j in range(2):
                        last = nc.tensor.matmul(proj_bank(u)[:, j * S:(j + 1) * S], A[:, 2 * u + j, :], xT[:, :],
                                                start=True, stop=True)
                else:
                    t, c = divmod(u - 8, 2)
                    last = nc.tensor.matmul(proj_bank(u), xT[:, t * P:(t + 1) * P], wv0[:, c * 512:(c + 1) * 512],
                                            start=True, stop=True)
                last.then_inc(s["proj0"], 1)
            for h in range(NH + 3):
                yield k0(h)
                if h < NH:
                    if h == 0:
                        pe.wait_ge(s["proj0_act"], 6)
                        pe.wait_ge(s["proj0_dve"], 6)
                    if h >= 2:
                        pe.wait_ge(s["exp0"], 2 * (h - 1))
                    for t in range(NT):
                        last = nc.tensor.matmul(bank1[h % 2][:, t * S:(t + 1) * S], GQ[:, h, t * P:(t + 1) * P],
                                                xT[:, :], start=True, stop=True)
                    last.then_inc(s["sc0"], 1)
                if 0 <= h - 2 < NH:
                    g = h - 2
                    pe.wait_ge(s["norm0"], g + 1)
                    if g >= 1:
                        et_wait(pe, "et0", g - 1)
                    for k in range(2):
                        for t in range(NT):
                            last = nc.tensor.transpose(bank1[2][:, k * S + t * P:k * S + (t + 1) * P],
                                                       E0[:, g % 3, t, k * P:(k + 1) * P], ident[:, :])
                    last.then_inc(s["tr0"], 1)
                if 0 <= h - 3:
                    g = h - 3
                    et_wait(pe, "et0", g)
                    if g >= 2 and g % 2 == 0:
                        pe.wait_ge(s["ot0_act"], g // 2)
                    r = 64 * (g % 2)
                    for k in range(2):
                        last = nc.tensor.matmul(bank1[3][r:r + DH, 0:S], V0[:, k, g * DH:(g + 1) * DH],
                                                ET0[:, g % 2, k, :], start=(k == 0), stop=(k == 1))
                    last.then_inc(s["av0"], 1)
            yield k0(NH + 3)
            pe.wait_ge(s["ot0_act"], NC)
            out_proj(bank1[0], OT0, wo0).then_inc(s["wo0_done"], 1)
            yield kf(0.1)
            pe.wait_ge(s["x1_ready"], 1)
            transposed(bank1[2], x1).then_inc(s["x1tr"], 1)
            yield kf(0.13)
            pe.wait_ge(s["x1T_ready"], 1)
            last = nc.tensor.matmul(bank1[1][0:COMP, 0:S], cw1[:, :], fT[:, :], start=True, stop=True)
            for t in range(NT):
                last = nc.tensor.matmul(bank1[0][:, t * P:t * P + CL + TILES], fT[:, t * P:(t + 1) * P], router[:, :],
                                        start=True, stop=True)
            last.then_inc(s["route_ready"], 1)
            yield kf(0.16)
            pe.wait_ge(s["gelu_ready"], 1)
            for t in range(NT):
                last = nc.tensor.matmul(bank1[3][:, 2 * t:2 * t + 2], gel[:, t * P:(t + 1) * P], cw2[:, :],
                                        start=True, stop=True)
            last.then_inc(s["compress_ready"], 1)
            yield kf(0.58)
            pe.wait_ge(s["hot_ready"], 1)
            for t in range(NT):
                last = nc.tensor.transpose(bank1[2][0:TILES, t * P:(t + 1) * P],
                                           hot[:, t, :, :].rearrange("p c l -> p (c l)"), ident[:, :])
            last.then_inc(s["hot_tr"], 1)
            pe.wait_ge(s["hotT_ready"], 1)
            for t in range(NT):
                last = nc.tensor.matmul(bank1[0][:, t * S:t * S + TBL], hotT[:, t * P:(t + 1) * P], tbl[:, :],
                                        start=True, stop=True)
            last.then_inc(s["got_ready"], 1)
            yield kf(0.88)
            pe.wait_ge(s["xn_ready"], 1)
            transposed(bank1[2], xn).then_inc(s["xn_tr"], 1)
            pe.wait_ge(s["hT_ready"], 1)
            for j, w in enumerate((3, 4)):
                last = nc.tensor.matmul(bank1[0][:, j * S:(j + 1) * S], w1a[:, w, :], hT[:, :], start=True, stop=True)
            last.then_inc(s["loc_q"], 1)
            last = nc.tensor.matmul(bank1[1][:, 0:S], w1a[:, 0, :], hT[:, :], start=True, stop=True)
            for t in range(NT):
                for j, w in enumerate((1, 2)):
                    last = nc.tensor.matmul(bank1[3 if j else 1][:, S + t * P:S + (t + 1) * P],
                                            hT[:, t * P:(t + 1) * P], w1a[:, w, :], start=True, stop=True)
            last.then_inc(s["lin_proj"], 1)
            yield kf(0.94)
            pe.wait_ge(s["klin_ready"], 1)
            pe.wait_ge(s["qlin_ready"], 1)
            for t in range(NT):
                last = nc.tensor.matmul(bank1[2][:, 0:2 * D], klin[:, t, :], vlin1[:, t, :, :].rearrange("p a n -> p (a n)"),
                                        start=(t == 0), stop=(t == NT - 1))
            last.then_inc(s["kv_done"], 1)
            pe.wait_ge(s["kv_copied"], 1)
            for j in range(2):
                last = nc.tensor.matmul(bank1[3][:, j * S:(j + 1) * S], kv[:, j, :], qlinT, start=True, stop=True)
            last.then_inc(s["lin_done"], 1)
            pe.wait_ge(s["kloc_ready"], 1)
            for u in range(8 + 2):
                yield kw(u)
                p, g = divmod(u, 4)
                if u == 0:
                    pe.wait_ge(s["linT_ready"], 1)
                    window_values(0)
                if u < 8:
                    pe.wait_ge(s["qm_ready"], g + 1)
                    if u >= 2:
                        pe.wait_ge(s["w_max"], 2 * (u - 1) - 1)
                    for hd in range(4):
                        for j in range(2):
                            h, t = 4 * g + hd, 2 * p + j
                            last = nc.tensor.matmul(bank1[u % 2][QT * j:QT * (j + 1), hd * P:(hd + 1) * P],
                                                    GQ[:, h, t * QT:(t + 1) * QT], kloc[:, KEY0[t]:KEY0[t] + P],
                                                    start=True, stop=True)
                    last.then_inc(s["w_sc"], 1)
                if u == 6:
                    window_out(0)
                    window_values(1)
                if u >= 2:
                    v = u - 2
                    pe.wait_ge(s["w_norm"], v + 1)
                    if v >= 1:
                        pe.wait_ge(s["w_et"], v)
                    for hd in range(4):
                        last = nc.tensor.transpose(bank1[2][:, hd * P:(hd + 1) * P], Sw[:, v % 3, hd, :], ident[:, :])
                    last.then_inc(s["w_tr"], 1)
                if u == 9:
                    window_out(1)
            yield K["g"]
            pe.wait_ge(s["winT_ready"], 1)
            for j, r in enumerate((linT, winT, hT[:, :])):
                last = nc.tensor.matmul(bank1[0][:, 0:S], wg1[:, j, :], r, start=(j == 0), stop=(j == 2))
            last.then_inc(s["g1_done"], 1)
            pe.wait_ge(s["g1_ready"], 1)
            nc.tensor.matmul(bank1[1][:, 0:S], wg2[:, :], hidg[:, :], start=True, stop=True).then_inc(s["g2_done"], 1)
            yield K["g"] + 5.5
            pe.wait_ge(s["mixed"], 1)
            for t in range(NT):
                last = nc.tensor.matmul(bank1[0][:, t * P:(t + 1) * P], gt[:, t * P:(t + 1) * P], wo1[:, :],
                                        start=True, stop=True)
            last.then_inc(s["o1_done"], 1)

        def window_out(pp):
            pe = nc.tensor
            pe.wait_ge(s["w_et"], 4 * (pp + 1))
            pe.wait_ge(s["vm_ready"], pp + 1)
            for j in range(2):
                t = 2 * pp + j
                for h in range(WH):
                    last = nc.tensor.matmul(bank1[3][:, t * QT:(t + 1) * QT], VM[:, j, h * P:(h + 1) * P],
                                            ETw[:, h, j * QT:(j + 1) * QT], start=(h == 0), stop=(h == WH - 1))
            last.then_inc(s["w_av"], 1)

        def window_values(pp):
            for j in range(2):
                k = KEY0[2 * pp + j]
                last = nc.tensor.matmul(bank1[3][:, pp * S + j * P:pp * S + (j + 1) * P], hT[:, k:k + P],
                                        w1a[:, 5, :], start=True, stop=True)
            last.then_inc(s["vm_proj"], 1)

        def et_wait(eng, name, g):
            eng.wait_ge(s[name + ("_dve" if g % 2 else "_act")], g // 2 + 1)

        def transposed(bank, src):
            for t in range(NT):
                last = nc.tensor.transpose(bank[:, t * P:(t + 1) * P], src[:, t, :], ident[:, :])
            return last

        def out_proj(bank, OT, wo):
            for t in range(NT):
                for c in range(NC):
                    last = nc.tensor.matmul(bank[:, t * P:(t + 1) * P], OT[:, c, t * P:(t + 1) * P], wo[:, c, :],
                                            start=(c == 0), stop=(c == NC - 1))
            return last

        def first_act(act):
            for u in range(0, 12, 2):
                yield kp(u)
                act.wait_ge(s["proj0"], u + 1)
                if u < 8:
                    nc.scalar.activation(GQ[:, 2 * u:2 * u + 2, :], tri(proj_bank(u), 2), ACT.Copy,
                                         scale=DH ** -0.5).then_inc(s["proj0_act"], 1)
                else:
                    t, c = divmod(u - 8, 2)
                    nc.scalar.activation(V0[:, t, c * 512:(c + 1) * 512], proj_bank(u), ACT.Copy)\
                        .then_inc(s["proj0_act"], 1)
            for h in range(NH + 3):
                yield k0(h)
                if h < NH:
                    act.wait_ge(s["max0"], h + 1)
                    if h >= 3:
                        act.wait_ge(s["tr0"], h - 2)
                    for t in range(NT):
                        nc.scalar.activation(E0[:, h % 3, t, :], bank1[h % 2][:, t * S:(t + 1) * S], ACT.Exp,
                                             bias=nm0[:, h, t:t + 1],
                                             accum_out=rs0[:, h, t:t + 1]).then_inc(s["exp0"], 1)
                g = h - 2
                if 0 <= g < NH and g % 2 == 0:
                    act.wait_ge(s["tr0"], g + 1)
                    if g >= 2:
                        act.wait_ge(s["av0"], g - 1)
                    nc.scalar.activation(ET0[:, 0, :, :], tri(bank1[2], 2), ACT.Copy).then_inc(s["et0_act"], 1)
                g = h - 3
                if g >= 0 and g % 2:
                    act.wait_ge(s["av0"], g + 1)
                    nc.scalar.activation(OT0[:, g // 2, :], bank1[3][:, 0:S], ACT.Copy).then_inc(s["ot0_act"], 1)
            yield kf(0.13)
            act.wait_ge(s["x1tr"], 1)
            nc.scalar.activation(fT[:, :], bank1[2][:, 0:S], ACT.Copy).then_inc(s["x1T_ready"], 1)
            act.wait_ge(s["route_ready"], 1)
            yield kf(0.16)
            nc.scalar.activation(gel[0:COMP, :], bank1[1][0:COMP, 0:S], ACT.Gelu, bias=cols[0:COMP, COLS["cb1"][0]:COLS["cb1"][0] + 1])\
                .then_inc(s["gelu_ready"], 1)
            act.wait_ge(s["compress_ready"], 1)
            nc.scalar.activation(comp[:, :, :].rearrange("p t n -> p (t n)"), bank1[3][:, 0:4], ACT.Tanh)\
                .then_inc(s["comp_ready"], 1)
            yield kf(0.19)
            act.wait_ge(s["sc_copied"], 1)
            nc.scalar.activation(ec[:, :].rearrange("p (t n) -> p t n", t=NT), scores[:, :, 0:CL], ACT.Exp,
                                 scale=-1.0).then_inc(s["exp_c"], 1)
            yield kf(0.38)
            act.wait_ge(s["sel_ready"], 1)
            nc.scalar.activation(el[:, :], sel[:, :, :].rearrange("p t n -> p (t n)"), ACT.Exp,
                                 scale=-1.0).then_inc(s["exp_l"], 1)
            yield kf(0.88)
            act.wait_ge(s["xn_tr"], 1)
            nc.scalar.activation(hT[:, :], bank1[2][:, 0:S], ACT.Identity, bias=col("l1_b"), scale=col("l1_g"))\
                .then_inc(s["hT_ready"], 1)
            act.wait_ge(s["loc_q"], 1)
            nc.scalar.activation(qloc[:, :], bank1[0][:, 0:S], ACT.Identity, bias=col("bq_loc"))\
                .then_inc(s["qloc_ready"], 1)
            nc.scalar.activation(kloc[:, :], bank1[0][:, S:2 * S], ACT.Identity, bias=col("bk_loc"))\
                .then_inc(s["kloc_ready"], 1)
            yield kf(0.91)
            act.wait_ge(s["klin_raw"], 1)
            nc.scalar.activation(q_e, q_e, ACT.Exp).then_inc(s["q_exp"], 1)
            nc.scalar.activation(k_e[:, :, :], k_e[:, :, :], ACT.Exp).then_inc(s["k_exp"], 1)
            yield kf(0.94)
            act.wait_ge(s["kv_done"], 1)
            nc.scalar.activation(kv[:, :, :], tri(bank1[2][:, 0:2 * D], 2), ACT.Copy).then_inc(s["kv_copied"], 1)
            for u in range(8 + 2):
                yield kw(u)
                if 1 <= u < 9:
                    v = u - 1
                    act.wait_ge(s["w_sub"], v + 1)
                    nc.scalar.activation(Sw[:, v % 3, :, :], Sw[:, v % 3, :, :], ACT.Exp).then_inc(s["w_exp"], 1)
                if u >= 2:
                    v = u - 2
                    p, g = divmod(v, 4)
                    act.wait_ge(s["w_tr"], v + 1)
                    if v == 4:
                        act.wait_ge(s["w_av"], 1)
                    nc.scalar.activation(ETw[:, 4 * g:4 * g + 4, :], tri(bank1[2], 4), ACT.Copy)\
                        .then_inc(s["w_et"], 1)
            yield K["g"]
            act.wait_ge(s["g2_done"], 1)
            nc.scalar.activation(gt[:, :], bank1[1][:, 0:S], ACT.Exp, bias=neg_bg2[:, :], scale=-1.0)\
                .then_inc(s["g_exp"], 1)

        def layer_norm(link, dve, src, dst, half, k):
            st, mv, ve, rstd = (st1, mv1, ve1, rstd1) if half == 1 else (st2, mv2, ve2, rstd2)
            key = NORM[half][k]
            link.at(key, key + 0.4 * KN_W, 2)
            yield key
            for t in range(NT):
                ins = nc.vector.bn_stats(st[:, t, :], src[:, t, :])
            yield from link(ins)
            for t in range(NT):
                ins = nc.vector.bn_aggr(mv[:, t, :], st[:, t, :])
            yield from link(ins)
            nc.vector.tensor_scalar(ve[:, :], mv[:, :, 1], EPS, None, ALU.add).then_inc(s[f"ve{half}_ready"], 1)
            yield key + 0.6 * KN_W
            dve.wait_ge(s[f"rstd{half}_ready"], k + 1)
            for t in range(NT):
                ins = nc.vector.tensor_scalar(dst[:, t, :], src[:, t, :], mv[:, t, 0:1], rstd[:, t:t + 1],
                                              ALU.subtract, ALU.mult)
            return ins

        def rstd_step(pool, half, k):
            ve, rstd = (ve1, rstd1) if half == 1 else (ve2, rstd2)
            yield NORM[half][k] + 0.5 * KN_W
            pool.wait_ge(s[f"ve{half}_ready"], k + 1)
            nc.gpsimd.tensor_tensor(rstd[:, :], ve[:, :], half_neg[:, 0:NT], ALU.pow)\
                .then_inc(s[f"rstd{half}_ready"], 1)

        def calibrate(link, e):
            n = NT * 8
            yield from link(nc.vector.tensor_scalar(fx[:, :], e[:, :], 1.0, None, ALU.add))
            yield from link(nc.vector.reciprocal(fx[:, :], fx[:, :]))
            yield from link(nc.vector.tensor_scalar(fx[:, :], fx[:, :], float(KN - 1), None, ALU.mult))
            f = fx[:, :].unsqueeze(2).broadcast_to((P, n, KN - 1))
            nc.vector.tensor_tensor(m_a[:, :, :], f, row("jlo").unsqueeze(1).broadcast_to((P, n, KN - 1)), ALU.is_ge)
            yield from link(nc.vector.tensor_tensor(m_b[:, :, :], f, row("jhi").unsqueeze(1).broadcast_to((P, n, KN - 1)),
                                         ALU.is_lt))
            yield from link(nc.vector.tensor_tensor(m_a[:, :, :], m_a[:, :, :], m_b[:, :, :], ALU.mult))
            yield from link(nc.vector.tensor_tensor(pick[:, :, :, :], m_a[:, :, :].unsqueeze(2).broadcast_to((P, n, 3, KN - 1)),
                                         knot_tab[:, :, :].unsqueeze(1).broadcast_to((P, n, 3, KN - 1)), ALU.mult))
            yield from link(nc.vector.tensor_reduce(picked[:, :, :], pick[:, :, :, :], AX, ALU.add))
            g = gates[:, :, :].rearrange("p t n -> p (t n)")
            yield from link(nc.vector.tensor_tensor(g, fx[:, :], picked[:, :, 2], ALU.subtract))
            yield from link(nc.vector.tensor_tensor(g, g, picked[:, :, 1], ALU.mult))
            yield from link(nc.vector.tensor_tensor(g, g, picked[:, :, 0], ALU.add))

        def first_max(link, hot_):
            b = (P, NT, 8)
            yield from link(nc.vector.tensor_reduce(gmax[:, :], gates[:, :, :], AX, ALU.max))
            yield from link(nc.vector.tensor_tensor(gates[:, :, :], gates[:, :, :], gmax[:, :].unsqueeze(2).broadcast_to(b), ALU.is_ge))
            yield from link(nc.vector.tensor_tensor(gates[:, :, :], gates[:, :, :], row_t("first"), ALU.mult))
            yield from link(nc.vector.tensor_reduce(gmax[:, :], gates[:, :, :], AX, ALU.max))
            return nc.vector.tensor_tensor(hot_[:, :, :], gates[:, :, :], gmax[:, :].unsqueeze(2).broadcast_to(b), ALU.is_equal)

        def first_dve(dve, both):
            link = Chain(dve, "dve1")

            for u in range(1, 12, 2):
                yield kp(u)
                dve.wait_ge(s["proj0"], u + 1)
                if u < 8:
                    nc.vector.tensor_scalar(GQ[:, 2 * u:2 * u + 2, :], tri(proj_bank(u), 2), DH ** -0.5, None,
                                            ALU.mult).then_inc(s["proj0_dve"], 1)
                else:
                    t, c = divmod(u - 8, 2)
                    nc.vector.tensor_copy(V0[:, t, c * 512:(c + 1) * 512], proj_bank(u)).then_inc(s["proj0_dve"], 1)
            for h in range(NH + 3):
                yield k0(h)
                if h < NH:
                    dve.wait_ge(s["sc0"], h + 1)
                    nc.vector.tensor_reduce(nm0[:, h, :], tri(bank1[h % 2], 2), AX, ALU.max, negate=True)\
                        .then_inc(s["max0"], 1)
                if 1 <= h <= NH:
                    dve.wait_ge(s["exp0"], 2 * h)
                    nc.vector.reciprocal(ri0[:, h - 1, :], rs0[:, h - 1, :]).then_inc(s["ri0_ready"], 1)
                g = h - 2
                if 0 <= g < NH and g % 2:
                    dve.wait_ge(s["tr0"], g + 1)
                    if g >= 2:
                        dve.wait_ge(s["av0"], g - 1)
                    nc.vector.tensor_copy(ET0[:, 1, :, :], tri(bank1[2], 2)).then_inc(s["et0_dve"], 1)
            yield k0(NH + 3)
            dve.wait_ge(s["wo0_done"], 1)
            dve.wait_ge(s["xb_ready"], 1)
            yield from link(nc.vector.tensor_tensor(y1[:, :, :], tri(bank1[0][:, 0:S], 2), xb[:, :, :], ALU.add))
            (yield from layer_norm(link, dve, y1, x1, 1, 0)).then_inc(s["x1_ready"], 1)
            yield kf(0.16)
            dve.wait_ge(s["route_ready"], 1)
            nc.vector.tensor_scalar(scores[:, :, :], tri(bank1[0][:, 0:S], 2)[:, :, 0:CL + TILES], inv_t[:, :], -87.0,
                                    ALU.mult, ALU.max).then_inc(s["sc_copied"], 1)
            yield link.at(kf(0.19), kf(0.38), 16)
            dve.wait_ge(s["exp_c"], 1)
            yield from calibrate(link, ec)
            yield from link((yield from first_max(link, hot_c)))
            by = scores[:, :, CL:CL + TILES].rearrange("p t (c l) -> p t l c", c=CL)
            yield from link(nc.vector.tensor_tensor(selp[:, :, :, :], by, hot_c[:, :, :].unsqueeze(2).broadcast_to((P, NT, TPC, CL)),
                                         ALU.mult))
            nc.vector.tensor_reduce(sel[:, :, :], selp[:, :, :, :], AX, ALU.add).then_inc(s["sel_ready"], 1)
            yield link.at(kf(0.38), kf(0.55), 15)
            dve.wait_ge(s["exp_l"], 1)
            yield from calibrate(link, el)
            yield from link((yield from first_max(link, hot_l)))
            yield kf(0.55)
            for t in range(NT):
                ins = nc.vector.tensor_tensor(hot[:, t, :, :], hot_c[:, t, :].unsqueeze(2).broadcast_to((P, CL, TPC)),
                                              hot_l[:, t, :].unsqueeze(1).broadcast_to((P, CL, TPC)), ALU.mult)
            ins.then_inc(s["hot_ready"], 1)
            yield link.at(kf(0.58), kf(0.68), 8)
            dve.wait_ge(s["hot_tr"], 1)
            nc.vector.tensor_copy(hotT[:, :], bank1[2][0:TILES, 0:S]).then_inc(s["hotT_ready"], 1)
            dve.wait_ge(s["got_ready"], 1)
            yield from link(nc.vector.tensor_copy(got[:, :, :], tri(bank1[0], 2)[:, :, 0:TBL]))
            dve.wait_ge(s["comp_ready"], 1)
            G = GRID
            for t in range(NT):
                ins = nc.vector.scalar_tensor_tensor(out=hh[:, t, :], in0=got[:, t, 0:G], scalar=comp[:, t, 0:1],
                                                     in1=got[:, t, 2 * G:3 * G], op0=ALU.mult, op1=ALU.add)
            yield from link(ins)
            for t in range(NT):
                ins = nc.vector.scalar_tensor_tensor(out=hh[:, t, :], in0=got[:, t, G:2 * G], scalar=comp[:, t, 1:2],
                                                     in1=hh[:, t, :], op0=ALU.mult, op1=ALU.add)
            yield from link(ins)
            for t in range(NT):
                ins = nc.vector.scalar_tensor_tensor(out=hh[:, t, :], in0=hh[:, t, :], scalar=0.0,
                                                     in1=got[:, t, 3 * G:4 * G], op0=ALU.max, op1=ALU.mult)
            yield from link(ins)
            yield from link(nc.vector.tensor_reduce(mag[:, :], hh[:, :, :], AX, ALU.add))
            yield from link(nc.vector.tensor_tensor(mag[:, :], mag[:, :], got[:, :, 4 * G], ALU.add))
            yield from link(nc.vector.tensor_scalar(mag[:, :], mag[:, :], col("oscale"), None, ALU.mult))
            for t in range(NT):
                ins = nc.vector.scalar_tensor_tensor(out=y1[:, t, :], in0=got[:, t, 4 * G + 1:TBL],
                                                     scalar=mag[:, t:t + 1], in1=x1[:, t, :], op0=ALU.mult, op1=ALU.add)
            yield from link(ins)
            yield kf(0.68)
            yield from link((yield from layer_norm(link, dve, y1, xn, 1, 1)))
            yield from link(nc.vector.tensor_tensor(xn[:, :, :], xn[:, :, :], row_t("gamma"), ALU.mult))
            dve.wait_ge(s["x1b_ready"], 1)
            yield from link(nc.vector.tensor_tensor(y1[:, :, :], xn[:, :, :], x1b[:, :, :], ALU.add))
            yield kf(0.75)
            ins = (yield from layer_norm(link, dve, y1, x2, 1, 2))
            ins.then_inc(s["x2_ready"], 1)
            dve.wait_ge(s["x2_ready"], 1)
            yield kf(0.82)
            (yield from layer_norm(link, dve, x2, xn, 1, 3)).then_inc(s["xn_ready"], 1)
            yield link.at(kf(0.88), kf(0.90), 1)
            dve.wait_ge(s["lin_proj"], 1)
            b = (P, NT, D)
            nc.vector.tensor_tensor(vlin1[:, :, 0, :], tri(bank1[3][:, S:2 * S], 2), row_t("bv_lin"), ALU.add)
            yield from link(nc.vector.tensor_tensor(klin[:, :, :], tri(bank1[1][:, S:2 * S], 2), row_t("bk_lin"), ALU.add))
            nc.vector.tensor_scalar(q_e, bank1[1][:, 0:S], col("bq_lin"), 0.0, ALU.add, ALU.min)
            nc.vector.tensor_scalar(k_e[:, :, :], klin[:, :, :], 0.0, None, ALU.min).then_inc(s["klin_raw"], 1)
            yield link.at(kf(0.92), kf(0.94), 3)
            yield from link(nc.vector.tensor_scalar(qlinT, bank1[1][:, 0:S], col("bq_lin"), 0.0, ALU.add, ALU.max))
            yield from link(nc.vector.tensor_scalar(klin[:, :, :], klin[:, :, :], 0.0, None, ALU.max))
            dve.wait_ge(s["q_exp"], 1)
            nc.vector.tensor_tensor(qlinT, q_e, qlinT, ALU.add).then_inc(s["qlin_ready"], 1)
            dve.wait_ge(s["k_exp"], 1)
            nc.vector.tensor_tensor(klin[:, :, :], k_e[:, :, :], klin[:, :, :], ALU.add).then_inc(s["klin_ready"], 1)
            yield link.at(kf(0.94), kw(0), 3)
            dve.wait_ge(s["lin_done"], 1)
            yield from link(nc.vector.tensor_scalar(den[:, :], bank1[3][:, S:2 * S], 1e-6, None, ALU.add))
            yield from link(nc.vector.reciprocal(den[:, :], den[:, :]))
            nc.vector.tensor_tensor(linT, bank1[3][:, 0:S], den[:, :], ALU.mult).then_inc(s["linT_ready"], 1)

            def vm_copy(pp):
                dve.wait_ge(s["vm_proj"], pp + 1)
                for j in range(2):
                    src = bank1[3][:, pp * S + j * P:pp * S + (j + 1) * P]
                    dst = VM[:, j, :].rearrange("p (h n) -> p h n", h=WH)[:, :, 0:WD]
                    ins = nc.vector.tensor_copy(dst, src.rearrange("p (h n) -> p h n", h=WH))
                ins.then_inc(s["vm_ready"], 1)

            for u in range(8 + 2):
                yield kw(u)
                p, g = divmod(u, 4)
                if u == 0:
                    vm_copy(0)
                if u < 8:
                    dve.wait_ge(s["w_sc"], u + 1)
                    if u >= 3:
                        dve.wait_ge(s["w_tr"], u - 2)
                    nc.vector.tensor_tensor(Sw[:, u % 3, :, :], tri(bank1[u % 2], 4), bias_t[:, p, 4 * g:4 * g + 4, :],
                                            ALU.add).then_inc(s["w_max"], 1)
                    dve.wait_ge(s["w_max"], 2 * u + 1)
                    nc.vector.tensor_reduce(nmw[:, u % 3, :], Sw[:, u % 3, :, :], AX, ALU.max)\
                        .then_inc(s["w_max"], 1)
                if 1 <= u < 9:
                    v = u - 1
                    dve.wait_ge(s["w_exp"], v + 1)
                    yield from link(nc.vector.tensor_reduce(rsw[:, v % 3, :], Sw[:, v % 3, :, :], AX, ALU.add))
                    nc.vector.reciprocal(rsw[:, v % 3, :], rsw[:, v % 3, :]).then_inc(s["w_sum"], 1)
                if u == 6:
                    vm_copy(1)
            yield kw(9) + 0.1
            dve.wait_ge(s["w_av"], 2)
            nc.vector.tensor_scalar(winT, bank1[3][:, 0:S], col("bv_loc"), None, ALU.add)\
                .then_inc(s["winT_ready"], 1)
            yield link.at(K["g"], K["g"] + 5, 5)
            dve.wait_ge(s["g1_done"], 1)
            nc.vector.tensor_scalar(hidg[:, :], bank1[0][:, 0:S], col("bg1"), 0.0, ALU.add, ALU.max)\
                .then_inc(s["g1_ready"], 1)
            dve.wait_ge(s["winT_ready"], 1)
            dve.wait_ge(s["g1_done"], 1)
            yield from link(nc.vector.tensor_tensor(linT, linT, winT, ALU.subtract))
            dve.wait_ge(s["g_exp"], 1)
            yield from link(nc.vector.tensor_scalar(gt[:, :], gt[:, :], 1.0, None, ALU.add))
            yield from link(nc.vector.reciprocal(gt[:, :], gt[:, :]))
            yield from link(nc.vector.tensor_tensor(gt[:, :], gt[:, :], linT, ALU.mult))
            nc.vector.tensor_tensor(gt[:, :], gt[:, :], winT, ALU.add).then_inc(s["mixed"], 1)
            yield K["g"] + 6
            dve.wait_ge(s["o1_done"], 1)
            dve.wait_ge(s["x2b_ready"], 2)
            yield from link(nc.vector.tensor_tensor(y1[:, :, :], tri(bank1[0][:, 0:S], 2), x2b[:, :, :], ALU.add))
            if both:
                dve.wait_ge(s["x3_taken"], 1)
            (yield from layer_norm(link, dve, y1, x3, 1, 4)).then_inc(s["x3_ready"], 1)

        def first_pool(pool):
            yield 0
            nc.gpsimd.tensor_tensor(xb[:, :, :], xr[:, :, :], row_t("bo0"), ALU.add).then_inc(s["xb_ready"], 1)
            for h in range(1, NH + 1):
                yield k0(h)
                g = h - 1
                pool.wait_ge(s["ri0_ready"], g + 1)
                nc.gpsimd.tensor_tensor(E0[:, g % 3, :, :], E0[:, g % 3, :, :],
                                        ri0[:, g, :].unsqueeze(2).broadcast_to((P, NT, S)), ALU.mult)\
                    .then_inc(s["norm0"], 1)
            yield k0(NH + 3)
            yield from rstd_step(pool, 1, 0)
            yield kf(0.16)
            pool.wait_ge(s["x1_ready"], 1)
            nc.gpsimd.tensor_tensor(x1b[:, :, :], x1[:, :, :], row_t("beta"), ALU.add).then_inc(s["x1b_ready"], 1)
            yield kf(0.68)
            yield from rstd_step(pool, 1, 1)
            yield kf(0.75)
            yield from rstd_step(pool, 1, 2)
            yield kf(0.82)
            yield from rstd_step(pool, 1, 3)
            yield kf(0.88)
            pool.wait_ge(s["x2_ready"], 1)
            nc.gpsimd.tensor_tensor(x2b[:, :, :], x2[:, :, :], x2[:, :, :], ALU.add).then_inc(s["x2b_ready"], 1)
            pool.wait_ge(s["x2b_ready"], 1)
            nc.gpsimd.tensor_tensor(x2b[:, :, :], x2b[:, :, :], row_t("bo1"), ALU.add).then_inc(s["x2b_ready"], 1)
            pool.wait_ge(s["qloc_ready"], 1)
            for g in range(4):
                nc.gpsimd.tensor_tensor(GQ[:, 4 * g:4 * g + 4, :], qloc[:, :].unsqueeze(1).broadcast_to((P, 4, S)),
                                        col("headmask", 4 * g, 4).unsqueeze(2).broadcast_to((P, 4, S)), ALU.mult)\
                    .then_inc(s["qm_ready"], 1)
            for u in range(8 + 1):
                yield kw(u) + 0.05
                if u < 8:
                    pool.wait_ge(s["w_max"], 2 * u + 2)
                    nc.gpsimd.tensor_tensor(Sw[:, u % 3, :, :], Sw[:, u % 3, :, :],
                                            nmw[:, u % 3, :].unsqueeze(2).broadcast_to((P, 4, P)), ALU.subtract)\
                        .then_inc(s["w_sub"], 1)
                if u >= 1:
                    v = u - 1
                    pool.wait_ge(s["w_sum"], v + 1)
                    nc.gpsimd.tensor_tensor(Sw[:, v % 3, :, :], Sw[:, v % 3, :, :],
                                            rsw[:, v % 3, :].unsqueeze(2).broadcast_to((P, 4, P)), ALU.mult)\
                        .then_inc(s["w_norm"], 1)
            yield K["g"] + 6
            yield from rstd_step(pool, 1, 4)

        QKU = [(half, kind, t) for half in range(2) for kind in range(2) for t in range(NT)]

        BLOCKS = [(0, 0), (1, 0), (1, 1)]

        def second_pe(pe):
            yield KN_W
            pe.wait_ge(s["xn2_ready"], 1)
            transposed(bank2[2], xn2).then_inc(s["tr2"], 1)
            pe.wait_ge(s["hT2_ready"], 1)
            for u in range(4):
                yield kv2(u)
                if u >= 2:
                    pe.wait_ge(s["v2_copied"], u - 1)
                t, c = divmod(u, 2)
                nc.tensor.matmul(bank2[u % 2], h2T[:, t * P:(t + 1) * P], wqkv[:, 2, c * 512:(c + 1) * 512],
                                 start=True, stop=True).then_inc(s["v2_proj"], 1)
            for u in range(len(QKU) + 1):
                yield kq(u)
                if u < len(QKU):
                    half, kind, t = QKU[u]
                    if u == 0:
                        pe.wait_ge(s["v2_copied"], 4)
                    if u >= 2:
                        pe.wait_ge(s["qn_ready"], u - 1)
                    nc.tensor.matmul(bank2[u % 2], h2T[:, t * P:(t + 1) * P],
                                     wqkv[:, kind, half * 512:(half + 1) * 512], start=True, stop=True)\
                        .then_inc(s["qk_proj"], 1)
                if u >= 1:
                    v = u - 1
                    pe.wait_ge(s["qn_ready"], v + 1)
                    if v >= 1:
                        qk_wait(pe, v - 1)
                    for c in range(4):
                        last = nc.tensor.transpose(bank2[2][:, c * P:(c + 1) * P],
                                                   qn[:, v % 2, 2 * c:2 * c + 2, :].rearrange("p a n -> p (a n)"),
                                                   ident[:, :])
                    last.then_inc(s["qk_tr"], 1)
            for h in range(NH + 3):
                yield k2(h)
                if h < NH:
                    if h == 0:
                        pe.wait_ge(s["q_copied"], 4)
                        pe.wait_ge(s["k_copied"], 4)
                    if h >= 2:
                        pe.wait_ge(s["exp2"], 2 * (h - 1))
                    c, r = h // 2, 64 * (h % 2)
                    for j, (t, k) in enumerate(BLOCKS):
                        o = bank2[h % 2][:, j * P:(j + 1) * P]
                        last = nc.tensor.matmul(o, QK[r:r + DH, 0, c, t * P:(t + 1) * P],
                                                QK[r:r + DH, 1, c, k * P:(k + 1) * P], start=True, stop=(t != k))
                        if t == k:
                            last = nc.tensor.matmul(o, ident_bf[:, :], causal[:, :], start=False, stop=True)
                    last.then_inc(s["sc2"], 1)
                g = h - 2
                if 0 <= g < NH:
                    pe.wait_ge(s["norm2"], g + 1)
                    if g >= 1:
                        et_wait(pe, "et2", g - 1)
                    for j in range(len(BLOCKS)):
                        last = nc.tensor.transpose(bank2[2][:, j * P:(j + 1) * P], E2[:, g % 3, j * P:(j + 1) * P],
                                                   ident[:, :])
                    last.then_inc(s["tr2e"], 1)
                g = h - 3
                if g >= 0:
                    et_wait(pe, "et2", g)
                    if g >= 2 and g % 2 == 0:
                        pe.wait_ge(s["ot2_done"], g // 2)
                    r = 64 * (g % 2)
                    for j, (t, k) in enumerate(BLOCKS):
                        last = nc.tensor.matmul(bank2[3][r:r + DH, t * P:(t + 1) * P], V2[:, k, g * DH:(g + 1) * DH],
                                                ET2[:, g % 2, j * P:(j + 1) * P], start=(k == 0), stop=(k == t))
                    last.then_inc(s["av2"], 1)
            yield K["o"]
            pe.wait_ge(s["ot2_done"], NC)
            out_proj(bank2[0], OT2, wo2).then_inc(s["wo2_done"], 1)
            yield K["o"] + KN_W
            pe.wait_ge(s["o2_ready"], 1)
            transposed(bank2[2], xn2).then_inc(s["o2_tr"], 1)
            pe.wait_ge(s["o2T_ready"], 1)
            for t in range(NT):
                last = nc.tensor.matmul(bank2[3][:, t * NE:(t + 1) * NE], h2T[:, t * P:(t + 1) * P], gate_w[:, :],
                                        start=True, stop=True)
            last.then_inc(s["gate_done"], 1)
            for u in range(2 * (NE + 1)):
                e, j = divmod(u, 2)
                yield kx(e)
                if e < NE:
                    if u >= 2:
                        pe.wait_ge(s["hid_ready"], 2 * (u - 1))
                    for f in range(2):
                        last = nc.tensor.matmul(bank2[u % 2][:, f * S:(f + 1) * S],
                                                w1[:, e, (2 * j + f) * P:(2 * j + f + 1) * P], h2T[:, :],
                                                start=True, stop=True)
                    last.then_inc(s["hid_done"], 1)
                if u == 1:
                    pe.wait_ge(s["gate_ready"], 1)
                    for t in range(NT):
                        last = nc.tensor.transpose(bank2[2][0:NE, t * P:(t + 1) * P], gl[:, t, :], ident[:, :])
                    last.then_inc(s["gate_tr"], 1)
                    pe.wait_ge(s["gateT_ready"], 1)
                    for t in range(NT):
                        last = nc.tensor.matmul(bank2[3][:, t * P:(t + 1) * P], gateT[:, t * P:(t + 1) * P], b2[:, :],
                                                start=True, stop=True)
                    last.then_inc(s["out_done"], 1)
                if e >= 1 and j == 1:
                    x = e - 1
                    pe.wait_ge(s["hid_ready"], 4 * (x + 1))
                    if x >= 1:
                        pe.wait_ge(s["out_used"], x)
                    for t in range(NT):
                        for f in range(FC):
                            last = nc.tensor.matmul(bank2[2 + x % 2][:, t * P:(t + 1) * P],
                                                    hid[:, x % 2, f, t * P:(t + 1) * P], w2[:, x, f, :],
                                                    start=(f == 0), stop=(f == FC - 1))
                    last.then_inc(s["out_done"], 1)

        def qk_wait(eng, v):
            kind = QKU[v][1]
            n = sum(1 for x in QKU[:v + 1] if x[1] == kind)
            eng.wait_ge(s["k_copied" if kind else "q_copied"], n)

        def second_act(act):
            yield KN_W
            act.wait_ge(s["tr2"], 1)
            nc.scalar.activation(h2T[:, :], bank2[2][:, 0:S], ACT.Identity, bias=col("f_b"), scale=col("f_g"))\
                .then_inc(s["hT2_ready"], 1)
            for u in range(4):
                yield kv2(u)
                t, c = divmod(u, 2)
                act.wait_ge(s["v2_proj"], u + 1)
                nc.scalar.activation(V2[:, t, c * 512:(c + 1) * 512], bank2[u % 2], ACT.Copy)\
                    .then_inc(s["v2_copied"], 1)
            for u in range(len(QKU) + 1):
                yield kq(u)
                if u < len(QKU):
                    act.wait_ge(s["qk_proj"], u + 1)
                    if u >= 2:
                        act.wait_ge(s["ss_ready"], u - 1)
                    nc.scalar.activation(sq[:, u % 2, :, :], tri(bank2[u % 2], 8), ACT.Square).then_inc(s["sq_ready"], 1)
                if u >= 1 and QKU[u - 1][1] == 0:
                    half, _, t = QKU[u - 1]
                    act.wait_ge(s["qk_tr"], u)
                    nc.scalar.activation(QK[:, 0, 4 * half:4 * half + 4, t * P:(t + 1) * P], tri(bank2[2], 4),
                                         ACT.Copy).then_inc(s["q_copied"], 1)
            for h in range(NH + 3):
                yield k2(h)
                if h < NH:
                    act.wait_ge(s["max2"], h + 1)
                    if h >= 3:
                        act.wait_ge(s["tr2e"], h - 2)
                    for t in range(NT):
                        o = slice(t * P, t * P + (t + 1) * P)
                        nc.scalar.activation(E2[:, h % 3, o], bank2[h % 2][:, o], ACT.Exp, bias=nm2[:, h, t:t + 1],
                                             accum_out=rs2[:, h, t:t + 1]).then_inc(s["exp2"], 1)
                g = h - 2
                if 0 <= g < NH and g % 2 == 0:
                    act.wait_ge(s["tr2e"], g + 1)
                    if g >= 2:
                        act.wait_ge(s["av2"], g - 1)
                    nc.scalar.activation(ET2[:, 0, :], bank2[2][:, 0:384], ACT.Copy).then_inc(s["et2_act"], 1)
                g = h - 3
                if g >= 0 and g % 2:
                    act.wait_ge(s["av2"], g + 1)
                    nc.scalar.activation(OT2[:, g // 2, :], bank2[3][:, 0:S], ACT.Copy).then_inc(s["ot2_done"], 1)
            yield K["o"] + KN_W
            act.wait_ge(s["o2_tr"], 1)
            nc.scalar.activation(h2T[:, :], bank2[2][:, 0:S], ACT.Identity, bias=col("f_b"), scale=col("f_g"))\
                .then_inc(s["o2T_ready"], 1)
            yield K["o"] + KN_W + 1.2
            act.wait_ge(s["gl_ready"], 1)
            nc.scalar.activation(gl[:, :, :], gl[:, :, :], ACT.Exp).then_inc(s["gexp_done"], 1)
            for u in range(2 * NE):
                e, j = divmod(u, 2)
                yield kx(e)
                act.wait_ge(s["hid_done"], u + 1)
                if e >= 2:
                    act.wait_ge(s["out_done"], e)
                for f in range(2):
                    fc = 2 * j + f
                    nc.scalar.activation(hid[:, e % 2, fc, :], bank2[u % 2][:, f * S:(f + 1) * S], ACT.Gelu_apprx_tanh,
                                         bias=col("b1", e * FC + fc)).then_inc(s["hid_ready"], 1)

        def second_dve(dve):
            link = Chain(dve, "dve2")

            yield 0
            nc.vector.tensor_copy(xh[:, :, :], x3[:, :, :]).then_inc(s["x3_taken"], 1)
            dve.wait_ge(s["x3_taken"], 1)
            (yield from layer_norm(link, dve, xh, xn2, 2, 0)).then_inc(s["xn2_ready"], 1)
            for u in range(len(QKU) + 1):
                yield kq(u)
                if u < len(QKU):
                    dve.wait_ge(s["sq_ready"], u + 1)
                    yield from link(nc.vector.tensor_reduce(ss[:, u, :], sq[:, u % 2, :, :], AX, ALU.add))
                    nc.vector.tensor_scalar(ss[:, u, :], ss[:, u, :], 1e-12, None, ALU.add).then_inc(s["ss_ready"], 1)
                if u >= 1 and QKU[u - 1][1] == 1:
                    half, _, t = QKU[u - 1]
                    dve.wait_ge(s["qk_tr"], u)
                    nc.vector.tensor_tensor(QK[:, 1, 4 * half:4 * half + 4, t * P:(t + 1) * P], tri(bank2[2], 4),
                                            kqs[:, 4 * half:4 * half + 4].unsqueeze(2).broadcast_to((P, 4, P)),
                                            ALU.mult).then_inc(s["k_copied"], 1)
                if u < len(QKU):
                    dve.wait_ge(s["rn_ready"], u + 1)
                    if u >= 2:
                        dve.wait_ge(s["qk_tr"], u - 1)
                    nc.vector.tensor_tensor(qn[:, u % 2, :, :], tri(bank2[u % 2], 8),
                                            rn[:, u, :].unsqueeze(2).broadcast_to((P, 8, DH)), ALU.mult)\
                        .then_inc(s["qn_ready"], 1)
            for h in range(NH + 3):
                yield k2(h)
                if h < NH:
                    dve.wait_ge(s["sc2"], h + 1)
                    for t in range(NT):
                        ins = nc.vector.tensor_reduce(nm2[:, h, t:t + 1], bank2[h % 2][:, t * P:t * P + (t + 1) * P],
                                                      AX, ALU.max, negate=True)
                    ins.then_inc(s["max2"], 1)
                if 1 <= h <= NH:
                    dve.wait_ge(s["exp2"], 2 * h)
                    nc.vector.reciprocal(ri2[:, h - 1, :], rs2[:, h - 1, :]).then_inc(s["ri2_ready"], 1)
                g = h - 2
                if 0 <= g < NH and g % 2:
                    dve.wait_ge(s["tr2e"], g + 1)
                    if g >= 2:
                        dve.wait_ge(s["av2"], g - 1)
                    nc.vector.tensor_copy(ET2[:, 1, :], bank2[2][:, 0:384]).then_inc(s["et2_dve"], 1)
            yield K["o"]
            dve.wait_ge(s["wo2_done"], 1)
            yield from link(nc.vector.tensor_copy(acc[:, :, :], tri(bank2[0][:, 0:S], 2)))
            (yield from layer_norm(link, dve, acc, xn2, 2, 1)).then_inc(s["o2_ready"], 1)
            yield link.at(K["o"] + KN_W, K["o"] + KN_W + 1, 2)
            b = (P, NT, NE)
            dve.wait_ge(s["gate_done"], 1)
            yield from link(nc.vector.tensor_tensor(gl[:, :, :], tri(bank2[3][:, 0:NT * NE], NT), row_t("gate_b"), ALU.add))
            yield from link(nc.vector.tensor_reduce(gm[:, :], gl[:, :, :], AX, ALU.max))
            nc.vector.tensor_tensor(gl[:, :, :], gl[:, :, :], gm[:, :].unsqueeze(2).broadcast_to(b), ALU.subtract)\
                .then_inc(s["gl_ready"], 1)
            yield link.at(K["o"] + KN_W + 1.4, K["o"] + KN_W + 2, 2)
            dve.wait_ge(s["gexp_done"], 1)
            yield from link(nc.vector.tensor_reduce(gs[:, :], gl[:, :, :], AX, ALU.add))
            yield from link(nc.vector.reciprocal(gs[:, :], gs[:, :]))
            nc.vector.tensor_tensor(gl[:, :, :], gl[:, :, :], gs[:, :].unsqueeze(2).broadcast_to(b), ALU.mult)\
                .then_inc(s["gate_ready"], 1)
            yield kx(0)
            dve.wait_ge(s["gate_tr"], 1)
            nc.vector.tensor_copy(gateT[:, :], bank2[2][0:NE, 0:S]).then_inc(s["gateT_ready"], 1)
            dve.wait_ge(s["out_done"], 1)
            nc.vector.tensor_copy(acc[:, :, :], tri(bank2[3][:, 0:S], 2)).then_inc(s["out_used"], 1)
            dve.wait_ge(s["out_used"], 1)
            for x in range(NE):
                yield kx(x + 1)
                dve.wait_ge(s["out_done"], x + 2)
                for t in range(NT):
                    ins = nc.vector.scalar_tensor_tensor(out=acc[:, t, :], in0=bank2[2 + x % 2][:, t * P:(t + 1) * P],
                                                         scalar=gl[:, t, x:x + 1], in1=acc[:, t, :],
                                                         op0=ALU.mult, op1=ALU.add)
                ins.then_inc(s["out_used"], 1)
                dve.wait_ge(s["out_used"], x + 2)
            yield K["z"]
            yield from link((yield from layer_norm(link, dve, acc, xn2, 2, 2)))
            yield from link(nc.vector.tensor_tensor(xn2[:, :, :], xn2[:, :, :], row_t("f_g"), ALU.mult))
            yield from link(nc.vector.tensor_tensor(xn2[:, :, :], xn2[:, :, :], row_t("f_b"), ALU.add))
            yield from link(nc.vector.tensor_tensor(acc[:, :, :], xn2[:, :, :], xh[:, :, :], ALU.add))
            (yield from layer_norm(link, dve, acc, yo, 2, 3)).then_inc(s["y_ready"], 1)

        def second_pool(pool):
            yield 0
            yield from rstd_step(pool, 2, 0)
            for u in range(len(QKU)):
                yield kq(u)
                pool.wait_ge(s["ss_ready"], u + 1)
                nc.gpsimd.tensor_tensor(rn[:, u, :], ss[:, u, :], half_neg[:, 0:8], ALU.pow).then_inc(s["rn_ready"], 1)
            for h in range(1, NH + 1):
                yield k2(h)
                g = h - 1
                pool.wait_ge(s["ri2_ready"], g + 1)
                for t in range(NT):
                    o = slice(t * P, t * P + (t + 1) * P)
                    ins = nc.gpsimd.tensor_tensor(E2[:, g % 3, o], E2[:, g % 3, o],
                                                  ri2[:, g, t:t + 1].broadcast_to((P, (t + 1) * P)), ALU.mult)
                ins.then_inc(s["norm2"], 1)
            yield K["o"]
            yield from rstd_step(pool, 2, 1)
            yield K["z"]
            yield from rstd_step(pool, 2, 2)
            yield from rstd_step(pool, 2, 3)

        def second_sync(sp, batch):
            yield 1000
            sp.wait_ge(s["y_ready"], 1)
            sp.dma_start(d["y"][bass.ds(batch, 1), :, :, :].rearrange("a p t n -> (a p) t n"), yo[:, :, :])\
                .then_inc(s["y_stored"], 16)
            sp.wait_ge(s["y_stored"], 16)

        def body(first, second, i=0):
            def programs(eng, of_first, of_second):
                merged(*([of_first(eng)] if first else []), *([of_second(eng)] if second else []))

            with nc.Block(no_gpsimd_drain=True) as block:
                @block.vector
                def _(dve):
                    programs(dve, lambda e: first_dve(e, second), second_dve)

                @block.tensor
                def _(pe):
                    programs(pe, first_pe, second_pe)

                @block.scalar
                def _(act):
                    programs(act, first_act, second_act)

                @block.gpsimd
                def _(pool):
                    programs(pool, first_pool, second_pool)

                @block.sync
                def _(sp):
                    programs(sp, lambda e: first_sync(e, i + 2 if second else 1), lambda e: second_sync(e, i))
            nc.sync.sem_clear(loop_sems)
            nc.all_engine_barrier(sem_only=True)

        body(True, False)
        nc.sync.wait_ge(w_second, 16 * len(second_loads))
        nc.all_engine_barrier(sem_only=True)
        with nc.Fori(0, NB - 1) as i:
            body(True, True, i)
        body(False, True, NB - 1)


def kernel(**inputs):
    import numpy as np
    import concourse.bacc as bacc
    from concourse.bass_utils import run_bass_kernel_spmd

    x = {k: np.asarray(v) for k, v in inputs.items()}
    f = np.float32
    X = x["L0_attn_hidden_states"]
    nb = X.shape[0]
    pad = np.zeros((1, P, S), f)

    def chunks(w):
        return w.reshape(-1, P, w.shape[-1]).transpose(1, 0, 2)

    def heads_T(w):
        return w.reshape(D, NH, DH).transpose(2, 1, 0)

    col_of = {"l1_g": x["L1_attn_ln_g"], "l1_b": x["L1_attn_ln_b"], "bq_lin": x["L1_attn_bq_lin"],
              "bq_loc": x["L1_attn_bq_loc"], "bk_loc": x["L1_attn_bk_loc"], "bv_loc": x["L1_attn_bv_loc"],
              "bg1": x["L1_attn_bg1"], "bg2": x["L1_attn_bg2"], "f_g": x["L1_ffn_ln_g"], "f_b": x["L1_ffn_ln_b"],
              "oscale": np.broadcast_to(x["L0_ffn_output_scale"], (P,)),
              "temp": np.broadcast_to(x["L0_ffn_temperature"], (P,)),
              "qs": x["L1_ffn_q_scale"].reshape(NC, P).T, "ks": x["L1_ffn_k_scale"].reshape(NC, P).T,
              "b1": x["L1_ffn_b1"].reshape(NE * FC, P).T,
              "headmask": np.where(np.arange(P)[:, None] // WD == np.arange(WH), f(WD ** -0.5), f(0))}
    cols = np.zeros((P, N_COLS), f)
    for name, v in col_of.items():
        at, n = COLS[name]
        cols[:, at:at + n] = v.reshape(P, n)
    cols[0:COMP, COLS["cb1"][0]] = x["L0_ffn_compress_b1"]
    row_of = {"bo0": x["L0_attn_bo"], "gamma": x["L0_ffn_norm_gamma"], "beta": x["L0_ffn_norm_beta"],
              "bk_lin": x["L1_attn_bk_lin"], "bv_lin": x["L1_attn_bv_lin"], "bo1": x["L1_attn_bo"],
              "f_g": x["L1_ffn_ln_g"], "f_b": x["L1_ffn_ln_b"], "gate_b": x["L1_ffn_gate_b"],
              "knots": x["L0_ffn_knot_values"], "jlo": np.arange(KN - 1, dtype=f),
              "jhi": np.array([*range(1, KN - 1), 1e30], f), "first": np.arange(8, 0, -1, dtype=f)}
    rows = np.zeros((P, N_ROWS), f)
    for name, v in row_of.items():
        at, n = ROWS[name]
        rows[:, at:at + n] = v
    query = np.arange(P)[:, None] + P * np.arange(2)
    key = np.array(KEY0)[query // QT][:, :, None] + np.arange(P)
    off = key - query[:, :, None]
    seen = np.abs(off) <= HALF
    rel = x["L1_attn_rel_bias"]
    bias_t = np.where(seen[..., None], rel[np.where(seen, off, 0) + 2 * HALF], f(NEG)).transpose(0, 1, 3, 2)

    wkv = x["L0_attn_Wkv"]
    names = ["wq_lin", "wk_lin", "wv_lin", "wq_loc", "wk_loc", "wv_loc"]
    arrays = {
        "xT": np.concatenate([X.transpose(0, 2, 1), pad]),
        "xr": np.concatenate([X.reshape(nb, NT, P, D).transpose(0, 2, 1, 3), pad.reshape(1, P, NT, D)]),
        "wqT": heads_T(x["L0_attn_Wq"]), "wkT": heads_T(wkv[:, :NH * DH]), "wv0": wkv[:, NH * DH:],
        "wo0": chunks(x["L0_attn_Wo"]), "sigT": x["L0_ffn_signatures_raw"].T, "cw1": x["L0_ffn_compress_w1"],
        "cw2": np.concatenate([x["L0_ffn_compress_w2"], x["L0_ffn_compress_b2"][None]]),
        "tbl": np.concatenate([x["L0_ffn_spline_w1"].reshape(TILES, -1), x["L0_ffn_spline_b1"],
                               x["L0_ffn_spline_w2"].reshape(TILES, -1), x["L0_ffn_spline_b2"],
                               x["L0_ffn_directions"]], axis=1),
        "w1a": np.stack([x["L1_attn_" + n] for n in names], axis=1),
        "wg1": chunks(x["L1_attn_wg1"]), "wg2": x["L1_attn_wg2"], "wo1": x["L1_attn_wo"], "bias_t": bias_t,
        "wqkv": np.stack([x["L1_ffn_Wq"], x["L1_ffn_Wk"], x["L1_ffn_Wv"]], axis=1),
        "wo2": chunks(x["L1_ffn_Wo"]), "gate_w": x["L1_ffn_gate_w"],
        "w1": x["L1_ffn_w1"].transpose(1, 0, 2),
        "w2": x["L1_ffn_w2"].reshape(NE, FC, P, D).transpose(2, 0, 1, 3), "b2": x["L1_ffn_b2"],
        "cols": cols, "rows": rows, "ident": np.eye(P, dtype=f),
    }
    arrays = {k: np.ascontiguousarray(v, dtype=f) for k, v in arrays.items()}
    nc = bacc.Bacc("TRN2", target_bir_lowering=False, num_devices=1)
    d = {k: nc.dram_tensor("in_" + k, v.shape, F32, kind="ExternalInput").ap() for k, v in arrays.items()}
    d["y"] = nc.dram_tensor("out_y", (NB, P, NT, D), F32, kind="ExternalOutput").ap()
    whole_net(nc, d)
    r = run_bass_kernel_spmd(nc, [{"in_" + k: v for k, v in arrays.items()}], core_ids=[0])
    return r.results[0]["out_y"].transpose(0, 2, 1, 3).reshape(NB, S, D)
```

```python
import concourse.bass as bass
from concourse import mybir
from contextlib import ExitStack

F32 = mybir.dt.float32
BF16 = mybir.dt.bfloat16
ALU = mybir.AluOpType
ACT = mybir.ActivationFunctionType
AX = mybir.AxisListType.X

NB, S, D = 16, 256, 128
P = 128
NT = S // P
NP = 2
TT = NP * NT
TOK = NP * S
NH, DH = 16, 64
NC = NH * DH // P
CL, TPC, KN = 8, 8, 8
TILES = CL * TPC
GRID, COMP = 16, 32
WH, WD = 16, 8
QT = 64
HALF = 32
KEY0 = [0, 32, 96, 128]
NE, FF = 8, 512
FC = FF // P
EPS = 1e-5
NEG = -1e30
CAUSAL_FILL = -1e9
TBL = 2 * GRID + GRID + GRID + 1 + D

COLS = {}
ROWS = {}


def _place(table, names):
    at = 0
    for name, n in names:
        table[name] = (at, n)
        at += n
    return at


N_COLS = _place(COLS, [("l1_g", 1), ("l1_b", 1), ("bq_lin", 1), ("bq_loc", 1), ("bk_loc", 1), ("bv_loc", 1),
                       ("bg1", 1), ("bg2", 1), ("f_g", 1), ("f_b", 1), ("cb1", 1), ("oscale", 1), ("temp", 1),
                       ("qs", NC), ("ks", NC), ("b1", NE * FC), ("headmask", WH)])
N_ROWS = _place(ROWS, [("bo0", D), ("gamma", D), ("beta", D), ("bk_lin", D), ("bv_lin", D), ("bo1", D),
                       ("f_g", D), ("f_b", D), ("gate_b", NE), ("knots", KN), ("jlo", KN - 1), ("jhi", KN - 1),
                       ("first", 8)])


def merged(*programs):
    live = [[next(g, None), g] for g in programs]
    while live := [x for x in live if x[0] is not None]:
        first = min(live, key=lambda x: x[0])
        first[0] = next(first[1], None)


def whole_net(nc, d):
    ctx = ExitStack()
    with ctx:
        def sb(name, shape, dt=F32):
            return ctx.enter_context(nc.sbuf_tensor(name, shape, dt))

        def sem(name):
            return ctx.enter_context(nc.semaphore(name))

        cols = sb("cols", [P, N_COLS])
        rows = sb("rows", [P, N_ROWS])
        ident = sb("ident", [P, P])
        ident_bf = sb("ident_bf", [P, P], BF16)
        causal = sb("causal", [P, P], BF16)
        A = sb("A", [P, NH, P])
        wv0 = sb("wv0", [P, NH * DH])
        wo0 = sb("wo0", [P, NC, D])
        router = sb("router", [P, CL + TILES])
        cw1 = sb("cw1", [P, COMP])
        cw2 = sb("cw2", [COMP + 1, 2])
        tbl = sb("tbl", [TILES, TBL])
        w1a = sb("w1a", [P, 6, D])
        wg1 = sb("wg1", [P, 3, D])
        wg2 = sb("wg2", [P, D])
        wo1 = sb("wo1", [P, D])
        bias_t = sb("bias_t", [P, 2, WH, P])
        wqkv = sb("wqkv", [P, 3, NH * DH])
        wo2 = sb("wo2", [P, NC, D])
        gate_w = sb("gate_w", [P, NE])
        WB = 3
        w1 = sb("w1", [P, WB, FF])
        w2 = sb("w2", [P, WB, FC, D])
        b2 = sb("b2", [NE, D])
        half_neg = sb("half_neg", [P, 32])
        neg_bg2 = sb("neg_bg2", [P, 1])
        inv_t = sb("inv_t", [P, 1])
        kqs = sb("kqs", [P, NC])
        knot_tab = sb("knot_tab", [P, 3, KN - 1])

        xT = sb("xT", [P, NP, S])
        xr = sb("xr", [P, TT, D])
        xb = sb("xb", [P, TT, D])
        GQ = sb("GQ", [P, NH, S])
        Qm = GQ[:, :, :].rearrange("p h (t q) -> p (h t q)", q=QT).rearrange("p (t h q) -> p t h q", t=4, q=QT)
        OT0 = GQ[:, :, :].rearrange("p (c a) n -> p c a n", a=2)[:, :, 0, :]
        ETw = sb("ETw", [P, WH, P])
        V0 = ETw[:, :, :].rearrange("p (t a) n -> p t (a n)", t=NT)
        klin = ETw[:, 0:4, :]
        k_e = ETw[:, 4:8, :]
        E0 = sb("E0", [P, 3, NT, S])
        Sw = E0[:, :, :, :].rearrange("p a t (g n) -> p a (t g) n", n=P)
        ET0 = sb("ET0", [P, 2, 2, S])
        qlinT = ET0[:, 0, :, :].rearrange("p a n -> p (a n)")
        q_e = ET0[:, 1, :, :].rearrange("p a n -> p (a n)")
        linT, winT = qlinT, q_e
        nm0 = sb("nm0", [P, NH, NT])
        rs0 = sb("rs0", [P, NH, NT])
        ri0 = sb("ri0", [P, NH, NT])
        y1 = sb("y1", [P, TT, D])
        x1 = sb("x1", [P, TT, D])
        x2 = sb("x2", [P, TT, D])
        xn = sb("xn", [P, TT, D])
        x3 = sb("x3", [P, TT, D])
        fT = sb("fT", [P, TOK])
        den = fT
        hT = sb("hT", [P, TOK])
        st1 = sb("st1", [P, TT, 6])
        mv1 = sb("mv1", [P, TT, 2])
        ve1 = sb("ve1", [P, TT])
        rstd1 = sb("rstd1", [P, TT])
        gel = sb("gel", [COMP + 1, TOK])
        comp = sb("comp", [P, TT, 2])
        ec = sb("ec", [P, TT * 8])
        el = sb("el", [P, TT * 8])
        gates = sb("gates", [P, TT, 8])
        gmax = sb("gmax", [P, TT])
        hot_c = sb("hot_c", [P, TT, 8])
        hot_l = sb("hot_l", [P, TT, 8])
        sel = sb("sel", [P, TT, TPC])
        mag = sb("mag", [P, TT])
        fx = sb("fx", [P, TT * 8])
        picked = sb("picked", [P, TT * 8, 3])
        spare = GQ[:, :, :].rearrange("p h n -> p (h n)")
        used = [0]

        def part(n):
            used[0] += n
            return spare[:, used[0] - n:used[0]]

        scores = part(TT * (CL + TILES)).rearrange("p (t n) -> p t n", t=TT)
        m_a = part(TT * 8 * (KN - 1)).rearrange("p (n k) -> p n k", k=KN - 1)
        m_b = part(TT * 8 * (KN - 1)).rearrange("p (n k) -> p n k", k=KN - 1)
        pick = part(TT * 8 * 3 * (KN - 1)).rearrange("p (n a k) -> p n a k", a=3, k=KN - 1)
        selp = part(TT * TILES).rearrange("p (t l c) -> p t l c", t=TT, c=CL)
        hot = part(TT * TILES).rearrange("p (t n) -> p t n", t=TT)
        hotT = part(TOK)[0:TILES, :]
        got = part(TT * TBL).rearrange("p (t n) -> p t n", t=TT)
        hh = part(TT * GRID).rearrange("p (t n) -> p t n", t=TT)
        vlin1 = sb("vlin1", [P, TT, 2, D])
        kv = sb("kv", [P, NP, 2, D])
        qloc = sb("qloc", [P, TOK])
        kloc = sb("kloc", [P, TOK])
        hidg, gt = qloc, kloc
        VW = sb("VW", [P, NP, 4, WH, WD + 1])
        nmw = sb("nmw", [P, 3, 4])
        rsw = sb("rsw", [P, NP, 8 * 4])
        win = sb("win", [P, NT, D])

        xh = sb("xh", [P, TT, D])
        xn2 = sb("xn2", [P, TT, D])
        yo = xn2
        h2T = sb("h2T", [P, TOK])
        QK = sb("QK", [P, 2, NC, S])
        hid = QK[:, :, :, :].rearrange("p a (f b) n -> p a f (b n)", f=FC)
        OT2 = QK[:, 0, :, :]
        V2 = sb("V2", [P, NT, NH * DH])
        work2 = sb("work2", [P, 2048])
        sqn = work2[:, :].rearrange("p (a h n) -> p a h n", a=4, h=8)
        E2 = work2[:, 0:1152].rearrange("p (a n) -> p a n", a=3)
        ET2 = work2[:, 1152:1920].rearrange("p (a n) -> p a n", a=2)
        ss = sb("ss", [P, 8, 8])
        rn = sb("rn", [P, 8, 8])
        nm2 = sb("nm2", [P, NH, NT])
        rs2 = sb("rs2", [P, NH, NT])
        ri2 = sb("ri2", [P, NH, NT])
        st2 = sb("st2", [P, TT, 6])
        mv2 = sb("mv2", [P, TT, 2])
        ve2 = sb("ve2", [P, TT])
        rstd2 = sb("rstd2", [P, TT])
        gl = sb("gl", [P, TT, NE])
        gm = sb("gm", [P, TT])
        gs = sb("gs", [P, TT])
        gateT = sb("gateT", [NE, TOK])
        acc = sb("acc", [P, TT, D])

        wqT = spare[0:DH, 0:NH * P].rearrange("p (h n) -> p h n", h=NH)
        wkT = spare[0:DH, NH * P:2 * NH * P].rearrange("p (h n) -> p h n", h=NH)
        raw = spare[:, 0:S]

        ps = ctx.enter_context(nc.psum_tensor("ps", [P, 8, 512], F32))
        bank1 = [ps[:, n, :] for n in range(4)]
        bank2 = [ps[:, 4 + n, :] for n in range(4)]

        def col(name, n=0, w=1):
            at = COLS[name][0] + n
            return cols[:, at:at + w]

        def row(name):
            at, n = ROWS[name]
            return rows[:, at:at + n]

        def row_t(name):
            at, n = ROWS[name]
            return rows[:, at:at + n].unsqueeze(1).broadcast_to((P, TT, n))

        def tri(ap, a):
            return ap.rearrange("p (a n) -> p a n", a=a)

        w_qk = sem("w_qk")
        w_small = sem("w_small")
        w_first = sem("w_first")
        w_rest = sem("w_rest")
        w_second = sem("w_second")
        setup_pool = sem("setup_pool")
        setup_dve = sem("setup_dve")
        a_ready = sem("a_ready")
        a_copied = sem("a_copied")

        qk_loads = [(wqT, d["wqT"]), (wkT, d["wkT"])]
        small_loads = [(cols[:, :], d["cols"]), (rows[:, :], d["rows"]), (ident[:, :], d["ident"]),
                       (router[:, CL:CL + TILES], d["sigT"])]
        first_loads = [(xT[:, :, :], d["xT"][0, :, :, :]), (xr[:, :, :], d["xr"][0, :, :, :]),
                       (wv0[:, :], d["wv0"]), (wo0[:, :, :], d["wo0"])]
        rest_loads = [(cw1[:, :], d["cw1"]), (cw2[:, :], d["cw2"]), (tbl[:, :], d["tbl"]),
                      (w1a[:, :, :], d["w1a"]), (wg1[:, :, :], d["wg1"]), (wg2[:, :], d["wg2"]),
                      (wo1[:, :], d["wo1"]), (bias_t[:, :, :, :], d["bias_t"])]
        second_loads = [(wqkv[:, :, :], d["wqkv"]), (wo2[:, :, :], d["wo2"]), (gate_w[:, :], d["gate_w"]),
                        (b2[:, :], d["b2"])]

        with nc.Block(no_gpsimd_drain=True) as block:
            @block.sync
            def _(sp):
                for dst, src in qk_loads:
                    sp.dma_start(dst, src).then_inc(w_qk, 16)
                for dst, src in small_loads:
                    sp.dma_start(dst, src).then_inc(w_small, 16)
                for dst, src in first_loads:
                    sp.dma_start(dst, src).then_inc(w_first, 16)
                for dst, src in rest_loads:
                    sp.dma_start(dst, src).then_inc(w_rest, 16)
                for dst, src in second_loads:
                    sp.dma_start(dst, src).then_inc(w_second, 16)
                sp.wait_ge(w_first, 16 * len(first_loads))

            @block.gpsimd
            def _(pool):
                for n, (ap, value) in enumerate(((half_neg[:, :], -0.5), (vlin1[:, :, 1, :], 1.0), (gel[COMP:COMP + 1, :], 1.0),
                                                 (VW[:, :, :, :, WD], 1.0), (causal[:, :], 0.0))):
                    nc.gpsimd.memset(ap, value).then_inc(setup_pool, 1)
                    pool.wait_ge(setup_pool, n + 1)
                nc.gpsimd.affine_select(out=causal[:, :], in_=causal[:, :], compare_op=ALU.is_ge, fill=CAUSAL_FILL,
                                        base=0, pattern=[[-1, P]], channel_multiplier=1)

            @block.vector
            def _(dve):
                n = [0]

                def link(ins):
                    n[0] += 1
                    ins.then_inc(setup_dve, 1)
                    dve.wait_ge(setup_dve, n[0])

                dve.wait_ge(w_small, 16 * len(small_loads))
                nc.vector.tensor_copy(ident_bf[:, :], ident[:, :])
                nc.vector.tensor_scalar(neg_bg2[:, :], col("bg2"), -1.0, None, ALU.mult)
                link(nc.vector.tensor_scalar(inv_t[:, :], col("temp"), 1e-6, None, ALU.add))
                link(nc.vector.reciprocal(inv_t[:, :], inv_t[:, :]))
                link(nc.vector.tensor_tensor(kqs[:, :], col("qs", 0, NC), col("ks", 0, NC), ALU.mult))
                link(nc.vector.tensor_scalar(kqs[:, :], kqs[:, :], 10.0, None, ALU.mult))
                k = row("knots")
                nc.vector.tensor_copy(knot_tab[:, 0, :], k[:, 0:KN - 1])
                nc.vector.tensor_tensor(knot_tab[:, 1, :], k[:, 1:KN], k[:, 0:KN - 1], ALU.subtract)
                nc.vector.tensor_copy(knot_tab[:, 2, :], row("jlo"))
                dve.wait_ge(a_ready, 4)
                sig = router[:, CL:CL + TILES]
                q, low = raw[:, 0:TILES], raw[:, TILES:2 * TILES]
                nc.vector.tensor_scalar(q, sig, 0.3, None, ALU.is_gt)
                link(nc.vector.tensor_scalar(low, sig, -0.3, None, ALU.is_lt))
                link(nc.vector.tensor_tensor(q, q, low, ALU.subtract))
                link(nc.vector.tensor_tensor(q, q, sig, ALU.subtract))
                link(nc.vector.tensor_tensor(sig, sig, q, ALU.add))
                by = sig.rearrange("p (c t) -> p t c", c=CL)
                total, neg = raw[:, 128:128 + CL], raw[:, 136:136 + CL]
                link(nc.vector.tensor_tensor(total, by[:, 0, :], by[:, 1, :], ALU.add))
                for t in range(2, TPC):
                    link(nc.vector.tensor_tensor(total, total, by[:, t, :], ALU.add))
                nc.vector.tensor_scalar(neg, total, 0.0, None, ALU.is_lt)
                link(nc.vector.tensor_scalar(total, total, 0.0, None, ALU.is_gt))
                link(nc.vector.tensor_tensor(router[:, 0:CL], total, neg, ALU.subtract))

            @block.tensor
            def _(pe):
                pe.wait_ge(w_qk, 16 * len(qk_loads))
                for u in range(4):
                    for h in range(4 * u, 4 * u + 4):
                        last = nc.tensor.matmul(bank1[u][:, (h % 4) * P:(h % 4 + 1) * P], wqT[:, h, :], wkT[:, h, :],
                                                start=True, stop=True)
                    last.then_inc(a_ready, 1)

            @block.scalar
            def _(act):
                for u in range(4):
                    act.wait_ge(a_ready, u + 1)
                    nc.scalar.activation(A[:, 4 * u:4 * u + 4, :], tri(bank1[u], 4), ACT.Copy).then_inc(a_copied, 1)
                act.wait_ge(a_copied, 4)

        names = """
            x_next x_taken
            proj0 proj0_act proj0_dve sc0 max0 exp0 ri0_ready norm0 tr0 et0_act et0_dve av0 ot0_act wo0_done y1_ready
            xb_ready dve1 ve1_ready rstd1_ready x1b_ready
            x1_ready x1tr x1T_ready route_ready gelu_ready compress_ready comp_ready sc_copied exp_c sel_ready exp_l
            hot_ready hot_tr hotT_ready got_ready x2_ready x2b_ready xn_ready xn_tr hT_ready
            lin_qk lin_v q_exp k_exp klin_raw qlin_ready klin_ready vlin_ready kv_done kv_copied lin_done lin_ready linT_ready
            loc_q loc_k qloc_ready kloc_ready qm_ready vm_ready vm_proj
            w_sc w_add w_max w_exp w_sum w_tr w_et w_av w_scaled win_tr winT_ready
            g1_done g1_ready g2_done g_exp mixed o1_done x3_ready
            x3_taken dve2 dve2q acc_ready ve2_ready rstd2_ready xn2_ready tr2 hT2_ready
            v2_proj v2_copied qk_proj sq_ready ss_ready rn_ready qn_ready qk_tr q_copied k_copied
            sc2 max2 exp2 ri2_ready norm2 tr2e et2_act et2_dve av2 ot2_done wo2_done
            o2_ready o2_tr o2T_ready gate_done gl_ready gexp_done gate_ready gate_tr gateT_ready
            hid_done hid_ready out_done out_used y_ready y_stored w_e0 w_e1 w_e2
        """.split()
        s = {name: sem(name) for name in names}
        loop_sems = range(min(x.num for x in s.values()), max(x.num for x in s.values()) + 1)
        assert len(loop_sems) == len(names)

        class Chain:

            def __init__(self, eng, name):
                self.eng, self.sem, self.n, self.key, self.step = eng, s[name], 0, 0.0, 0.0

            def at(self, key, until=None, steps=0):
                self.key, self.step = key, (until - key) / (steps + 1) if steps else 0.0
                return key

            def __call__(self, ins):
                self.n += 1
                ins.then_inc(self.sem, 1)
                self.key += self.step
                yield self.key
                self.eng.wait_ge(self.sem, self.n)

        K = dict(p0=0, p1=78, h0=12, w=190, wb=-14.5, g=384.5, v=-6.5, v1=68, q=4, h2=23, o=143.5, e=142.5, z=221.5,
                 h0d0=[2.635, 2.635, 2.44, 2.878], h0d1=[1.778, 2.4, 2.4, 3.24], wd0=[3.535, 3.273, 3.031],
                 wd1=[6.929, 5.155, 4.439], qd0=2.03, qd1=1.652, h2d0=[3.229, 2.144, 2.422, 2.422], h2d1=[2.607,
                 2.607, 2.607, 2.817], ed=[6.48, 6.48, 7.646, 6.48, 5.508, 5.508, 4.682,
                 5.508, 5.508])
        KN_W = 2.605

        def after(steps, n, part):
            return sum(steps[i // part] for i in range(n))

        def kp(b, u):
            return K[f"p{b}"] + 0.9 * u

        def k0(b, h):
            return K[f"p{b}"] + K["h0"] + after(K[f"h0d{b}"], h, 5)

        def kw(b, u):
            return K["w"] + K["wb"] * b + after(K[f"wd{b}"], u, 4)

        def kf(x):
            return k0(1, NH + 3) + 1 + (kw(0, 0) - k0(1, NH + 3) - 1) * x

        def second_at(b):
            return K["v1"] if b else K["v"]

        def kv2(b, u):
            return second_at(b) + u

        def kq(b, u):
            return second_at(b) + K["q"] + K[f"qd{b}"] * u

        def k2(b, h):
            return second_at(b) + K["h2"] + after(K[f"h2d{b}"], h, 5)

        def kx(e, part=0.0):
            return K["e"] + after(K["ed"], e, 1) + K["ed"][e] * part

        NORM = {1: [k0(1, NH + 3) + 0.5, kf(0.66), kf(0.74), kf(0.81), K["g"] + 7],
                2: [0.1, K["o"] + 0.05, K["z"], K["z"] + KN_W + 2]}

        def first_sync(sp, next_pair):
            yield k0(1, NH)
            sp.wait_ge(s["sc0"], NP * NH)
            sp.wait_ge(s["xb_ready"], 1)
            sp.wait_ge(s["proj0"], NP * 12)
            sp.dma_start(xT[:, :, :], d["xT"][bass.ds(next_pair, 1), :, :, :].rearrange("a p t n -> (a p) t n"))\
                .then_inc(s["x_next"], 16)
            sp.dma_start(xr[:, :, :], d["xr"][bass.ds(next_pair, 1), :, :, :].rearrange("a p t n -> (a p) t n"))\
                .then_inc(s["x_next"], 16)
            yield 1000
            sp.wait_ge(s["x_next"], 32)

        def proj_bank(u):
            return bank1[u % 3]

        def first_pe(pe, both):
            for b in range(NP):
                for u in range(12):
                    yield kp(b, u)
                    if u >= 3:
                        v = u - 3
                        pe.wait_ge(s["proj0_dve" if v % 2 else "proj0_act"], 6 * b + v // 2 + 1)
                    if u == 0 and b:
                        pe.wait_ge(s["y1_ready"], b)
                    if u < 8:
                        for j in range(2):
                            last = nc.tensor.matmul(proj_bank(u)[:, j * S:(j + 1) * S], A[:, 2 * u + j, :], xT[:, b, :],
                                                    start=True, stop=True)
                    else:
                        t, c = divmod(u - 8, 2)
                        last = nc.tensor.matmul(proj_bank(u), xT[:, b, t * P:(t + 1) * P],
                                                wv0[:, c * 512:(c + 1) * 512], start=True, stop=True)
                    last.then_inc(s["proj0"], 1)
                for h in range(NH + 3):
                    yield k0(b, h)
                    if h < NH:
                        if h == 0:
                            pe.wait_ge(s["proj0_act"], 6 * (b + 1))
                            pe.wait_ge(s["proj0_dve"], 6 * (b + 1))
                        if h >= 2:
                            pe.wait_ge(s["exp0"], 2 * (NH * b + h - 1))
                        for t in range(NT):
                            last = nc.tensor.matmul(bank1[h % 2][:, t * S:(t + 1) * S], GQ[:, h, t * P:(t + 1) * P],
                                                    xT[:, b, :], start=True, stop=True)
                        last.then_inc(s["sc0"], 1)
                    g = h - 2
                    if 0 <= g < NH:
                        pe.wait_ge(s["norm0"], NH * b + g + 1)
                        if g >= 1:
                            et_wait(pe, "et0", b, g - 1)
                        for k in range(2):
                            for t in range(NT):
                                last = nc.tensor.transpose(bank1[2][:, k * S + t * P:k * S + (t + 1) * P],
                                                           E0[:, g % 3, t, k * P:(k + 1) * P], ident[:, :])
                        last.then_inc(s["tr0"], 1)
                    g = h - 3
                    if g >= 0:
                        et_wait(pe, "et0", b, g)
                        if g >= 2 and g % 2 == 0:
                            pe.wait_ge(s["ot0_act"], NC * b + g // 2)
                        r = 64 * (g % 2)
                        for k in range(2):
                            last = nc.tensor.matmul(bank1[3][r:r + DH, 0:S], V0[:, k, g * DH:(g + 1) * DH],
                                                    ET0[:, g % 2, k, :], start=(k == 0), stop=(k == 1))
                        last.then_inc(s["av0"], 1)
                yield k0(b, NH + 3)
                pe.wait_ge(s["ot0_act"], NC * (b + 1))
                out_proj(bank1[0], OT0, wo0).then_inc(s["wo0_done"], 1)
            yield kf(0.10)
            if not both:
                pe.wait_ge(w_rest, 16 * len(rest_loads))
            pe.wait_ge(s["x1_ready"], 1)
            transposed(bank1[2], x1).then_inc(s["x1tr"], 1)
            yield kf(0.13)
            pe.wait_ge(s["x1T_ready"], 1)
            nc.tensor.matmul(bank1[1][0:COMP, :], cw1[:, :], fT[:, :], start=True, stop=True)
            for t in range(TT):
                last = nc.tensor.matmul(bank1[0][:, t * P:t * P + CL + TILES], fT[:, t * P:(t + 1) * P], router[:, :],
                                        start=True, stop=True)
            last.then_inc(s["route_ready"], 1)
            yield kf(0.16)
            pe.wait_ge(s["gelu_ready"], 1)
            for t in range(TT):
                last = nc.tensor.matmul(bank1[3][:, 2 * t:2 * t + 2], gel[:, t * P:(t + 1) * P], cw2[:, :],
                                        start=True, stop=True)
            last.then_inc(s["compress_ready"], 1)
            yield kf(0.57)
            pe.wait_ge(s["hot_ready"], 1)
            for t in range(TT):
                last = nc.tensor.transpose(bank1[2][0:TILES, t * P:(t + 1) * P], hot[:, t, :], ident[:, :])
            last.then_inc(s["hot_tr"], 1)
            pe.wait_ge(s["hotT_ready"], 1)
            for t in range(TT):
                last = nc.tensor.matmul(bank1[t // 2][:, (t % 2) * S:(t % 2) * S + TBL], hotT[:, t * P:(t + 1) * P],
                                        tbl[:, :], start=True, stop=True)
            last.then_inc(s["got_ready"], 1)
            yield kf(0.88)
            pe.wait_ge(s["xn_ready"], 1)
            transposed(bank1[2], xn).then_inc(s["xn_tr"], 1)
            pe.wait_ge(s["hT_ready"], 1)
            nc.tensor.matmul(bank1[3][:, :], w1a[:, 0, :], hT[:, :], start=True, stop=True)
            for t in range(TT):
                last = nc.tensor.matmul(bank1[2][:, t * P:(t + 1) * P], hT[:, t * P:(t + 1) * P], w1a[:, 1, :],
                                        start=True, stop=True)
            last.then_inc(s["lin_qk"], 1)
            for t in range(TT):
                last = nc.tensor.matmul(bank1[0][:, t * P:(t + 1) * P], hT[:, t * P:(t + 1) * P], w1a[:, 2, :],
                                        start=True, stop=True)
            last.then_inc(s["lin_v"], 1)
            nc.tensor.matmul(bank1[1][:, :], w1a[:, 4, :], hT[:, :], start=True, stop=True).then_inc(s["loc_k"], 1)
            pe.wait_ge(s["vlin_ready"], 1)
            nc.tensor.matmul(bank1[0][:, :], w1a[:, 3, :], hT[:, :], start=True, stop=True).then_inc(s["loc_q"], 1)
            yield kf(0.94)
            pe.wait_ge(s["klin_ready"], 1)
            pe.wait_ge(s["qlin_ready"], 1)
            for b in range(NP):
                for t in range(NT):
                    last = nc.tensor.matmul(bank1[2][:, b * S:(b + 1) * S], klin[:, b * NT + t, :],
                                            vlin1[:, b * NT + t, :, :].rearrange("p a n -> p (a n)"),
                                            start=(t == 0), stop=(t == NT - 1))
            last.then_inc(s["kv_done"], 1)
            pe.wait_ge(s["kv_copied"], 1)
            for j in range(2):
                for b in range(NP):
                    last = nc.tensor.matmul(bank1[3 - j][:, b * S:(b + 1) * S], kv[:, b, j, :], qlinT[:, b * S:(b + 1) * S],
                                            start=True, stop=True)
            last.then_inc(s["lin_done"], 1)
            pe.wait_ge(s["kloc_ready"], 1)
            for b in range(NP):
                for u in range(8 + 3):
                    yield kw(b, u)
                    p, g = divmod(u, 4)
                    U = 8 * b + u
                    if u < 8:
                        pe.wait_ge(s["qm_ready"], 4 * b + g + 1)
                        if U >= 2:
                            pe.wait_ge(s["w_add"], U - 1)
                        for n in range(4):
                            h, t = 4 * g + n // 2 * 2, 2 * p + n % 2
                            k = b * S + KEY0[t]
                            last = nc.tensor.matmul(bank1[u % 2][:, n * P:(n + 1) * P],
                                                    Qm[:, t, h:h + 2, :].rearrange("p h q -> p (h q)"), kloc[:, k:k + P],
                                                    start=True, stop=True)
                        last.then_inc(s["w_sc"], 1)
                    if U == 1:
                        pe.wait_ge(s["linT_ready"], 1)
                        for a in range(NP):
                            for t in range(4):
                                k = a * S + KEY0[t]
                                last = nc.tensor.matmul(bank1[3 - a][:, t * P:(t + 1) * P], hT[:, k:k + P],
                                                        w1a[:, 5, :], start=True, stop=True)
                            last.then_inc(s["vm_proj"], 1)
                    if 2 <= u < 10:
                        V = U - 2
                        pe.wait_ge(s["w_exp"], V + 1)
                        if V >= 1:
                            pe.wait_ge(s["w_et"], V)
                        else:
                            pe.wait_ge(s["vm_ready"], NP)
                        for hd in range(4):
                            last = nc.tensor.transpose(bank1[2][:, hd * P:(hd + 1) * P], Sw[:, V % 3, hd, :],
                                                       ident[:, :])
                        last.then_inc(s["w_tr"], 1)
                    if b and u == 2:
                        window_T(b - 1)
                    if u >= 3:
                        V = U - 3
                        pp, g = divmod(u - 3, 4)
                        pe.wait_ge(s["w_et"], V + 1)
                        if u == 3 and b:
                            pe.wait_ge(s["winT_ready"], b)
                        for hd in range(4):
                            for j in range(2):
                                h, q = 4 * g + hd, QT * (hd % 2)
                                o = (pp * WH + h) * (WD + 1)
                                last = nc.tensor.matmul(bank1[3][QT * j:QT * (j + 1), o:o + WD + 1],
                                                        ETw[:, 4 * g + hd // 2 * 2 + j, q:q + QT],
                                                        VW[:, b, 2 * pp + j, h, :], start=True, stop=True)
                        last.then_inc(s["w_av"], 1)
            gate_hidden(0)
            yield kw(NP - 1, 11)
            window_T(NP - 1)
            yield K["g"]
            gate_hidden(1)
            for b in range(NP):
                pe.wait_ge(s["g1_ready"], b + 1)
                nc.tensor.matmul(bank1[2 + b][:, 0:S], wg2[:, :], hidg[:, b * S:(b + 1) * S], start=True, stop=True)\
                    .then_inc(s["g2_done"], 1)
            for b in range(NP):
                yield K["g"] + 5.5 + b
                pe.wait_ge(s["mixed"], b + 1)
                for t in range(NT):
                    k = b * S + t * P
                    last = nc.tensor.matmul(bank1[b][:, S + t * P:S + (t + 1) * P], gt[:, k:k + P], wo1[:, :],
                                            start=True, stop=True)
                last.then_inc(s["o1_done"], 1)

        def gate_hidden(b):
            pe = nc.tensor
            pe.wait_ge(s["winT_ready"], b + 1)
            for j, r in enumerate((linT, winT, hT[:, :])):
                last = nc.tensor.matmul(bank1[b][:, 0:S], wg1[:, j, :], r[:, b * S:(b + 1) * S],
                                        start=(j == 0), stop=(j == 2))
            last.then_inc(s["g1_done"], 1)

        def window_T(b):
            nc.tensor.wait_ge(s["w_scaled"], b + 1)
            for t in range(NT):
                last = nc.tensor.transpose(bank1[3][:, t * P:(t + 1) * P], win[:, t, :], ident[:, :])
            last.then_inc(s["win_tr"], 1)

        def et_wait(eng, name, b, g):
            eng.wait_ge(s[name + ("_dve" if g % 2 else "_act")], 8 * b + g // 2 + 1)

        def transposed(bank, src):
            for t in range(TT):
                last = nc.tensor.transpose(bank[:, t * P:(t + 1) * P], src[:, t, :], ident[:, :])
            return last

        def out_proj(bank, OT, wo):
            for t in range(NT):
                for c in range(NC):
                    last = nc.tensor.matmul(bank[:, t * P:(t + 1) * P], OT[:, c, t * P:(t + 1) * P], wo[:, c, :],
                                            start=(c == 0), stop=(c == NC - 1))
            return last

        def first_act(act):
            for b in range(NP):
                for u in range(0, 12, 2):
                    yield kp(b, u)
                    act.wait_ge(s["proj0"], 12 * b + u + 1)
                    if b and u == 0:
                        act.wait_ge(s["wo0_done"], b)
                    if u < 8:
                        nc.scalar.activation(GQ[:, 2 * u:2 * u + 2, :], tri(proj_bank(u), 2), ACT.Copy,
                                             scale=DH ** -0.5).then_inc(s["proj0_act"], 1)
                    else:
                        t, c = divmod(u - 8, 2)
                        nc.scalar.activation(V0[:, t, c * 512:(c + 1) * 512], proj_bank(u), ACT.Copy)\
                            .then_inc(s["proj0_act"], 1)
                for h in range(NH + 3):
                    yield k0(b, h)
                    if h < NH:
                        act.wait_ge(s["max0"], NH * b + h + 1)
                        if h >= 3:
                            act.wait_ge(s["tr0"], NH * b + h - 2)
                        for t in range(NT):
                            nc.scalar.activation(E0[:, h % 3, t, :], bank1[h % 2][:, t * S:(t + 1) * S], ACT.Exp,
                                                 bias=nm0[:, h, t:t + 1],
                                                 accum_out=rs0[:, h, t:t + 1]).then_inc(s["exp0"], 1)
                    g = h - 2
                    if 0 <= g < NH and g % 2 == 0:
                        act.wait_ge(s["tr0"], NH * b + g + 1)
                        if g >= 2:
                            act.wait_ge(s["av0"], NH * b + g - 1)
                        nc.scalar.activation(ET0[:, 0, :, :], tri(bank1[2], 2), ACT.Copy).then_inc(s["et0_act"], 1)
                    g = h - 3
                    if g >= 0 and g % 2:
                        act.wait_ge(s["av0"], NH * b + g + 1)
                        nc.scalar.activation(OT0[:, g // 2, :], bank1[3][:, 0:S], ACT.Copy).then_inc(s["ot0_act"], 1)
            yield kf(0.13)
            act.wait_ge(s["x1tr"], 1)
            nc.scalar.activation(fT[:, :], bank1[2], ACT.Copy).then_inc(s["x1T_ready"], 1)
            act.wait_ge(s["route_ready"], 1)
            yield kf(0.16)
            nc.scalar.activation(gel[0:COMP, :], bank1[1][0:COMP, :], ACT.Gelu,
                                 bias=cols[0:COMP, COLS["cb1"][0]:COLS["cb1"][0] + 1]).then_inc(s["gelu_ready"], 1)
            act.wait_ge(s["compress_ready"], 1)
            nc.scalar.activation(comp[:, :, :].rearrange("p t n -> p (t n)"), bank1[3][:, 0:2 * TT], ACT.Tanh)\
                .then_inc(s["comp_ready"], 1)
            yield kf(0.19)
            act.wait_ge(s["sc_copied"], 1)
            nc.scalar.activation(ec[:, :].rearrange("p (t n) -> p t n", t=TT), scores[:, :, 0:CL], ACT.Exp,
                                 scale=-1.0).then_inc(s["exp_c"], 1)
            yield kf(0.38)
            act.wait_ge(s["sel_ready"], 1)
            nc.scalar.activation(el[:, :], sel[:, :, :].rearrange("p t n -> p (t n)"), ACT.Exp,
                                 scale=-1.0).then_inc(s["exp_l"], 1)
            yield kf(0.88)
            act.wait_ge(s["xn_tr"], 1)
            nc.scalar.activation(hT[:, :], bank1[2], ACT.Identity, bias=col("l1_b"), scale=col("l1_g"))\
                .then_inc(s["hT_ready"], 1)
            act.wait_ge(s["loc_k"], 1)
            nc.scalar.activation(kloc[:, :], bank1[1], ACT.Identity, bias=col("bk_loc")).then_inc(s["kloc_ready"], 1)
            act.wait_ge(s["loc_q"], 1)
            nc.scalar.activation(qloc[:, :], bank1[0], ACT.Identity, bias=col("bq_loc")).then_inc(s["qloc_ready"], 1)
            yield kf(0.91)
            act.wait_ge(s["klin_raw"], 1)
            nc.scalar.activation(q_e, q_e, ACT.Exp).then_inc(s["q_exp"], 1)
            nc.scalar.activation(k_e, k_e, ACT.Exp).then_inc(s["k_exp"], 1)
            yield kf(0.94)
            act.wait_ge(s["kv_done"], 1)
            nc.scalar.activation(kv[:, :, :, :].rearrange("p b a n -> p (b a n)"), bank1[2], ACT.Copy)\
                .then_inc(s["kv_copied"], 1)
            for b in range(NP):
                for u in range(1, 8 + 2):
                    yield kw(b, u)
                    U = 8 * b + u
                    if u < 9:
                        v = (U - 1) % 3
                        act.wait_ge(s["w_max"], U)
                        for hd in range(4):
                            ins = nc.scalar.activation(Sw[:, v, hd, :], Sw[:, v, hd, :], ACT.Exp,
                                                       bias=nmw[:, v, hd:hd + 1])
                        ins.then_inc(s["w_exp"], 1)
                    if u >= 2:
                        g = (u - 2) % 4
                        act.wait_ge(s["w_tr"], U - 1)
                        if U >= 6:
                            act.wait_ge(s["w_av"], U - 5)
                        nc.scalar.activation(ETw[:, 4 * g:4 * g + 4, :], tri(bank1[2], 4), ACT.Copy)\
                            .then_inc(s["w_et"], 1)
            yield K["g"]
            for b in range(NP):
                act.wait_ge(s["g2_done"], b + 1)
                nc.scalar.activation(gt[:, b * S:(b + 1) * S], bank1[2 + b][:, 0:S], ACT.Exp, bias=neg_bg2[:, :],
                                     scale=-1.0).then_inc(s["g_exp"], 1)

        def layer_norm(link, dve, src, dst, half, k):
            st, mv, ve, rstd = (st1, mv1, ve1, rstd1) if half == 1 else (st2, mv2, ve2, rstd2)
            key = NORM[half][k]
            link.at(key, key + 0.4 * KN_W, 2)
            yield key
            for t in range(TT):
                ins = nc.vector.bn_stats(st[:, t, :], src[:, t, :])
            yield from link(ins)
            for t in range(TT):
                ins = nc.vector.bn_aggr(mv[:, t, :], st[:, t, :])
            yield from link(ins)
            nc.vector.tensor_scalar(ve[:, :], mv[:, :, 1], EPS, None, ALU.add).then_inc(s[f"ve{half}_ready"], 1)
            yield key + 0.6 * KN_W
            dve.wait_ge(s[f"rstd{half}_ready"], k + 1)
            for t in range(TT):
                ins = nc.vector.tensor_scalar(dst[:, t, :], src[:, t, :], mv[:, t, 0:1], rstd[:, t:t + 1],
                                              ALU.subtract, ALU.mult)
            return ins

        def rstd_step(pool, half, k):
            ve, rstd = (ve1, rstd1) if half == 1 else (ve2, rstd2)
            yield NORM[half][k] + 0.5 * KN_W
            pool.wait_ge(s[f"ve{half}_ready"], k + 1)
            nc.gpsimd.tensor_tensor(rstd[:, :], ve[:, :], half_neg[:, 0:TT], ALU.pow)\
                .then_inc(s[f"rstd{half}_ready"], 1)

        def calibrate(link, e):
            n = TT * 8
            yield from link(nc.vector.tensor_scalar(fx[:, :], e[:, :], 1.0, None, ALU.add))
            yield from link(nc.vector.reciprocal(fx[:, :], fx[:, :]))
            yield from link(nc.vector.tensor_scalar(fx[:, :], fx[:, :], float(KN - 1), None, ALU.mult))
            f = fx[:, :].unsqueeze(2).broadcast_to((P, n, KN - 1))
            nc.vector.tensor_tensor(m_a, f, row("jlo").unsqueeze(1).broadcast_to((P, n, KN - 1)), ALU.is_ge)
            yield from link(nc.vector.tensor_tensor(m_b, f, row("jhi").unsqueeze(1).broadcast_to((P, n, KN - 1)),
                                         ALU.is_lt))
            yield from link(nc.vector.tensor_tensor(m_a, m_a, m_b, ALU.mult))
            yield from link(nc.vector.tensor_tensor(pick, m_a.unsqueeze(2).broadcast_to((P, n, 3, KN - 1)),
                                         knot_tab[:, :, :].unsqueeze(1).broadcast_to((P, n, 3, KN - 1)), ALU.mult))
            yield from link(nc.vector.tensor_reduce(picked[:, :, :], pick, AX, ALU.add))
            g = gates[:, :, :].rearrange("p t n -> p (t n)")
            yield from link(nc.vector.tensor_tensor(g, fx[:, :], picked[:, :, 2], ALU.subtract))
            yield from link(nc.vector.tensor_tensor(g, g, picked[:, :, 1], ALU.mult))
            yield from link(nc.vector.tensor_tensor(g, g, picked[:, :, 0], ALU.add))

        def first_max(link, hot_):
            b = (P, TT, 8)
            yield from link(nc.vector.tensor_reduce(gmax[:, :], gates[:, :, :], AX, ALU.max))
            yield from link(nc.vector.tensor_tensor(gates[:, :, :], gates[:, :, :], gmax[:, :].unsqueeze(2).broadcast_to(b), ALU.is_ge))
            yield from link(nc.vector.tensor_tensor(gates[:, :, :], gates[:, :, :], row_t("first"), ALU.mult))
            yield from link(nc.vector.tensor_reduce(gmax[:, :], gates[:, :, :], AX, ALU.max))
            return nc.vector.tensor_tensor(hot_[:, :, :], gates[:, :, :], gmax[:, :].unsqueeze(2).broadcast_to(b), ALU.is_equal)

        def first_dve(dve, both):
            link = Chain(dve, "dve1")
            for b in range(NP):
                for u in range(1, 12, 2):
                    yield kp(b, u)
                    dve.wait_ge(s["proj0"], 12 * b + u + 1)
                    if b and u == 1:
                        dve.wait_ge(s["wo0_done"], b)
                    if u < 8:
                        nc.vector.tensor_scalar(GQ[:, 2 * u:2 * u + 2, :], tri(proj_bank(u), 2), DH ** -0.5, None,
                                                ALU.mult).then_inc(s["proj0_dve"], 1)
                    else:
                        t, c = divmod(u - 8, 2)
                        nc.vector.tensor_copy(V0[:, t, c * 512:(c + 1) * 512], proj_bank(u)).then_inc(s["proj0_dve"], 1)
                for h in range(NH + 3):
                    yield k0(b, h)
                    if h < NH:
                        dve.wait_ge(s["sc0"], NH * b + h + 1)
                        nc.vector.tensor_reduce(nm0[:, h, :], tri(bank1[h % 2], 2), AX, ALU.max, negate=True)\
                            .then_inc(s["max0"], 1)
                    if 1 <= h <= NH:
                        dve.wait_ge(s["exp0"], 2 * (NH * b + h))
                        nc.vector.reciprocal(ri0[:, h - 1, :], rs0[:, h - 1, :]).then_inc(s["ri0_ready"], 1)
                    g = h - 2
                    if 0 <= g < NH and g % 2:
                        dve.wait_ge(s["tr0"], NH * b + g + 1)
                        if g >= 2:
                            dve.wait_ge(s["av0"], NH * b + g - 1)
                        nc.vector.tensor_copy(ET0[:, 1, :, :], tri(bank1[2], 2)).then_inc(s["et0_dve"], 1)
                yield k0(b, NH + 3)
                dve.wait_ge(s["wo0_done"], b + 1)
                if b == 0:
                    dve.wait_ge(s["xb_ready"], 1)
                y = slice(b * NT, (b + 1) * NT)
                nc.vector.tensor_tensor(y1[:, y, :], tri(bank1[0][:, 0:S], 2), xb[:, y, :], ALU.add)\
                    .then_inc(s["y1_ready"], 1)
            dve.wait_ge(s["y1_ready"], NP)
            if not both:
                dve.wait_ge(w_rest, 16 * len(rest_loads))
            (yield from layer_norm(link, dve, y1, x1, 1, 0)).then_inc(s["x1_ready"], 1)
            yield kf(0.16)
            dve.wait_ge(s["route_ready"], 1)
            nc.vector.tensor_scalar(scores, tri(bank1[0], 4)[:, :, 0:CL + TILES], inv_t[:, :], -87.0,
                                    ALU.mult, ALU.max).then_inc(s["sc_copied"], 1)
            yield link.at(kf(0.19), kf(0.38), 16)
            dve.wait_ge(s["exp_c"], 1)
            yield from calibrate(link, ec)
            yield from link((yield from first_max(link, hot_c)))
            for t in range(TT):
                by = scores[:, t, CL:CL + TILES].rearrange("p (c l) -> p l c", c=CL)
                ins = nc.vector.tensor_tensor(selp[:, t, :, :], by, hot_c[:, t, :].unsqueeze(1).broadcast_to((P, TPC, CL)),
                                              ALU.mult)
            yield from link(ins)
            nc.vector.tensor_reduce(sel[:, :, :], selp, AX, ALU.add).then_inc(s["sel_ready"], 1)
            yield link.at(kf(0.38), kf(0.54), 15)
            dve.wait_ge(s["exp_l"], 1)
            yield from calibrate(link, el)
            yield from link((yield from first_max(link, hot_l)))
            yield kf(0.55)
            for t in range(TT):
                ins = nc.vector.tensor_tensor(hot[:, t, :].rearrange("p (c l) -> p c l", c=CL),
                                              hot_c[:, t, :].unsqueeze(2).broadcast_to((P, CL, TPC)),
                                              hot_l[:, t, :].unsqueeze(1).broadcast_to((P, CL, TPC)), ALU.mult)
            ins.then_inc(s["hot_ready"], 1)
            yield link.at(kf(0.57), kf(0.66), 8)
            dve.wait_ge(s["hot_tr"], 1)
            nc.vector.tensor_copy(hotT, bank1[2][0:TILES, :]).then_inc(s["hotT_ready"], 1)
            dve.wait_ge(s["got_ready"], 1)
            for j in range(2):
                ins = nc.vector.tensor_copy(got[:, 2 * j:2 * j + 2, :], tri(bank1[j], 2)[:, :, 0:TBL])
            yield from link(ins)
            dve.wait_ge(s["comp_ready"], 1)
            G = GRID

            def bc(ap):
                return ap.broadcast_to((P, TT, G))

            yield from link(nc.vector.tensor_tensor(hh, got[:, :, 0:G], bc(comp[:, :, 0:1]), ALU.mult))
            yield from link(nc.vector.tensor_tensor(got[:, :, 0:G], got[:, :, G:2 * G], bc(comp[:, :, 1:2]), ALU.mult))
            yield from link(nc.vector.tensor_tensor(hh, hh, got[:, :, 0:G], ALU.add))
            yield from link(nc.vector.tensor_tensor(hh, hh, got[:, :, 2 * G:3 * G], ALU.add))
            yield from link(nc.vector.scalar_tensor_tensor(out=hh, in0=hh, scalar=0.0, in1=got[:, :, 3 * G:4 * G],
                                                           op0=ALU.max, op1=ALU.mult))
            yield from link(nc.vector.tensor_reduce(mag[:, :], hh, AX, ALU.add))
            yield from link(nc.vector.tensor_tensor(mag[:, :], mag[:, :], got[:, :, 4 * G], ALU.add))
            yield from link(nc.vector.tensor_scalar(mag[:, :], mag[:, :], col("oscale"), None, ALU.mult))
            for t in range(TT):
                ins = nc.vector.scalar_tensor_tensor(out=y1[:, t, :], in0=got[:, t, 4 * G + 1:TBL],
                                                     scalar=mag[:, t:t + 1], in1=x1[:, t, :], op0=ALU.mult, op1=ALU.add)
            yield from link(ins)
            yield kf(0.66)
            yield from link((yield from layer_norm(link, dve, y1, xn, 1, 1)))
            yield from link(nc.vector.tensor_tensor(xn[:, :, :], xn[:, :, :], row_t("gamma"), ALU.mult))
            dve.wait_ge(s["x1b_ready"], 1)
            yield from link(nc.vector.tensor_tensor(y1[:, :, :], xn[:, :, :], xb[:, :, :], ALU.add))
            yield kf(0.74)
            ins = (yield from layer_norm(link, dve, y1, x2, 1, 2))
            ins.then_inc(s["x2_ready"], 1)
            dve.wait_ge(s["x2_ready"], 1)
            yield kf(0.81)
            (yield from layer_norm(link, dve, x2, xn, 1, 3)).then_inc(s["xn_ready"], 1)
            yield link.at(kf(0.88), kf(0.90), 1)
            dve.wait_ge(s["lin_qk"], 1)
            yield from link(nc.vector.tensor_tensor(klin, tri(bank1[2], 4), row_t("bk_lin"), ALU.add))
            nc.vector.tensor_scalar(q_e, bank1[3], col("bq_lin"), 0.0, ALU.add, ALU.min)
            nc.vector.tensor_scalar(k_e, klin, 0.0, None, ALU.min).then_inc(s["klin_raw"], 1)
            dve.wait_ge(s["lin_v"], 1)
            nc.vector.tensor_tensor(vlin1[:, :, 0, :], tri(bank1[0], 4), row_t("bv_lin"), ALU.add)\
                .then_inc(s["vlin_ready"], 1)
            yield link.at(kf(0.92), kf(0.94), 3)
            yield from link(nc.vector.tensor_scalar(qlinT, bank1[3], col("bq_lin"), 0.0, ALU.add, ALU.max))
            yield from link(nc.vector.tensor_scalar(klin, klin, 0.0, None, ALU.max))
            dve.wait_ge(s["q_exp"], 1)
            nc.vector.tensor_tensor(qlinT, q_e, qlinT, ALU.add).then_inc(s["qlin_ready"], 1)
            dve.wait_ge(s["k_exp"], 1)
            nc.vector.tensor_tensor(klin, k_e, klin, ALU.add).then_inc(s["klin_ready"], 1)
            yield link.at(kf(0.94), kw(0, 0), 3)
            dve.wait_ge(s["lin_done"], 1)
            yield from link(nc.vector.tensor_scalar(den[:, :], bank1[2], 1e-6, None, ALU.add))
            yield from link(nc.vector.reciprocal(den[:, :], den[:, :]))
            nc.vector.tensor_tensor(linT, bank1[3], den[:, :], ALU.mult).then_inc(s["linT_ready"], 1)

            def scaled(b):
                dve.wait_ge(s["w_av"], 8 * (b + 1))
                out = bank1[3][:, 0:NT * WH * (WD + 1)].rearrange("p (h n) -> p h n", n=WD + 1)
                nc.vector.reciprocal(rsw[:, b, :], out[:, :, WD]).then_inc(s["w_sum"], 1)
                dve.wait_ge(s["w_sum"], b + 1)
                if b:
                    dve.wait_ge(s["win_tr"], b)
                nc.vector.tensor_tensor(win[:, :, :].rearrange("p t (h n) -> p (t h) n", n=WD),
                                        out[:, :, 0:WD],
                                        rsw[:, b, :].unsqueeze(2).broadcast_to((P, NT * WH, WD)), ALU.mult)\
                    .then_inc(s["w_scaled"], 1)

            def win_biased(b):
                dve.wait_ge(s["win_tr"], b + 1)
                nc.vector.tensor_scalar(winT[:, b * S:(b + 1) * S], bank1[3][:, 0:S], col("bv_loc"), None, ALU.add)\
                    .then_inc(s["winT_ready"], 1)

            for b in range(NP):
                for u in range(8):
                    yield kw(b, u)
                    p, g = divmod(u, 4)
                    U = 8 * b + u
                    dve.wait_ge(s["w_sc"], U + 1)
                    if U >= 3:
                        dve.wait_ge(s["w_tr"], U - 2)
                    nc.vector.tensor_tensor(Sw[:, U % 3, :, :], tri(bank1[u % 2], 4),
                                            bias_t[:, p, 4 * g:4 * g + 4, :], ALU.add).then_inc(s["w_add"], 1)
                    if b and u == 2:
                        win_biased(b - 1)
                    dve.wait_ge(s["w_add"], U + 1)
                    nc.vector.tensor_reduce(nmw[:, U % 3, :], Sw[:, U % 3, :, :], AX, ALU.max, negate=True)\
                        .then_inc(s["w_max"], 1)
                    if U == 1:
                        for a in range(NP):
                            dve.wait_ge(s["vm_proj"], a + 1)
                            nc.vector.tensor_copy(VW[:, a, :, :, 0:WD],
                                                  bank1[3 - a].rearrange("p (t h n) -> p t h n", t=4, h=WH))\
                                .then_inc(s["vm_ready"], 1)
                    if b and u == 1:
                        scaled(b - 1)
                yield kw(b, 10) + 0.1
            scaled(NP - 1)
            yield kw(NP - 1, 11)
            win_biased(NP - 1)
            yield link.at(K["g"], K["g"] + 6, 10)
            for b in range(NP):
                dve.wait_ge(s["g1_done"], b + 1)
                nc.vector.tensor_scalar(hidg[:, b * S:(b + 1) * S], bank1[b][:, 0:S], col("bg1"), 0.0, ALU.add, ALU.max)\
                    .then_inc(s["g1_ready"], 1)
            dve.wait_ge(s["winT_ready"], NP)
            yield from link(nc.vector.tensor_tensor(linT, linT, winT, ALU.subtract))
            for b in range(NP):
                g, dif, w = (x[:, b * S:(b + 1) * S] for x in (gt, linT, winT))
                dve.wait_ge(s["g_exp"], b + 1)
                yield from link(nc.vector.tensor_scalar(g, g, 1.0, None, ALU.add))
                yield from link(nc.vector.reciprocal(g, g))
                yield from link(nc.vector.tensor_tensor(g, g, dif, ALU.mult))
                nc.vector.tensor_tensor(g, g, w, ALU.add).then_inc(s["mixed"], 1)
            dve.wait_ge(s["x2b_ready"], 2)
            for b in range(NP):
                yield K["g"] + 6 + b
                dve.wait_ge(s["o1_done"], b + 1)
                y = slice(b * NT, (b + 1) * NT)
                ins = nc.vector.tensor_tensor(y1[:, y, :], tri(bank1[b][:, S:2 * S], 2), xb[:, y, :], ALU.add)
            yield from link(ins)
            if both:
                dve.wait_ge(s["x3_taken"], 1)
                dve.wait_ge(s["xn2_ready"], 1)
            (yield from layer_norm(link, dve, y1, x3, 1, 4)).then_inc(s["x3_ready"], 1)

        def first_pool(pool):
            yield 0
            nc.gpsimd.tensor_tensor(xb[:, :, :], xr[:, :, :], row_t("bo0"), ALU.add).then_inc(s["xb_ready"], 1)
            for b in range(NP):
                for h in range(1, NH + 1):
                    yield k0(b, h)
                    g = h - 1
                    pool.wait_ge(s["ri0_ready"], NH * b + g + 1)
                    nc.gpsimd.tensor_tensor(E0[:, g % 3, :, :], E0[:, g % 3, :, :],
                                            ri0[:, g, :].unsqueeze(2).broadcast_to((P, NT, S)), ALU.mult)\
                        .then_inc(s["norm0"], 1)
            yield from rstd_step(pool, 1, 0)
            yield kf(0.16)
            pool.wait_ge(s["x1_ready"], 1)
            nc.gpsimd.tensor_tensor(xb[:, :, :], x1[:, :, :], row_t("beta"), ALU.add).then_inc(s["x1b_ready"], 1)
            yield from rstd_step(pool, 1, 1)
            yield from rstd_step(pool, 1, 2)
            yield from rstd_step(pool, 1, 3)
            yield kf(0.90)
            pool.wait_ge(s["x2_ready"], 1)
            nc.gpsimd.tensor_tensor(xb[:, :, :], x2[:, :, :], x2[:, :, :], ALU.add).then_inc(s["x2b_ready"], 1)
            pool.wait_ge(s["x2b_ready"], 1)
            nc.gpsimd.tensor_tensor(xb[:, :, :], xb[:, :, :], row_t("bo1"), ALU.add).then_inc(s["x2b_ready"], 1)
            pool.wait_ge(s["qloc_ready"], 1)

            def masked(b, g):
                if b:
                    pool.wait_ge(s["w_sc"], 8 * b - 4 + g + 1)
                shape = (P, 4, 4, QT)
                nc.gpsimd.tensor_tensor(Qm[:, :, 4 * g:4 * g + 4, :],
                                        tri(qloc[:, b * S:(b + 1) * S], 4).unsqueeze(2).broadcast_to(shape),
                                        col("headmask", 4 * g, 4).unsqueeze(1).unsqueeze(3).broadcast_to(shape),
                                        ALU.mult)\
                    .then_inc(s["qm_ready"], 1)

            for g in range(4):
                masked(0, g)
            for b in range(NP):
                if b + 1 < NP:
                    for g in range(4):
                        yield kw(b, 5 + g) + 0.05
                        masked(b + 1, g)
            yield K["g"] + 6
            yield from rstd_step(pool, 1, 4)

        QKU = [(half, kind, t) for half in range(2) for kind in range(2) for t in range(NT)]

        BLOCKS = [(0, 0), (1, 0), (1, 1)]

        def second_pe(pe):
            yield KN_W
            pe.wait_ge(s["xn2_ready"], 1)
            transposed(bank2[2], xn2).then_inc(s["tr2"], 1)
            pe.wait_ge(s["hT2_ready"], 1)
            for b in range(NP):
                for u in range(4):
                    yield kv2(b, u)
                    if u >= 2:
                        pe.wait_ge(s["v2_copied"], 4 * b + u - 1)
                    if b and u == 0:
                        pe.wait_ge(s["acc_ready"], b)
                    t, c = divmod(u, 2)
                    nc.tensor.matmul(bank2[u % 2], h2T[:, (b * NT + t) * P:(b * NT + t + 1) * P],
                                     wqkv[:, 2, c * 512:(c + 1) * 512], start=True, stop=True).then_inc(s["v2_proj"], 1)
                for u in range(len(QKU) + 3):
                    yield kq(b, u)
                    if u < len(QKU):
                        half, kind, t = QKU[u]
                        if u == 0:
                            pe.wait_ge(s["v2_copied"], 4 * (b + 1))
                        if u >= 3:
                            pe.wait_ge(s["qn_ready"], 8 * b + u - 2)
                        nc.tensor.matmul(qk_bank(u), h2T[:, (b * NT + t) * P:(b * NT + t + 1) * P],
                                         wqkv[:, kind, half * 512:(half + 1) * 512], start=True, stop=True)\
                            .then_inc(s["qk_proj"], 1)
                    if u >= 3:
                        v = u - 3
                        pe.wait_ge(s["qn_ready"], 8 * b + v + 1)
                        if v >= 1:
                            qk_wait(pe, b, v - 1)
                        for c in range(4):
                            last = nc.tensor.transpose(bank2[2][:, c * P:(c + 1) * P],
                                                       sqn[:, v % 4, 2 * c:2 * c + 2, :].rearrange("p a n -> p (a n)"),
                                                       ident[:, :])
                        last.then_inc(s["qk_tr"], 1)
                for h in range(NH + 3):
                    yield k2(b, h)
                    if h < NH:
                        if h == 0:
                            pe.wait_ge(s["q_copied"], 4 * (b + 1))
                            pe.wait_ge(s["k_copied"], 4 * (b + 1))
                        if h >= 2:
                            pe.wait_ge(s["exp2"], 2 * (NH * b + h - 1))
                        c, r = h // 2, 64 * (h % 2)
                        for j, (t, k) in enumerate(BLOCKS):
                            o = bank2[h % 2][:, j * P:(j + 1) * P]
                            last = nc.tensor.matmul(o, QK[r:r + DH, 0, c, t * P:(t + 1) * P],
                                                    QK[r:r + DH, 1, c, k * P:(k + 1) * P], start=True, stop=(t != k))
                            if t == k:
                                last = nc.tensor.matmul(o, ident_bf[:, :], causal[:, :], start=False, stop=True)
                        last.then_inc(s["sc2"], 1)
                    g = h - 2
                    if 0 <= g < NH:
                        pe.wait_ge(s["norm2"], NH * b + g + 1)
                        if g >= 1:
                            et_wait(pe, "et2", b, g - 1)
                        for j in range(len(BLOCKS)):
                            last = nc.tensor.transpose(bank2[2][:, j * P:(j + 1) * P], E2[:, g % 3, j * P:(j + 1) * P],
                                                       ident[:, :])
                        last.then_inc(s["tr2e"], 1)
                    g = h - 3
                    if g >= 0:
                        et_wait(pe, "et2", b, g)
                        if g >= 2 and g % 2 == 0:
                            pe.wait_ge(s["ot2_done"], NC * b + g // 2)
                        r = 64 * (g % 2)
                        for j, (t, k) in enumerate(BLOCKS):
                            last = nc.tensor.matmul(bank2[3][r:r + DH, t * P:(t + 1) * P],
                                                    V2[:, k, g * DH:(g + 1) * DH], ET2[:, g % 2, j * P:(j + 1) * P],
                                                    start=(k == 0), stop=(k == t))
                        last.then_inc(s["av2"], 1)
                yield k2(b, NH + 3)
                pe.wait_ge(s["ot2_done"], NC * (b + 1))
                out_proj(bank2[0], OT2, wo2).then_inc(s["wo2_done"], 1)
            yield K["o"] + KN_W
            pe.wait_ge(s["o2_ready"], 1)
            transposed(bank2[2], xn2).then_inc(s["o2_tr"], 1)
            pe.wait_ge(s["o2T_ready"], 1)
            for t in range(TT):
                last = nc.tensor.matmul(bank2[3][:, t * NE:(t + 1) * NE], h2T[:, t * P:(t + 1) * P], gate_w[:, :],
                                        start=True, stop=True)
            last.then_inc(s["gate_done"], 1)
            for e in range(NE + 1):
                for f in range(FC):
                    yield kx(e, f / FC)
                    u = FC * e + f
                    if e < NE:
                        if f == 0:
                            pe.wait_ge(s[f"w_e{e % WB}"], 32 * (e // WB + 1))
                        if u >= 2:
                            pe.wait_ge(s["hid_ready"], u - 1)
                        nc.tensor.matmul(bank2[u % 2], w1[:, e % WB, f * P:(f + 1) * P], h2T[:, :],
                                         start=True, stop=True).then_inc(s["hid_done"], 1)
                    if u == 1:
                        pe.wait_ge(s["gate_ready"], 1)
                        for t in range(TT):
                            last = nc.tensor.transpose(bank2[2][0:NE, t * P:(t + 1) * P], gl[:, t, :], ident[:, :])
                        last.then_inc(s["gate_tr"], 1)
                        pe.wait_ge(s["gateT_ready"], 1)
                        for t in range(TT):
                            last = nc.tensor.matmul(bank2[3][:, t * P:(t + 1) * P], gateT[:, t * P:(t + 1) * P],
                                                    b2[:, :], start=True, stop=True)
                        last.then_inc(s["out_done"], 1)
                    if e >= 1:
                        x, t = e - 1, f
                        if t == 0:
                            pe.wait_ge(s["hid_ready"], FC * (x + 1))
                            if x >= 1:
                                pe.wait_ge(s["out_used"], x)
                        for c in range(FC):
                            last = nc.tensor.matmul(bank2[2 + x % 2][:, t * P:(t + 1) * P],
                                                    hid[:, x % 2, c, t * P:(t + 1) * P], w2[:, x % WB, c, :],
                                                    start=(c == 0), stop=(c == FC - 1))
                        if t == TT - 1:
                            last.then_inc(s["out_done"], 1)

        def qk_bank(u):
            return bank2[(0, 1, 3)[u % 3]]

        def qk_wait(eng, b, v):
            kind = QKU[v][1]
            n = sum(1 for x in QKU[:v + 1] if x[1] == kind)
            eng.wait_ge(s["k_copied" if kind else "q_copied"], 4 * b + n)

        def second_act(act):
            yield 0
            nc.scalar.activation(xh[:, :, :], x3[:, :, :], ACT.Copy).then_inc(s["x3_taken"], 1)
            yield KN_W
            act.wait_ge(s["tr2"], 1)
            nc.scalar.activation(h2T[:, :], bank2[2], ACT.Identity, bias=col("f_b"), scale=col("f_g"))\
                .then_inc(s["hT2_ready"], 1)
            for b in range(NP):
                for u in range(4):
                    yield kv2(b, u)
                    t, c = divmod(u, 2)
                    act.wait_ge(s["v2_proj"], 4 * b + u + 1)
                    nc.scalar.activation(V2[:, t, c * 512:(c + 1) * 512], bank2[u % 2], ACT.Copy)\
                        .then_inc(s["v2_copied"], 1)
                for u in range(len(QKU) + 3):
                    yield kq(b, u)
                    if u < len(QKU):
                        act.wait_ge(s["qk_proj"], 8 * b + u + 1)
                        if u >= 4:
                            act.wait_ge(s["qk_tr"], 8 * b + u - 3)
                        nc.scalar.activation(sqn[:, u % 4, :, :], tri(qk_bank(u), 8), ACT.Square)\
                            .then_inc(s["sq_ready"], 1)
                    if u >= 3 and QKU[u - 3][1] == 0:
                        half, _, t = QKU[u - 3]
                        act.wait_ge(s["qk_tr"], 8 * b + u - 2)
                        if b and u == 3:
                            act.wait_ge(s["wo2_done"], b)
                        nc.scalar.activation(QK[:, 0, 4 * half:4 * half + 4, t * P:(t + 1) * P], tri(bank2[2], 4),
                                             ACT.Copy).then_inc(s["q_copied"], 1)
                for h in range(NH + 3):
                    yield k2(b, h)
                    if h < NH:
                        act.wait_ge(s["max2"], NH * b + h + 1)
                        if h >= 3:
                            act.wait_ge(s["tr2e"], NH * b + h - 2)
                        for t in range(NT):
                            o = slice(t * P, t * P + (t + 1) * P)
                            nc.scalar.activation(E2[:, h % 3, o], bank2[h % 2][:, o], ACT.Exp, bias=nm2[:, h, t:t + 1],
                                                 accum_out=rs2[:, h, t:t + 1]).then_inc(s["exp2"], 1)
                    g = h - 2
                    if 0 <= g < NH and g % 2 == 0:
                        act.wait_ge(s["tr2e"], NH * b + g + 1)
                        if g >= 2:
                            act.wait_ge(s["av2"], NH * b + g - 1)
                        nc.scalar.activation(ET2[:, 0, :], bank2[2][:, 0:384], ACT.Copy).then_inc(s["et2_act"], 1)
                    g = h - 3
                    if g >= 0 and g % 2:
                        act.wait_ge(s["av2"], NH * b + g + 1)
                        nc.scalar.activation(OT2[:, g // 2, :], bank2[3][:, 0:S], ACT.Copy).then_inc(s["ot2_done"], 1)
            yield K["o"] + KN_W
            act.wait_ge(s["o2_tr"], 1)
            nc.scalar.activation(h2T[:, :], bank2[2], ACT.Identity, bias=col("f_b"), scale=col("f_g"))\
                .then_inc(s["o2T_ready"], 1)
            yield K["o"] + KN_W + 1.2
            act.wait_ge(s["gl_ready"], 1)
            nc.scalar.activation(gl[:, :, :], gl[:, :, :], ACT.Exp).then_inc(s["gexp_done"], 1)
            for e in range(NE):
                for f in range(FC):
                    yield kx(e, f / FC)
                    u = FC * e + f
                    act.wait_ge(s["hid_done"], u + 1)
                    if f == 0 and e >= 2:
                        act.wait_ge(s["out_done"], e)
                    nc.scalar.activation(hid[:, e % 2, f, :], bank2[u % 2], ACT.Gelu_apprx_tanh,
                                         bias=col("b1", e * FC + f)).then_inc(s["hid_ready"], 1)

        def second_dve(dve):
            link = Chain(dve, "dve2")
            yield 0
            (yield from layer_norm(link, dve, x3, xn2, 2, 0)).then_inc(s["xn2_ready"], 1)
            for b in range(NP):
                for u in range(len(QKU) + 3):
                    yield kq(b, u)
                    if u < len(QKU):
                        dve.wait_ge(s["sq_ready"], 8 * b + u + 1)
                        nc.vector.tensor_reduce(ss[:, u, :], sqn[:, u % 4, :, :], AX, ALU.add).then_inc(s["dve2q"], 1)
                    if u >= 3 and QKU[u - 3][1] == 1:
                        half, _, t = QKU[u - 3]
                        dve.wait_ge(s["qk_tr"], 8 * b + u - 2)
                        nc.vector.tensor_tensor(QK[:, 1, 4 * half:4 * half + 4, t * P:(t + 1) * P], tri(bank2[2], 4),
                                                kqs[:, 4 * half:4 * half + 4].unsqueeze(2).broadcast_to((P, 4, P)),
                                                ALU.mult).then_inc(s["k_copied"], 1)
                    if u < len(QKU):
                        dve.wait_ge(s["dve2q"], 8 * b + u + 1)
                        nc.vector.tensor_scalar(ss[:, u, :], ss[:, u, :], 1e-12, None, ALU.add).then_inc(s["ss_ready"], 1)
                        yield kq(b, u) + 0.6 * K[f"qd{b}"]
                        dve.wait_ge(s["rn_ready"], 8 * b + u + 1)
                        nc.vector.tensor_tensor(sqn[:, u % 4, :, :], tri(qk_bank(u), 8),
                                                rn[:, u, :].unsqueeze(2).broadcast_to((P, 8, DH)), ALU.mult)\
                            .then_inc(s["qn_ready"], 1)
                for h in range(NH + 3):
                    yield k2(b, h)
                    if h < NH:
                        dve.wait_ge(s["sc2"], NH * b + h + 1)
                        for t in range(NT):
                            ins = nc.vector.tensor_reduce(nm2[:, h, t:t + 1],
                                                          bank2[h % 2][:, t * P:t * P + (t + 1) * P],
                                                          AX, ALU.max, negate=True)
                        ins.then_inc(s["max2"], 1)
                    if 1 <= h <= NH:
                        dve.wait_ge(s["exp2"], 2 * (NH * b + h))
                        nc.vector.reciprocal(ri2[:, h - 1, :], rs2[:, h - 1, :]).then_inc(s["ri2_ready"], 1)
                    g = h - 2
                    if 0 <= g < NH and g % 2:
                        dve.wait_ge(s["tr2e"], NH * b + g + 1)
                        if g >= 2:
                            dve.wait_ge(s["av2"], NH * b + g - 1)
                        nc.vector.tensor_copy(ET2[:, 1, :], bank2[2][:, 0:384]).then_inc(s["et2_dve"], 1)
                yield k2(b, NH + 3)
                dve.wait_ge(s["wo2_done"], b + 1)
                nc.vector.tensor_copy(acc[:, b * NT:(b + 1) * NT, :], tri(bank2[0][:, 0:S], 2)).then_inc(s["acc_ready"], 1)
            dve.wait_ge(s["acc_ready"], NP)
            (yield from layer_norm(link, dve, acc, xn2, 2, 1)).then_inc(s["o2_ready"], 1)
            yield link.at(K["o"] + KN_W, K["o"] + KN_W + 1, 2)
            b = (P, TT, NE)
            dve.wait_ge(s["gate_done"], 1)
            yield from link(nc.vector.tensor_tensor(gl[:, :, :], tri(bank2[3][:, 0:TT * NE], TT), row_t("gate_b"), ALU.add))
            yield from link(nc.vector.tensor_reduce(gm[:, :], gl[:, :, :], AX, ALU.max))
            nc.vector.tensor_tensor(gl[:, :, :], gl[:, :, :], gm[:, :].unsqueeze(2).broadcast_to(b), ALU.subtract)\
                .then_inc(s["gl_ready"], 1)
            yield link.at(K["o"] + KN_W + 1.4, K["o"] + KN_W + 2, 2)
            dve.wait_ge(s["gexp_done"], 1)
            yield from link(nc.vector.tensor_reduce(gs[:, :], gl[:, :, :], AX, ALU.add))
            yield from link(nc.vector.reciprocal(gs[:, :], gs[:, :]))
            nc.vector.tensor_tensor(gl[:, :, :], gl[:, :, :], gs[:, :].unsqueeze(2).broadcast_to(b), ALU.mult)\
                .then_inc(s["gate_ready"], 1)
            yield kx(0, 1 / FC)
            dve.wait_ge(s["gate_tr"], 1)
            nc.vector.tensor_copy(gateT[:, :], bank2[2][0:NE, :]).then_inc(s["gateT_ready"], 1)
            dve.wait_ge(s["out_done"], 1)
            nc.vector.tensor_copy(acc[:, :, :], tri(bank2[3], TT)).then_inc(s["out_used"], 1)
            dve.wait_ge(s["out_used"], 1)
            for x in range(NE):
                yield kx(x + 1, 0.76)
                dve.wait_ge(s["out_done"], x + 2)
                for t in range(TT):
                    ins = nc.vector.scalar_tensor_tensor(out=acc[:, t, :], in0=bank2[2 + x % 2][:, t * P:(t + 1) * P],
                                                         scalar=gl[:, t, x:x + 1], in1=acc[:, t, :],
                                                         op0=ALU.mult, op1=ALU.add)
                ins.then_inc(s["out_used"], 1)
                yield kx(x + 1, 0.8)
                dve.wait_ge(s["out_used"], x + 2)
            yield K["z"]
            yield from link((yield from layer_norm(link, dve, acc, xn2, 2, 2)))
            yield from link(nc.vector.tensor_tensor(xn2[:, :, :], xn2[:, :, :], row_t("f_g"), ALU.mult))
            yield from link(nc.vector.tensor_tensor(xn2[:, :, :], xn2[:, :, :], row_t("f_b"), ALU.add))
            dve.wait_ge(s["x3_taken"], 1)
            yield from link(nc.vector.tensor_tensor(acc[:, :, :], xn2[:, :, :], xh[:, :, :], ALU.add))
            (yield from layer_norm(link, dve, acc, yo, 2, 3)).then_inc(s["y_ready"], 1)

        def second_pool(pool):
            yield 0
            yield from rstd_step(pool, 2, 0)
            for b in range(NP):
                for u in range(len(QKU)):
                    yield kq(b, u) + 0.5 * K[f"qd{b}"]
                    pool.wait_ge(s["ss_ready"], 8 * b + u + 1)
                    nc.gpsimd.tensor_tensor(rn[:, u, :], ss[:, u, :], half_neg[:, 0:8], ALU.pow)\
                        .then_inc(s["rn_ready"], 1)
                for h in range(1, NH + 1):
                    yield k2(b, h)
                    g = h - 1
                    pool.wait_ge(s["ri2_ready"], NH * b + g + 1)
                    for t in range(NT):
                        o = slice(t * P, t * P + (t + 1) * P)
                        ins = nc.gpsimd.tensor_tensor(E2[:, g % 3, o], E2[:, g % 3, o],
                                                      ri2[:, g, t:t + 1].broadcast_to((P, (t + 1) * P)), ALU.mult)
                    ins.then_inc(s["norm2"], 1)
            yield from rstd_step(pool, 2, 1)
            yield from rstd_step(pool, 2, 2)
            yield from rstd_step(pool, 2, 3)

        def second_sync(sp, pair):
            for e in range(NE):
                yield kx(e - WB + 1, 0.76) if e >= WB else 0
                if e >= WB:
                    sp.wait_ge(s["out_done"], e - WB + 2)
                sp.dma_start(w1[:, e % WB, :], d["w1"][:, e, :]).then_inc(s[f"w_e{e % WB}"], 16)
                sp.dma_start(w2[:, e % WB, :, :], d["w2"][:, e, :, :]).then_inc(s[f"w_e{e % WB}"], 16)
            yield 1000
            sp.wait_ge(s["y_ready"], 1)
            sp.dma_start(d["y"][bass.ds(pair, 1), :, :, :].rearrange("a p t n -> (a p) t n"), yo[:, :, :])\
                .then_inc(s["y_stored"], 16)
            sp.wait_ge(s["y_stored"], 16)

        def body(first, second, i=0):
            def programs(eng, of_first, of_second):
                merged(*([of_first(eng)] if first else []), *([of_second(eng)] if second else []))

            with nc.Block(no_gpsimd_drain=True) as block:
                @block.vector
                def _(dve):
                    programs(dve, lambda e: first_dve(e, second), second_dve)

                @block.tensor
                def _(pe):
                    programs(pe, lambda e: first_pe(e, second), second_pe)

                @block.scalar
                def _(act):
                    programs(act, first_act, second_act)

                @block.gpsimd
                def _(pool):
                    programs(pool, first_pool, second_pool)

                @block.sync
                def _(sp):
                    programs(sp, lambda e: first_sync(e, i + 2 if second else 1), lambda e: second_sync(e, i))
            nc.sync.sem_clear(loop_sems)
            nc.all_engine_barrier(sem_only=True)

        body(True, False)
        nc.sync.wait_ge(w_second, 16 * len(second_loads))
        nc.all_engine_barrier(sem_only=True)
        with nc.Fori(0, NB // NP - 1) as i:
            body(True, True, i)
        body(False, True, NB // NP - 1)


def kernel(**inputs):
    import numpy as np
    import concourse.bacc as bacc
    from concourse.bass_utils import run_bass_kernel_spmd

    x = {k: np.asarray(v) for k, v in inputs.items()}
    f = np.float32
    X = x["L0_attn_hidden_states"]
    pad = np.zeros((NP, D, S), f)

    def by_pair(a):
        return a.reshape(-1, NP, *a.shape[1:])

    XT = by_pair(np.concatenate([X.transpose(0, 2, 1), pad])).transpose(0, 2, 1, 3)
    XR = np.concatenate([X, pad.reshape(NP, S, D)]).reshape(-1, TT, P, D).transpose(0, 2, 1, 3)

    def chunks(w):
        return w.reshape(-1, P, w.shape[-1]).transpose(1, 0, 2)

    def heads_T(w):
        return w.reshape(D, NH, DH).transpose(2, 1, 0)

    col_of = {"l1_g": x["L1_attn_ln_g"], "l1_b": x["L1_attn_ln_b"], "bq_lin": x["L1_attn_bq_lin"],
              "bq_loc": x["L1_attn_bq_loc"], "bk_loc": x["L1_attn_bk_loc"], "bv_loc": x["L1_attn_bv_loc"],
              "bg1": x["L1_attn_bg1"], "bg2": x["L1_attn_bg2"], "f_g": x["L1_ffn_ln_g"], "f_b": x["L1_ffn_ln_b"],
              "oscale": np.broadcast_to(x["L0_ffn_output_scale"], (P,)),
              "temp": np.broadcast_to(x["L0_ffn_temperature"], (P,)),
              "qs": x["L1_ffn_q_scale"].reshape(NC, P).T, "ks": x["L1_ffn_k_scale"].reshape(NC, P).T,
              "b1": x["L1_ffn_b1"].reshape(NE * FC, P).T,
              "headmask": np.where(np.arange(P)[:, None] // WD == np.arange(WH), f(WD ** -0.5), f(0))}
    cols = np.zeros((P, N_COLS), f)
    for name, v in col_of.items():
        at, n = COLS[name]
        cols[:, at:at + n] = v.reshape(P, n)
    cols[0:COMP, COLS["cb1"][0]] = x["L0_ffn_compress_b1"]
    row_of = {"bo0": x["L0_attn_bo"], "gamma": x["L0_ffn_norm_gamma"], "beta": x["L0_ffn_norm_beta"],
              "bk_lin": x["L1_attn_bk_lin"], "bv_lin": x["L1_attn_bv_lin"], "bo1": x["L1_attn_bo"],
              "f_g": x["L1_ffn_ln_g"], "f_b": x["L1_ffn_ln_b"], "gate_b": x["L1_ffn_gate_b"],
              "knots": x["L0_ffn_knot_values"], "jlo": np.arange(KN - 1, dtype=f),
              "jhi": np.array([*range(1, KN - 1), 1e30], f), "first": np.arange(8, 0, -1, dtype=f)}
    rows = np.zeros((P, N_ROWS), f)
    for name, v in row_of.items():
        at, n = ROWS[name]
        rows[:, at:at + n] = v
    query = np.arange(P)[:, None] + P * np.arange(2)
    key = np.array(KEY0)[query // QT][:, :, None] + np.arange(P)
    off = key - query[:, :, None]
    seen = np.abs(off) <= HALF
    rel = x["L1_attn_rel_bias"]
    bias_t = np.where(seen[..., None], rel[np.where(seen, off, 0) + 2 * HALF], f(NEG))
    bias_t = bias_t.reshape(2, QT, 2, P, WH // 2, 2).transpose(5, 1, 2, 4, 0, 3).reshape(P, 2, WH, P)

    wkv = x["L0_attn_Wkv"]
    names = ["wq_lin", "wk_lin", "wv_lin", "wq_loc", "wk_loc", "wv_loc"]
    arrays = {
        "xT": XT, "xr": XR,
        "wqT": heads_T(x["L0_attn_Wq"]), "wkT": heads_T(wkv[:, :NH * DH]), "wv0": wkv[:, NH * DH:],
        "wo0": chunks(x["L0_attn_Wo"]), "sigT": x["L0_ffn_signatures_raw"].T, "cw1": x["L0_ffn_compress_w1"],
        "cw2": np.concatenate([x["L0_ffn_compress_w2"], x["L0_ffn_compress_b2"][None]]),
        "tbl": np.concatenate([x["L0_ffn_spline_w1"].reshape(TILES, -1), x["L0_ffn_spline_b1"],
                               x["L0_ffn_spline_w2"].reshape(TILES, -1), x["L0_ffn_spline_b2"],
                               x["L0_ffn_directions"]], axis=1),
        "w1a": np.stack([x["L1_attn_" + n] for n in names], axis=1),
        "wg1": chunks(x["L1_attn_wg1"]), "wg2": x["L1_attn_wg2"], "wo1": x["L1_attn_wo"], "bias_t": bias_t,
        "wqkv": np.stack([x["L1_ffn_Wq"], x["L1_ffn_Wk"], x["L1_ffn_Wv"]], axis=1),
        "wo2": chunks(x["L1_ffn_Wo"]), "gate_w": x["L1_ffn_gate_w"],
        "w1": x["L1_ffn_w1"].transpose(1, 0, 2),
        "w2": x["L1_ffn_w2"].reshape(NE, FC, P, D).transpose(2, 0, 1, 3), "b2": x["L1_ffn_b2"],
        "cols": cols, "rows": rows, "ident": np.eye(P, dtype=f),
    }
    arrays = {k: np.ascontiguousarray(v, dtype=f) for k, v in arrays.items()}
    nc = bacc.Bacc("TRN2", target_bir_lowering=False, num_devices=1)
    d = {k: nc.dram_tensor("in_" + k, v.shape, F32, kind="ExternalInput").ap() for k, v in arrays.items()}
    d["y"] = nc.dram_tensor("out_y", (NB // NP, P, TT, D), F32, kind="ExternalOutput").ap()
    whole_net(nc, d)
    r = run_bass_kernel_spmd(nc, [{"in_" + k: v for k, v in arrays.items()}], core_ids=[0])
    return r.results[0]["out_y"].transpose(0, 2, 1, 3).reshape(NB, S, D)
```
